# Optimizing a Trainium2 kernel written in Bass

```python
import numpy as np
import jax
import jax.numpy as jnp

def _softmax(x, axis=-1):
    return jax.nn.softmax(x, axis=axis)

def _gelu(x):
    return jax.nn.gelu(x, approximate=True)

def _silu(x):
    return jax.nn.silu(x)

def _sigmoid(x):
    return jax.nn.sigmoid(x)

def _layernorm(x, axis=-1, eps=1e-05):
    m = jnp.mean(x, axis=axis, keepdims=True)
    v = jnp.var(x, axis=axis, keepdims=True)
    return (x - m) / jnp.sqrt(v + eps)

def _scatter_add(tgt, idx, src, axis=0):
    return tgt.at[idx].add(src)

def _segment_sum(src, seg, n):
    return jax.ops.segment_sum(src, seg, n)
kernel_name = 'mk_decoder_postln_d2_seqx_r4_9a0803'

def setup_inputs(seed: int=0):
    np.random.seed(seed)
    _w = jnp.asarray

    def _rec_inputs():
        import jax
        import jax.numpy as jnp
        _rk = jax.random.key(seed)
        x = -0.0002928 + 1 * jax.random.normal(jax.random.fold_in(_rk, 1), (4, 512, 256), jnp.float32)
        _lenS = 512 - jax.random.randint(jax.random.fold_in(_rk, 7), (4,), 0, max(1, 512 // 4) + 1, jnp.int32)
        _lenS2 = 1601 - jax.random.randint(jax.random.fold_in(_rk, 8), (4,), 0, max(1, 1601 // 4) + 1, jnp.int32)
        _ctx_512P = jax.random.normal(jax.random.fold_in(_rk, 11), (4, 16, 128), jnp.float32)
        _ctx_512c = jax.random.dirichlet(jax.random.fold_in(_rk, 511), 0.3 * jnp.ones((16,), jnp.float32), (4, 1601))
        _ctx_512t = jnp.einsum('bsk,bkd->bsd', _ctx_512c, _ctx_512P)
        _ctx_512t = _ctx_512t * jax.lax.rsqrt(jnp.mean(jnp.square(_ctx_512t)) + 1e-12) * 0.953939
        ctx_512 = 0.00222621 + 0.99962 * (_ctx_512t + 0.3 * jax.random.normal(jax.random.fold_in(_rk, 611), (4, 1601, 128), jnp.float32))
        return (x, ctx_512)
    x, ctx_512 = _rec_inputs()

    def _L0_attn_setup():
        import jax, jax.numpy as jnp
        import numpy as np
        D_MODEL = 256
        B, T = (4, 1024)
        LN_EPS = 1e-05
        DEN_EPS = 1e-06
        key = jax.random.key(seed)
        ks = jax.random.split(key, 10)
        s = 1.0 / np.sqrt(D_MODEL)
        return {'x': jax.random.normal(ks[0], (B, T, D_MODEL), dtype=jnp.float32), 'w_qkv': jax.random.normal(ks[1], (D_MODEL, 3 * D_MODEL), dtype=jnp.float32) * s, 'b_qkv': jnp.zeros((3 * D_MODEL,), dtype=jnp.float32), 'w_gate': jax.random.normal(ks[2], (D_MODEL, D_MODEL), dtype=jnp.float32) * s, 'b_gate': jnp.zeros((D_MODEL,), dtype=jnp.float32), 'w_proj': jax.random.normal(ks[3], (D_MODEL, D_MODEL), dtype=jnp.float32) * s, 'b_proj': jnp.zeros((D_MODEL,), dtype=jnp.float32), 'ln_g': jnp.ones((D_MODEL,), dtype=jnp.float32), 'ln_b': jnp.zeros((D_MODEL,), dtype=jnp.float32)}
    _L0_attn_all = _L0_attn_setup()
    _L0_attn_in = {k: v for k, v in _L0_attn_all.items() if k in ('w_qkv', 'b_qkv', 'w_gate', 'b_gate', 'w_proj', 'b_proj', 'ln_g', 'ln_b')}
    del _L0_attn_all

    def _L0_xattn_setup():
        import jax, jax.numpy as jnp
        import numpy as np
        B, T, TC, C, CC, H = (2, 512, 128, 256, 128, 16)
        D = C // H

        def _heads(t):
            b, l, _ = t.shape
            return t.reshape(b, l, H, D).transpose(0, 2, 1, 3)
        key = jax.random.key(seed)
        ks = jax.random.split(key, 18)
        w = lambda k, i, o: jax.random.normal(k, (i, o), jnp.float32) / np.sqrt(i).astype(np.float32)
        return {'x': jax.random.normal(ks[0], (B, T, C), jnp.float32), 'cross_input': jax.random.normal(ks[1], (B, TC, CC), jnp.float32), 'Wk': w(ks[2], C, C), 'bk': jnp.zeros((C,), jnp.float32), 'Wq': w(ks[3], C, C), 'bq': jnp.zeros((C,), jnp.float32), 'Wv': w(ks[4], C, C), 'bv': jnp.zeros((C,), jnp.float32), 'Wck': w(ks[5], CC, C), 'bck': jnp.zeros((C,), jnp.float32), 'Wcq': w(ks[6], C, C), 'bcq': jnp.zeros((C,), jnp.float32), 'Wcv': w(ks[7], CC, C), 'bcv': jnp.zeros((C,), jnp.float32), 'Wp': w(ks[8], C, C), 'bp': jnp.zeros((C,), jnp.float32)}
    _L0_xattn_all = _L0_xattn_setup()
    _L0_xattn_in = {k: v for k, v in _L0_xattn_all.items() if k in ('Wk', 'bk', 'Wq', 'bq', 'Wv', 'bv', 'Wck', 'bck', 'Wcq', 'bcq', 'Wcv', 'bcv', 'Wp', 'bp')}
    del _L0_xattn_all

    def _L0_ffn_setup():
        import jax, jax.numpy as jnp
        import numpy as np
        MICRO_BATCHES = 2
        TOP_K = 2
        LN_EPS = 1e-05
        B, S, D = (4, 1024, 256)
        E = 8
        DFF = 4 * D

        def _layernorm(x, g, b):
            mu = jnp.mean(x, axis=-1, keepdims=True)
            var = jnp.mean(jnp.square(x - mu), axis=-1, keepdims=True)
            return (x - mu) * jax.lax.rsqrt(var + LN_EPS) * g + b
        key = jax.random.key(seed)
        ks = jax.random.split(key, 12)
        sd = 1.0 / np.sqrt(D)
        sf = 1.0 / np.sqrt(DFF)
        return {'x': jax.random.normal(ks[0], (B, S, D), dtype=jnp.float32), 'ln_g': jnp.ones((D,), jnp.float32), 'ln_b': jnp.zeros((D,), jnp.float32), 'attn_w': jax.random.normal(ks[1], (D, D), jnp.float32) * sd, 'attn_b': jnp.zeros((D,), jnp.float32), 'gate_w': jax.random.normal(ks[2], (D, E), jnp.float32) * sd, 'w1': jax.random.normal(ks[3], (E, D, DFF), jnp.float32) * sd, 'b1': jnp.zeros((E, DFF), jnp.float32), 'w2': jax.random.normal(ks[4], (E, DFF, D), jnp.float32) * sf, 'b2': jnp.zeros((E, D), jnp.float32), 'next_w': jax.random.normal(ks[5], (D, D), jnp.float32) * sd, 'next_b': jnp.zeros((D,), jnp.float32)}
    _L0_ffn_all = _L0_ffn_setup()
    _L0_ffn_in = {k: v for k, v in _L0_ffn_all.items() if k in ('ln_g', 'ln_b', 'attn_w', 'attn_b', 'gate_w', 'w1', 'b1', 'w2', 'b2', 'next_w', 'next_b')}
    del _L0_ffn_all

    def _L1_attn_setup():
        import jax, jax.numpy as jnp
        import numpy as np
        D_MODEL = 256
        D_STATE = 64
        D_CONV = 4
        EXPAND = 2
        INNER = EXPAND * D_STATE
        PROJ = D_STATE + 2 * INNER
        B, L = (8, 1024)
        EPS = 0.0001

        def _ssm_forward(x, conv_w, conv_b, in_proj_w, in_proj_b, A_log, out_proj_w, out_proj_b):
            bsz, L_in, _ = x.shape
            pad = (D_CONV - 1) // 2
            xc = jnp.transpose(x, (0, 2, 1))
            xc = jax.lax.conv_general_dilated(xc, conv_w, window_strides=(1,), padding=[(pad, pad)], dimension_numbers=('NCH', 'OIH', 'NCH'), feature_group_count=D_MODEL)
            xc = xc + conv_b[None, :, None]
            Lc = xc.shape[2]
            if Lc < L_in:
                xc = jnp.pad(xc, ((0, 0), (0, 0), (0, L_in - Lc)))
            elif Lc > L_in:
                xc = xc[:, :, :L_in]
            xc = jnp.transpose(xc, (0, 2, 1))
            proj = xc @ in_proj_w.T + in_proj_b
            delta = proj[..., :D_STATE]
            B_in = proj[..., D_STATE:D_STATE + INNER]
            C = proj[..., D_STATE + INNER:]
            n_groups = INNER // D_STATE
            B_in = B_in.reshape(bsz, L_in, D_STATE, n_groups).mean(axis=-1)
            C = C.reshape(bsz, L_in, D_STATE, n_groups).mean(axis=-1)
            A = -jnp.exp(A_log)[None, None, :]
            delta = jax.nn.softplus(delta)
            dA = delta * A
            A_bar = jnp.exp(dA)
            A_safe = jnp.where(jnp.abs(A) < EPS, EPS * jnp.sign(A) + EPS, A)
            scale = (A_bar - 1.0) / A_safe
            taylor = 1.0 + dA / 2.0 + dA * dA / 6.0
            scale = jnp.where(jnp.abs(A) < EPS, taylor, scale)
            B_bar = scale * B_in

            def comb(e1, e2):
                a1, b1 = e1
                a2, b2 = e2
                return (a1 * a2, a2 * b1 + b2)
            _, h = jax.lax.associative_scan(comb, (A_bar, B_bar), axis=1)
            y_state = C * h
            return y_state @ out_proj_w.T + out_proj_b
        key = jax.random.key(seed)
        ks = jax.random.split(key, 6)
        x = jax.random.normal(ks[0], (B, L, D_MODEL), dtype=jnp.float32)
        conv_w = jax.random.normal(ks[1], (D_MODEL, 1, D_CONV), dtype=jnp.float32) / np.sqrt(D_CONV)
        conv_b = jnp.zeros((D_MODEL,), dtype=jnp.float32)
        in_proj_w = jax.random.normal(ks[2], (PROJ, D_MODEL), dtype=jnp.float32) / np.sqrt(D_MODEL)
        in_proj_b = jnp.zeros((PROJ,), dtype=jnp.float32)
        A_log = jax.random.normal(ks[3], (D_STATE,), dtype=jnp.float32) * 0.1
        out_proj_w = jax.random.normal(ks[4], (D_MODEL, D_STATE), dtype=jnp.float32) / np.sqrt(D_STATE)
        out_proj_b = jnp.zeros((D_MODEL,), dtype=jnp.float32)
        return {'x': x, 'conv_w': conv_w, 'conv_b': conv_b, 'in_proj_w': in_proj_w, 'in_proj_b': in_proj_b, 'A_log': A_log, 'out_proj_w': out_proj_w, 'out_proj_b': out_proj_b}
    _L1_attn_all = _L1_attn_setup()
    _L1_attn_in = {k: v for k, v in _L1_attn_all.items() if k in ('conv_w', 'conv_b', 'in_proj_w', 'in_proj_b', 'A_log', 'out_proj_w', 'out_proj_b')}
    del _L1_attn_all

    def _L1_xattn_setup():
        import jax, jax.numpy as jnp
        import numpy as np
        H, D, C1, C2, S, M, B, W = (16, 32, 256, 128, 512, 128, 2, 4)

        def _ln(x, g, b):
            m = jnp.mean(x, -1, keepdims=True)
            v = jnp.var(x, -1, keepdims=True)
            return (x - m) * jax.lax.rsqrt(v + 1e-05) * g + b

        def _mha(x, y, wq, wk, wv, li1_w, li1_b, lnx_g, lnx_b, lny_g, lny_b, ln3_g, ln3_b, li2_w, li2_b, li3_w, li3_b, causal):
            xn = _ln(x, lnx_g, lnx_b)
            yn = _ln(y, lny_g, lny_b)
            q = jnp.einsum('bsc,hcd->bhsd', xn, wq)
            k = jnp.einsum('btc,hcd->bhtd', yn, wk)
            v = jnp.einsum('btc,hcd->bhtd', yn, wv)
            a = jax.nn.softmax(jnp.einsum('bhsd,bhtd->bhst', q, k) * D ** (-0.5), axis=-1)
            if causal:
                s, t = (a.shape[-2], a.shape[-1])
                mask = (jnp.arange(t)[None, :] > jnp.arange(s)[:, None]).astype(a.dtype)
                a = a * mask
            o = jnp.einsum('bhst,bhtd->bhsd', a, v)
            o = o.transpose(0, 2, 1, 3).reshape(x.shape[0], x.shape[1], H * D)
            x_out = x + o @ li1_w + li1_b
            h = jax.nn.gelu(_ln(x_out, ln3_g, ln3_b) @ li2_w + li2_b, approximate=False)
            return x_out + h @ li3_w + li3_b
        key = jax.random.key(seed)
        ks = iter(jax.random.split(key, 64))

        def w(shape, scale=0.02):
            return jax.random.normal(next(ks), shape, jnp.float32) * scale
        inp = {'xx': jax.random.normal(next(ks), (B, S, C1), jnp.float32), 'ee': jax.random.normal(next(ks), (B, M, C2), jnp.float32), 'ln1_g': jnp.ones(C1, jnp.float32), 'ln1_b': jnp.zeros(C1, jnp.float32), 'ln2_g': jnp.ones(C1, jnp.float32), 'ln2_b': jnp.zeros(C1, jnp.float32)}
        for pfx, cy in (('a1', C1), ('a2', C2)):
            inp[pfx + '_wq'] = w((H, C1, D))
            inp[pfx + '_wk'] = w((H, cy, D))
            inp[pfx + '_wv'] = w((H, cy, D))
            inp[pfx + '_li1_w'] = w((H * D, C1))
            inp[pfx + '_li1_b'] = jnp.zeros(C1, jnp.float32)
            inp[pfx + '_lnx_g'] = jnp.ones(C1, jnp.float32)
            inp[pfx + '_lnx_b'] = jnp.zeros(C1, jnp.float32)
            inp[pfx + '_lny_g'] = jnp.ones(cy, jnp.float32)
            inp[pfx + '_lny_b'] = jnp.zeros(cy, jnp.float32)
            inp[pfx + '_ln3_g'] = jnp.ones(C1, jnp.float32)
            inp[pfx + '_ln3_b'] = jnp.zeros(C1, jnp.float32)
            inp[pfx + '_li2_w'] = w((C1, C1 * W))
            inp[pfx + '_li2_b'] = jnp.zeros(C1 * W, jnp.float32)
            inp[pfx + '_li3_w'] = w((C1 * W, C1))
            inp[pfx + '_li3_b'] = jnp.zeros(C1, jnp.float32)
        inp['training'] = 0
        return inp
    _L1_xattn_all = _L1_xattn_setup()
    _L1_xattn_in = {k: v for k, v in _L1_xattn_all.items() if k in ('ln1_g', 'ln1_b', 'ln2_g', 'ln2_b', 'a1_wq', 'a1_wk', 'a1_wv', 'a1_li1_w', 'a1_li1_b', 'a1_lnx_g', 'a1_lnx_b', 'a1_lny_g', 'a1_lny_b', 'a1_ln3_g', 'a1_ln3_b', 'a1_li2_w', 'a1_li2_b', 'a1_li3_w', 'a1_li3_b', 'a2_wq', 'a2_wk', 'a2_wv', 'a2_li1_w', 'a2_li1_b', 'a2_lnx_g', 'a2_lnx_b', 'a2_lny_g', 'a2_lny_b', 'a2_ln3_g', 'a2_ln3_b', 'a2_li2_w', 'a2_li2_b', 'a2_li3_w', 'a2_li3_b')}
    del _L1_xattn_all

    def _L1_ffn_setup():
        import jax, jax.numpy as jnp
        import numpy as np
        D_IN, D_HID = (256, 1024)

        def _ternary(key, shape):
            return jax.random.randint(key, shape, -1, 2).astype(jnp.float32)

        def _tlin(x, w, s):
            return jnp.einsum('bsi,oi->bso', x, w) * s
        key = jax.random.key(seed)
        ks = jax.random.split(key, 12)
        inv = lambda fan: 1.0 / np.sqrt(fan).astype(np.float32)
        return {'x': jax.random.normal(ks[0], (4, 512, D_IN), dtype=jnp.float32), 'w1_w': _ternary(ks[1], (D_HID, D_IN)), 'w1_s': jax.random.uniform(ks[2], (D_HID,), dtype=jnp.float32) * inv(D_IN), 'w2_w': _ternary(ks[3], (D_HID, D_IN)), 'w2_s': jax.random.uniform(ks[4], (D_HID,), dtype=jnp.float32) * inv(D_IN), 'h1_w': _ternary(ks[5], (D_HID, D_HID)), 'h1_s': jax.random.uniform(ks[6], (D_HID,), dtype=jnp.float32) * inv(D_HID), 'h2_w': _ternary(ks[7], (D_HID, D_HID)), 'h2_s': jax.random.uniform(ks[8], (D_HID,), dtype=jnp.float32) * inv(D_HID), 'w3_w': _ternary(ks[9], (D_IN, D_HID)), 'w3_s': jax.random.uniform(ks[10], (D_IN,), dtype=jnp.float32) * inv(D_HID)}
    _L1_ffn_all = _L1_ffn_setup()
    _L1_ffn_in = {k: v for k, v in _L1_ffn_all.items() if k in ('w1_w', 'w1_s', 'w2_w', 'w2_s', 'h1_w', 'h1_s', 'h2_w', 'h2_s', 'w3_w', 'w3_s')}
    del _L1_ffn_all
    return {'x': x, 'ctx_512': ctx_512, 'L0_attn_w_qkv': _L0_attn_in['w_qkv'], 'L0_attn_b_qkv': _L0_attn_in['b_qkv'], 'L0_attn_w_gate': _L0_attn_in['w_gate'], 'L0_attn_b_gate': _L0_attn_in['b_gate'], 'L0_attn_w_proj': _L0_attn_in['w_proj'], 'L0_attn_b_proj': _L0_attn_in['b_proj'], 'L0_attn_ln_g': _L0_attn_in['ln_g'], 'L0_attn_ln_b': _L0_attn_in['ln_b'], 'L0_xattn_Wk': _L0_xattn_in['Wk'], 'L0_xattn_bk': _L0_xattn_in['bk'], 'L0_xattn_Wq': _L0_xattn_in['Wq'], 'L0_xattn_bq': _L0_xattn_in['bq'], 'L0_xattn_Wv': _L0_xattn_in['Wv'], 'L0_xattn_bv': _L0_xattn_in['bv'], 'L0_xattn_Wck': _L0_xattn_in['Wck'], 'L0_xattn_bck': _L0_xattn_in['bck'], 'L0_xattn_Wcq': _L0_xattn_in['Wcq'], 'L0_xattn_bcq': _L0_xattn_in['bcq'], 'L0_xattn_Wcv': _L0_xattn_in['Wcv'], 'L0_xattn_bcv': _L0_xattn_in['bcv'], 'L0_xattn_Wp': _L0_xattn_in['Wp'], 'L0_xattn_bp': _L0_xattn_in['bp'], 'L0_ffn_ln_g': _L0_ffn_in['ln_g'], 'L0_ffn_ln_b': _L0_ffn_in['ln_b'], 'L0_ffn_attn_w': _L0_ffn_in['attn_w'], 'L0_ffn_attn_b': _L0_ffn_in['attn_b'], 'L0_ffn_gate_w': _L0_ffn_in['gate_w'], 'L0_ffn_w1': _L0_ffn_in['w1'], 'L0_ffn_b1': _L0_ffn_in['b1'], 'L0_ffn_w2': _L0_ffn_in['w2'], 'L0_ffn_b2': _L0_ffn_in['b2'], 'L0_ffn_next_w': _L0_ffn_in['next_w'], 'L0_ffn_next_b': _L0_ffn_in['next_b'], 'L1_attn_conv_w': _L1_attn_in['conv_w'], 'L1_attn_conv_b': _L1_attn_in['conv_b'], 'L1_attn_in_proj_w': _L1_attn_in['in_proj_w'], 'L1_attn_in_proj_b': _L1_attn_in['in_proj_b'], 'L1_attn_A_log': _L1_attn_in['A_log'], 'L1_attn_out_proj_w': _L1_attn_in['out_proj_w'], 'L1_attn_out_proj_b': _L1_attn_in['out_proj_b'], 'L1_xattn_ln1_g': _L1_xattn_in['ln1_g'], 'L1_xattn_ln1_b': _L1_xattn_in['ln1_b'], 'L1_xattn_ln2_g': _L1_xattn_in['ln2_g'], 'L1_xattn_ln2_b': _L1_xattn_in['ln2_b'], 'L1_xattn_a1_wq': _L1_xattn_in['a1_wq'], 'L1_xattn_a1_wk': _L1_xattn_in['a1_wk'], 'L1_xattn_a1_wv': _L1_xattn_in['a1_wv'], 'L1_xattn_a1_li1_w': _L1_xattn_in['a1_li1_w'], 'L1_xattn_a1_li1_b': _L1_xattn_in['a1_li1_b'], 'L1_xattn_a1_lnx_g': _L1_xattn_in['a1_lnx_g'], 'L1_xattn_a1_lnx_b': _L1_xattn_in['a1_lnx_b'], 'L1_xattn_a1_lny_g': _L1_xattn_in['a1_lny_g'], 'L1_xattn_a1_lny_b': _L1_xattn_in['a1_lny_b'], 'L1_xattn_a1_ln3_g': _L1_xattn_in['a1_ln3_g'], 'L1_xattn_a1_ln3_b': _L1_xattn_in['a1_ln3_b'], 'L1_xattn_a1_li2_w': _L1_xattn_in['a1_li2_w'], 'L1_xattn_a1_li2_b': _L1_xattn_in['a1_li2_b'], 'L1_xattn_a1_li3_w': _L1_xattn_in['a1_li3_w'], 'L1_xattn_a1_li3_b': _L1_xattn_in['a1_li3_b'], 'L1_xattn_a2_wq': _L1_xattn_in['a2_wq'], 'L1_xattn_a2_wk': _L1_xattn_in['a2_wk'], 'L1_xattn_a2_wv': _L1_xattn_in['a2_wv'], 'L1_xattn_a2_li1_w': _L1_xattn_in['a2_li1_w'], 'L1_xattn_a2_li1_b': _L1_xattn_in['a2_li1_b'], 'L1_xattn_a2_lnx_g': _L1_xattn_in['a2_lnx_g'], 'L1_xattn_a2_lnx_b': _L1_xattn_in['a2_lnx_b'], 'L1_xattn_a2_lny_g': _L1_xattn_in['a2_lny_g'], 'L1_xattn_a2_lny_b': _L1_xattn_in['a2_lny_b'], 'L1_xattn_a2_ln3_g': _L1_xattn_in['a2_ln3_g'], 'L1_xattn_a2_ln3_b': _L1_xattn_in['a2_ln3_b'], 'L1_xattn_a2_li2_w': _L1_xattn_in['a2_li2_w'], 'L1_xattn_a2_li2_b': _L1_xattn_in['a2_li2_b'], 'L1_xattn_a2_li3_w': _L1_xattn_in['a2_li3_w'], 'L1_xattn_a2_li3_b': _L1_xattn_in['a2_li3_b'], 'L1_ffn_w1_w': _L1_ffn_in['w1_w'], 'L1_ffn_w1_s': _L1_ffn_in['w1_s'], 'L1_ffn_w2_w': _L1_ffn_in['w2_w'], 'L1_ffn_w2_s': _L1_ffn_in['w2_s'], 'L1_ffn_h1_w': _L1_ffn_in['h1_w'], 'L1_ffn_h1_s': _L1_ffn_in['h1_s'], 'L1_ffn_h2_w': _L1_ffn_in['h2_w'], 'L1_ffn_h2_s': _L1_ffn_in['h2_s'], 'L1_ffn_w3_w': _L1_ffn_in['w3_w'], 'L1_ffn_w3_s': _L1_ffn_in['w3_s']}

def reference(x, ctx_512, L0_attn_w_qkv, L0_attn_b_qkv, L0_attn_w_gate, L0_attn_b_gate, L0_attn_w_proj, L0_attn_b_proj, L0_attn_ln_g, L0_attn_ln_b, L0_xattn_Wk, L0_xattn_bk, L0_xattn_Wq, L0_xattn_bq, L0_xattn_Wv, L0_xattn_bv, L0_xattn_Wck, L0_xattn_bck, L0_xattn_Wcq, L0_xattn_bcq, L0_xattn_Wcv, L0_xattn_bcv, L0_xattn_Wp, L0_xattn_bp, L0_ffn_ln_g, L0_ffn_ln_b, L0_ffn_attn_w, L0_ffn_attn_b, L0_ffn_gate_w, L0_ffn_w1, L0_ffn_b1, L0_ffn_w2, L0_ffn_b2, L0_ffn_next_w, L0_ffn_next_b, L1_attn_conv_w, L1_attn_conv_b, L1_attn_in_proj_w, L1_attn_in_proj_b, L1_attn_A_log, L1_attn_out_proj_w, L1_attn_out_proj_b, L1_xattn_ln1_g, L1_xattn_ln1_b, L1_xattn_ln2_g, L1_xattn_ln2_b, L1_xattn_a1_wq, L1_xattn_a1_wk, L1_xattn_a1_wv, L1_xattn_a1_li1_w, L1_xattn_a1_li1_b, L1_xattn_a1_lnx_g, L1_xattn_a1_lnx_b, L1_xattn_a1_lny_g, L1_xattn_a1_lny_b, L1_xattn_a1_ln3_g, L1_xattn_a1_ln3_b, L1_xattn_a1_li2_w, L1_xattn_a1_li2_b, L1_xattn_a1_li3_w, L1_xattn_a1_li3_b, L1_xattn_a2_wq, L1_xattn_a2_wk, L1_xattn_a2_wv, L1_xattn_a2_li1_w, L1_xattn_a2_li1_b, L1_xattn_a2_lnx_g, L1_xattn_a2_lnx_b, L1_xattn_a2_lny_g, L1_xattn_a2_lny_b, L1_xattn_a2_ln3_g, L1_xattn_a2_ln3_b, L1_xattn_a2_li2_w, L1_xattn_a2_li2_b, L1_xattn_a2_li3_w, L1_xattn_a2_li3_b, L1_ffn_w1_w, L1_ffn_w1_s, L1_ffn_w2_w, L1_ffn_w2_s, L1_ffn_h1_w, L1_ffn_h1_s, L1_ffn_h2_w, L1_ffn_h2_s, L1_ffn_w3_w, L1_ffn_w3_s):
    import jax
    import jax.numpy as jnp

    def _L0_attn_ref(x, w_qkv, b_qkv, w_gate, b_gate, w_proj, b_proj, ln_g, ln_b):
        import jax, jax.numpy as jnp
        import numpy as np
        D_MODEL = 256
        B, T = (4, 1024)
        LN_EPS = 1e-05
        DEN_EPS = 1e-06
        mu = jnp.mean(x, axis=-1, keepdims=True)
        var = jnp.mean(jnp.square(x - mu), axis=-1, keepdims=True)
        xn = (x - mu) * jax.lax.rsqrt(var + LN_EPS) * ln_g + ln_b
        qkv = xn @ w_qkv + b_qkv
        q, k, v = jnp.split(qkv, 3, axis=-1)
        gate = jax.nn.sigmoid(xn @ w_gate + b_gate)
        k = k * gate
        q = jax.nn.elu(q) + 1.0
        k = jax.nn.elu(k) + 1.0
        attn = jnp.einsum('btd,bsd->bts', q, k)
        tq = jnp.arange(q.shape[1])
        mask = (tq[:, None] >= tq[None, :]).astype(attn.dtype)
        attn = attn * mask
        out_num = jnp.einsum('bts,bsd->btd', attn, v)
        k_cumsum = jnp.cumsum(k, axis=1)
        out_den = jnp.sum(q * k_cumsum, axis=-1, keepdims=True) + DEN_EPS
        return out_num / out_den @ w_proj + b_proj

    def _L0_xattn_ref(x, cross_input, Wk, bk, Wq, bq, Wv, bv, Wck, bck, Wcq, bcq, Wcv, bcv, Wp, bp):
        import jax, jax.numpy as jnp
        import numpy as np
        B, T, TC, C, CC, H = (2, 512, 128, 256, 128, 16)
        D = C // H

        def _heads(t):
            b, l, _ = t.shape
            return t.reshape(b, l, H, D).transpose(0, 2, 1, 3)
        scale = np.float32(1.0 / np.sqrt(D))
        q = _heads(x @ Wq + bq)
        k = _heads(x @ Wk + bk)
        v = _heads(x @ Wv + bv)
        att = jnp.einsum('bhqd,bhkd->bhqk', q, k) * scale
        causal = jnp.tril(jnp.ones((T, T), bool))
        att = jnp.where(causal[None, None], att, -jnp.inf)
        y = jnp.einsum('bhqk,bhkd->bhqd', jax.nn.softmax(att, axis=-1), v)
        qc = _heads(x @ Wcq + bcq)
        kc = _heads(cross_input @ Wck + bck)
        vc = _heads(cross_input @ Wcv + bcv)
        attc = jnp.einsum('bhqd,bhkd->bhqk', qc, kc) * scale
        y = y + jnp.einsum('bhqk,bhkd->bhqd', jax.nn.softmax(attc, axis=-1), vc)
        y = y.transpose(0, 2, 1, 3).reshape(x.shape[0], T, C)
        return y @ Wp + bp

    def _L0_ffn_ref(x, ln_g, ln_b, attn_w, attn_b, gate_w, w1, b1, w2, b2, next_w, next_b):
        import jax, jax.numpy as jnp
        import numpy as np
        MICRO_BATCHES = 2
        TOP_K = 2
        LN_EPS = 1e-05
        B, S, D = (4, 1024, 256)
        E = 8
        DFF = 4 * D

        def _layernorm(x, g, b):
            mu = jnp.mean(x, axis=-1, keepdims=True)
            var = jnp.mean(jnp.square(x - mu), axis=-1, keepdims=True)
            return (x - mu) * jax.lax.rsqrt(var + LN_EPS) * g + b
        Bx, Sx, Dx = x.shape
        N = Bx * Sx
        x_flat = x.reshape(N, Dx)
        x_attn = _layernorm(x_flat, ln_g, ln_b) @ attn_w + attn_b + x_flat
        logits = x_attn @ gate_w
        _ = jax.lax.top_k(logits, TOP_K)
        tpe = N // (MICRO_BATCHES * E)
        g = x_attn.reshape(MICRO_BATCHES, E, tpe, Dx)
        h = jax.nn.gelu(jnp.einsum('metd,edf->metf', g, w1) + b1[None, :, None, :], approximate=False)
        y = jnp.einsum('metf,efd->metd', h, w2) + b2[None, :, None, :]
        out = jax.nn.gelu(y @ next_w + next_b, approximate=False)
        return out.reshape(Bx, Sx, Dx)

    def _L1_attn_ref(x, conv_w, conv_b, in_proj_w, in_proj_b, A_log, out_proj_w, out_proj_b):
        import jax, jax.numpy as jnp
        import numpy as np
        D_MODEL = 256
        D_STATE = 64
        D_CONV = 4
        EXPAND = 2
        INNER = EXPAND * D_STATE
        PROJ = D_STATE + 2 * INNER
        B, L = (8, 1024)
        EPS = 0.0001

        def _ssm_forward(x, conv_w, conv_b, in_proj_w, in_proj_b, A_log, out_proj_w, out_proj_b):
            bsz, L_in, _ = x.shape
            pad = (D_CONV - 1) // 2
            xc = jnp.transpose(x, (0, 2, 1))
            xc = jax.lax.conv_general_dilated(xc, conv_w, window_strides=(1,), padding=[(pad, pad)], dimension_numbers=('NCH', 'OIH', 'NCH'), feature_group_count=D_MODEL)
            xc = xc + conv_b[None, :, None]
            Lc = xc.shape[2]
            if Lc < L_in:
                xc = jnp.pad(xc, ((0, 0), (0, 0), (0, L_in - Lc)))
            elif Lc > L_in:
                xc = xc[:, :, :L_in]
            xc = jnp.transpose(xc, (0, 2, 1))
            proj = xc @ in_proj_w.T + in_proj_b
            delta = proj[..., :D_STATE]
            B_in = proj[..., D_STATE:D_STATE + INNER]
            C = proj[..., D_STATE + INNER:]
            n_groups = INNER // D_STATE
            B_in = B_in.reshape(bsz, L_in, D_STATE, n_groups).mean(axis=-1)
            C = C.reshape(bsz, L_in, D_STATE, n_groups).mean(axis=-1)
            A = -jnp.exp(A_log)[None, None, :]
            delta = jax.nn.softplus(delta)
            dA = delta * A
            A_bar = jnp.exp(dA)
            A_safe = jnp.where(jnp.abs(A) < EPS, EPS * jnp.sign(A) + EPS, A)
            scale = (A_bar - 1.0) / A_safe
            taylor = 1.0 + dA / 2.0 + dA * dA / 6.0
            scale = jnp.where(jnp.abs(A) < EPS, taylor, scale)
            B_bar = scale * B_in

            def comb(e1, e2):
                a1, b1 = e1
                a2, b2 = e2
                return (a1 * a2, a2 * b1 + b2)
            _, h = jax.lax.associative_scan(comb, (A_bar, B_bar), axis=1)
            y_state = C * h
            return y_state @ out_proj_w.T + out_proj_b
        return _ssm_forward(x, conv_w, conv_b, in_proj_w, in_proj_b, A_log, out_proj_w, out_proj_b)

    def _L1_xattn_ref(xx, ee, ln1_g, ln1_b, ln2_g, ln2_b, a1_wq, a1_wk, a1_wv, a1_li1_w, a1_li1_b, a1_lnx_g, a1_lnx_b, a1_lny_g, a1_lny_b, a1_ln3_g, a1_ln3_b, a1_li2_w, a1_li2_b, a1_li3_w, a1_li3_b, a2_wq, a2_wk, a2_wv, a2_li1_w, a2_li1_b, a2_lnx_g, a2_lnx_b, a2_lny_g, a2_lny_b, a2_ln3_g, a2_ln3_b, a2_li2_w, a2_li2_b, a2_li3_w, a2_li3_b, training):
        import jax, jax.numpy as jnp
        import numpy as np
        H, D, C1, C2, S, M, B, W = (16, 32, 256, 128, 512, 128, 2, 4)

        def _ln(x, g, b):
            m = jnp.mean(x, -1, keepdims=True)
            v = jnp.var(x, -1, keepdims=True)
            return (x - m) * jax.lax.rsqrt(v + 1e-05) * g + b

        def _mha(x, y, wq, wk, wv, li1_w, li1_b, lnx_g, lnx_b, lny_g, lny_b, ln3_g, ln3_b, li2_w, li2_b, li3_w, li3_b, causal):
            xn = _ln(x, lnx_g, lnx_b)
            yn = _ln(y, lny_g, lny_b)
            q = jnp.einsum('bsc,hcd->bhsd', xn, wq)
            k = jnp.einsum('btc,hcd->bhtd', yn, wk)
            v = jnp.einsum('btc,hcd->bhtd', yn, wv)
            a = jax.nn.softmax(jnp.einsum('bhsd,bhtd->bhst', q, k) * D ** (-0.5), axis=-1)
            if causal:
                s, t = (a.shape[-2], a.shape[-1])
                mask = (jnp.arange(t)[None, :] > jnp.arange(s)[:, None]).astype(a.dtype)
                a = a * mask
            o = jnp.einsum('bhst,bhtd->bhsd', a, v)
            o = o.transpose(0, 2, 1, 3).reshape(x.shape[0], x.shape[1], H * D)
            x_out = x + o @ li1_w + li1_b
            h = jax.nn.gelu(_ln(x_out, ln3_g, ln3_b) @ li2_w + li2_b, approximate=False)
            return x_out + h @ li3_w + li3_b
        x = _ln(xx, ln1_g, ln1_b)
        x = x + _mha(x, x, a1_wq, a1_wk, a1_wv, a1_li1_w, a1_li1_b, a1_lnx_g, a1_lnx_b, a1_lny_g, a1_lny_b, a1_ln3_g, a1_ln3_b, a1_li2_w, a1_li2_b, a1_li3_w, a1_li3_b, causal=True)
        x = _ln(x, ln2_g, ln2_b)
        return x + _mha(x, ee, a2_wq, a2_wk, a2_wv, a2_li1_w, a2_li1_b, a2_lnx_g, a2_lnx_b, a2_lny_g, a2_lny_b, a2_ln3_g, a2_ln3_b, a2_li2_w, a2_li2_b, a2_li3_w, a2_li3_b, causal=False)

    def _L1_ffn_ref(x, w1_w, w1_s, w2_w, w2_s, h1_w, h1_s, h2_w, h2_s, w3_w, w3_s):
        import jax, jax.numpy as jnp
        import numpy as np
        D_IN, D_HID = (256, 1024)

        def _ternary(key, shape):
            return jax.random.randint(key, shape, -1, 2).astype(jnp.float32)

        def _tlin(x, w, s):
            return jnp.einsum('bsi,oi->bso', x, w) * s
        h = jax.nn.silu(_tlin(x, w1_w, w1_s)) * _tlin(x, w2_w, w2_s)
        h = jax.nn.gelu(_tlin(h, h1_w, h1_s), approximate=False)
        h = jax.nn.gelu(_tlin(h, h2_w, h2_s), approximate=False)
        return _tlin(h, w3_w, w3_s)
    x = _layernorm(x + _L0_attn_ref(x, L0_attn_w_qkv, L0_attn_b_qkv, L0_attn_w_gate, L0_attn_b_gate, L0_attn_w_proj, L0_attn_b_proj, L0_attn_ln_g, L0_attn_ln_b), axis=-1)
    x = _layernorm(x + _L0_xattn_ref(x, ctx_512, L0_xattn_Wk, L0_xattn_bk, L0_xattn_Wq, L0_xattn_bq, L0_xattn_Wv, L0_xattn_bv, L0_xattn_Wck, L0_xattn_bck, L0_xattn_Wcq, L0_xattn_bcq, L0_xattn_Wcv, L0_xattn_bcv, L0_xattn_Wp, L0_xattn_bp), axis=-1)
    x = _layernorm(x + _L0_ffn_ref(x, L0_ffn_ln_g, L0_ffn_ln_b, L0_ffn_attn_w, L0_ffn_attn_b, L0_ffn_gate_w, L0_ffn_w1, L0_ffn_b1, L0_ffn_w2, L0_ffn_b2, L0_ffn_next_w, L0_ffn_next_b), axis=-1)
    x = _layernorm(x + _L1_attn_ref(x, L1_attn_conv_w, L1_attn_conv_b, L1_attn_in_proj_w, L1_attn_in_proj_b, L1_attn_A_log, L1_attn_out_proj_w, L1_attn_out_proj_b), axis=-1)
    x = _layernorm(x + _L1_xattn_ref(x, ctx_512, L1_xattn_ln1_g, L1_xattn_ln1_b, L1_xattn_ln2_g, L1_xattn_ln2_b, L1_xattn_a1_wq, L1_xattn_a1_wk, L1_xattn_a1_wv, L1_xattn_a1_li1_w, L1_xattn_a1_li1_b, L1_xattn_a1_lnx_g, L1_xattn_a1_lnx_b, L1_xattn_a1_lny_g, L1_xattn_a1_lny_b, L1_xattn_a1_ln3_g, L1_xattn_a1_ln3_b, L1_xattn_a1_li2_w, L1_xattn_a1_li2_b, L1_xattn_a1_li3_w, L1_xattn_a1_li3_b, L1_xattn_a2_wq, L1_xattn_a2_wk, L1_xattn_a2_wv, L1_xattn_a2_li1_w, L1_xattn_a2_li1_b, L1_xattn_a2_lnx_g, L1_xattn_a2_lnx_b, L1_xattn_a2_lny_g, L1_xattn_a2_lny_b, L1_xattn_a2_ln3_g, L1_xattn_a2_ln3_b, L1_xattn_a2_li2_w, L1_xattn_a2_li2_b, L1_xattn_a2_li3_w, L1_xattn_a2_li3_b, 0), axis=-1)
    x = _layernorm(x + _L1_ffn_ref(x, L1_ffn_w1_w, L1_ffn_w1_s, L1_ffn_w2_w, L1_ffn_w2_s, L1_ffn_h1_w, L1_ffn_h1_s, L1_ffn_h2_w, L1_ffn_h2_s, L1_ffn_w3_w, L1_ffn_w3_s), axis=-1)
    return x

_drawn_inputs = setup_inputs


def setup_inputs(seed=0):
    import zlib

    import numpy as np

    out = dict(_drawn_inputs(seed))
    spreads = {'L0_attn_b_qkv': (0.0, 0.1),
     'L0_attn_b_gate': (0.0, 0.8),
     'L0_attn_b_proj': (0.0, 0.1),
     'L0_attn_ln_g': (1.0, 0.2),
     'L0_attn_ln_b': (0.0, 0.1),
     'L0_xattn_bk': (0.0, 0.8),
     'L0_xattn_bq': (0.0, 0.608),
     'L0_xattn_bv': (0.0, 0.1),
     'L0_xattn_bck': (0.0, 0.8),
     'L0_xattn_bcq': (0.0, 0.374),
     'L0_xattn_bcv': (0.0, 0.1),
     'L0_xattn_bp': (0.0, 0.1),
     'L0_ffn_ln_g': (1.0, 0.2),
     'L0_ffn_ln_b': (0.0, 0.1),
     'L0_ffn_attn_b': (0.0, 0.1),
     'L0_ffn_b1': (0.0, 0.1),
     'L0_ffn_b2': (0.0, 0.1),
     'L0_ffn_next_b': (0.0, 0.1),
     'L1_attn_conv_b': (0.0, 0.1),
     'L1_attn_in_proj_b': (0.0, 0.1),
     'L1_attn_out_proj_b': (0.0, 0.1),
     'L1_xattn_ln1_g': (1.0, 0.2),
     'L1_xattn_ln1_b': (0.0, 0.1),
     'L1_xattn_ln2_g': (1.0, 0.2),
     'L1_xattn_ln2_b': (0.0, 0.1),
     'L1_xattn_a1_li1_b': (0.0, 0.271),
     'L1_xattn_a1_lnx_g': (1.0, 0.6),
     'L1_xattn_a1_lnx_b': (0.0, 0.8),
     'L1_xattn_a1_lny_g': (1.0, 0.6),
     'L1_xattn_a1_lny_b': (0.0, 0.8),
     'L1_xattn_a1_ln3_g': (1.0, 0.6),
     'L1_xattn_a1_ln3_b': (0.0, 0.8),
     'L1_xattn_a1_li2_b': (0.0, 0.702),
     'L1_xattn_a1_li3_b': (0.0, 0.1),
     'L1_xattn_a2_li1_b': (0.0, 0.1),
     'L1_xattn_a2_lnx_g': (1.0, 0.6),
     'L1_xattn_a2_lnx_b': (0.0, 0.8),
     'L1_xattn_a2_lny_g': (1.0, 0.6),
     'L1_xattn_a2_lny_b': (0.0, 0.8),
     'L1_xattn_a2_ln3_g': (1.0, 0.6),
     'L1_xattn_a2_ln3_b': (0.0, 0.8),
     'L1_xattn_a2_li2_b': (0.0, 0.675),
     'L1_xattn_a2_li3_b': (0.0, 0.1)}
    factors = {'L0_attn_w_gate': 8.0,
     'L1_xattn_a1_wq': 8.0,
     'L1_xattn_a1_wk': 8.0,
     'L1_xattn_a1_wv': 4.424,
     'L1_xattn_a1_li1_w': 4.413,
     'L1_xattn_a2_wq': 8.0,
     'L1_xattn_a2_wk': 8.0,
     'L1_xattn_a2_wv': 3.336,
     'L1_xattn_a2_li1_w': 3.223,
     'L1_ffn_w1_w': 8.0,
     'L1_ffn_w1_s': 8.0,
     'L1_ffn_w2_w': 8.0,
     'L1_ffn_w2_s': 8.0,
     'L1_ffn_h1_w': 8.0,
     'L1_ffn_h1_s': 8.0,
     'L1_ffn_h2_w': 8.0,
     'L1_ffn_h2_s': 8.0,
     'L1_ffn_w3_w': 8.0,
     'L1_ffn_w3_s': 8.0}
    for name, (base, spread) in spreads.items():
        noise = np.random.default_rng([zlib.crc32(name.encode()), seed]).standard_normal(out[name].shape)
        drawn = base * np.exp(spread * noise) if base else spread * noise
        out[name] = jnp.asarray(drawn.astype(out[name].dtype))
    for name, factor in factors.items():
        out[name] = (out[name] * factor).astype(out[name].dtype)
    return out
```

```python
from contextlib import ExitStack

import numpy as np

import concourse.bass as bass
from concourse import mybir

F32 = mybir.dt.float32
F32R = mybir.dt.float32r
BF16 = mybir.dt.bfloat16
ALU = mybir.AluOpType
ACT = mybir.ActivationFunctionType
AX = mybir.AxisListType

P = 128
NB, T, C = 4, 512, 256
TB = T // P
NT = NB * TB
KC = C // P
H, HG = 16, 4
NG = H // HG
CTX, CC = 1601, 128
CTXE = CTX + 1
CB = (CTX + P - 1) // P
KEY_CUTS = [(0, 384), (384, 384), (768, 384), (1152, 450)]
E = 8
LN_EPS = 1e-5
DEN_EPS = 1e-6
MAXROW = 96
NEG = -1e30
EARLY_TO, A_FROM, A_TO = 0.5, 0.0, 0.95
SS = 64
FF = 4 * C

COLS = [
    ("L0_attn_ln_g", 256), ("L0_attn_ln_b", 256), ("L0_attn_bq", 256), ("L0_attn_bk", 256),
    ("L0_attn_b_gate", 256),
    ("L0_xattn_bq", 256), ("L0_xattn_bk", 256), ("L0_xattn_bcq", 256), ("L0_xattn_bck", 256),
    ("L0_ffn_ln_g", 256), ("L0_ffn_ln_b", 256), ("L0_ffn_attn_b", 256),
    ("L0_ffn_b1", 8 * 1024), ("L0_ffn_b2", 8 * 256),
    ("conv0", 256), ("conv1", 256), ("conv2", 256), ("conv3", 256), ("L1_attn_conv_b", 256),
    ("ssm_bd", 128), ("ssm_bb0", 128), ("ssm_bb1", 128), ("ssm_bc0", 128), ("ssm_bc1", 128),
    ("ssm_alog", 128),
    ("a1_lnx_g", 256), ("a1_lnx_b", 256), ("a1_lny_g", 256), ("a1_lny_b", 256),
    ("a1_ln3_g", 256), ("a1_ln3_b", 256), ("a1_li2_b", 1024),
    ("a2_lnx_g", 256), ("a2_lnx_b", 256), ("a2_lny_g", 128), ("a2_lny_b", 128),
    ("a2_ln3_g", 256), ("a2_ln3_b", 256), ("a2_li2_b", 1024),
    ("w1_s", 1024), ("w2_s", 1024), ("h1_s", 1024), ("h2_s", 1024),
]
COL_AT = {}
for _name, _n in COLS:
    COL_AT[_name] = (sum(n // P for _, n in COLS[:len(COL_AT)]), _n // P)
NCOLS = sum(n // P for _, n in COLS)


class Lane:

    def __init__(self, nc, ctx, name, eng):
        self.eng, self.sem, self.count, self.seen = eng, ctx.enter_context(nc.semaphore(f"{name}_done")), 0, {}

    def mark(self, ins):
        ins.then_inc(self.sem, 1)
        self.count += 1
        return (self.sem, self.count)

    def wait(self, *tokens):
        for token in tokens:
            if token is None:
                continue
            if isinstance(token, list):
                self.wait(*token)
                continue
            sem, value = token
            if self.seen.get(sem.name, 0) < value:
                self.seen[sem.name] = value
                self.eng.wait_ge(sem, value)


class Arrivals:

    def __init__(self, nc, ctx, name):
        self.sem, self.count = ctx.enter_context(nc.semaphore(name)), 0

    def load(self, lane, out, in_):
        lane.eng.dma_start(out, in_).then_inc(self.sem, 16)
        self.count += 16
        return self.token()

    def token(self):
        return (self.sem, self.count)


class Slot:

    def __init__(self, tile, landed=None):
        self.tile, self.free, self.landed = tile, [], landed


class Ring:
    def __init__(self, slots):
        self.slots, self.at = slots, 0

    def take(self, lane=None):
        slot = self.slots[self.at % len(self.slots)]
        self.at += 1
        if lane is not None:
            lane.wait(slot.free)
        return slot


def drive(gens, width):
    waiting, running = list(gens), []
    while waiting or running:
        while waiting and len(running) < width:
            running.append(waiting.pop(0))
        for g in list(running):
            try:
                next(g)
            except StopIteration:
                running.remove(g)


HELD = "held"


def beside(main, n_main, sides):
    sides = [[g, n, lo, hi, 0] for g, n, lo, hi in sides if g is not None]
    done = 0
    for _ in main:
        done += 1
        for side in sides:
            g, n, lo, hi, out = side
            part = (done / n_main - lo) / (hi - lo)
            while side[4] < n * part:
                try:
                    if next(g) == HELD:
                        break
                    side[4] += 1
                except StopIteration:
                    side[4] = float("inf")
    for side in sides:
        for _ in side[0]:
            pass


class Decoder:
    def __init__(self, nc, ctx, a, out, last_stage=99):
        self.nc, self.a, self.out, self.last_stage = nc, a, out, last_stage
        self.pe = Lane(nc, ctx, "pe", nc.tensor)
        self.act = Lane(nc, ctx, "act", nc.scalar)
        self.dve = Lane(nc, ctx, "dve", nc.vector)
        self.pool = Lane(nc, ctx, "pool", nc.gpsimd)
        self.sp = Lane(nc, ctx, "sp", nc.sync)
        self.ctx = ctx
        self.banks = [Slot(ctx.enter_context(nc.psum_tensor(f"bank{i}", [P, 512], F32))) for i in range(8)]
        self.dma_sems = []
        self.fences = 0

    def sb(self, scope, name, shape, dt=F32):
        return scope.enter_context(self.nc.sbuf_tensor(name, shape, dt))

    def arrivals(self, name):
        a = Arrivals(self.nc, self.ctx, name)
        self.dma_sems.append(a)
        return a

    def fence(self):
        lanes = [self.pe, self.act, self.dve, self.pool]
        last = [(l.sem, l.count) for l in lanes if l.count] + [d.token() for d in self.dma_sems if d.count]
        for lane in lanes + [self.sp]:
            lane.wait(last)
        for b in self.banks:
            b.free = []

    def col(self, name, i=0, rows=P):
        at, n = COL_AT[name]
        return self.cols[0:rows, at + i:at + i + 1]

    def constants(self):
        sb, pool, dve = self.sb, self.pool, self.dve
        ctx = self.ctx
        self.cols = sb(ctx, "cols", [P, NCOLS])
        self.X = sb(ctx, "X", [P, NT, C])
        self.ident = sb(ctx, "ident", [P, P])
        self.identb = sb(ctx, "identb", [P, P], BF16)
        self.ones = sb(ctx, "ones", [P, P])
        self.neghalf = sb(ctx, "neghalf", [P, 4])
        self.x_in = self.arrivals("x_landed")
        self.cols_in = self.arrivals("cols_landed")
        xv = self.a["x"].rearrange("b (t p) c -> p (b t) c", p=P)
        for b in range(NB):
            self.x_in.load(self.sp, self.X[:, TB * b:TB * b + TB, :], xv[:, TB * b:TB * b + TB, :])
        self.cols_in.load(self.sp, self.cols[:, :], self.a["cols"])
        g = self.nc.gpsimd
        zero = pool.mark(g.memset(self.ident[:, :], 0.0))
        pool.mark(g.memset(self.ones[:, :], 1.0))
        pool.mark(g.memset(self.neghalf[:, :], -0.5))
        pool.wait(zero)
        t = pool.mark(g.affine_select(out=self.ident[:, :], in_=self.ident[:, :], compare_op=ALU.not_equal,
                                      fill=1.0, base=0, pattern=[[-1, P]], channel_multiplier=1))
        pool.wait(t)
        t = pool.mark(g.tensor_copy(self.identb[:, :], self.ident[:, :]))
        for lane in (self.pe, self.act, self.dve, self.pool):
            lane.wait(t, self.x_in.token(), self.cols_in.token())
        self.stat = Ring([Slot((sb(ctx, f"st{i}", [P, 4, 6]), sb(ctx, f"mv{i}", [P, 4, 2]),
                                sb(ctx, f"ve{i}", [P, 4]), sb(ctx, f"rs{i}", [P, 4]))) for i in range(4)])

    def stats(self, rows, n, after, np_=P):
        dve, pool, v = self.dve, self.pool, self.nc.vector
        slot = self.stat.take(dve)
        st, mv, ve, rs = slot.tile
        for i in range(n):
            dve.wait(after[i])
            t = dve.mark(v.bn_stats(st[0:np_, i, :], rows(i)))
        dve.wait(t)
        for i in range(n):
            t = dve.mark(v.bn_aggr(mv[0:np_, i, :], st[0:np_, i, :]))
        dve.wait(t)
        t = dve.mark(v.tensor_scalar(ve[0:np_, 0:n], mv[0:np_, 0:n, 1], LN_EPS, None, ALU.add))
        pool.wait(t)
        t = pool.mark(self.nc.gpsimd.tensor_tensor(rs[0:np_, 0:n], ve[0:np_, 0:n], self.neghalf[0:np_, 0:n], ALU.pow))
        return slot, t

    def normalize(self, slot, t, out, rows, n, np_=P):
        dve, v = self.dve, self.nc.vector
        _, mv, _, rs = slot.tile
        dve.wait(t)
        done = [dve.mark(v.tensor_scalar(out(i), rows(i), mv[0:np_, i, 0:1], rs[0:np_, i:i + 1],
                                         ALU.subtract, ALU.mult)) for i in range(n)]
        slot.free = [done[-1]]
        return done

    def turn(self, ring, src, after, evac):
        pe = self.pe
        for c in range(KC):
            bank = ring.take(pe)
            for i in range(TB):
                pe.wait(after[i])
                m = self.nc.tensor.transpose(bank.tile[:, P * i:P * i + P], src[:, i, P * c:P * c + P], self.ident[:, :])
            bank.free = [evac(c, bank.tile, pe.mark(m))]

    def product(self, bank, pairs, after):
        self.pe.wait(after)
        for k, (l, r) in enumerate(pairs):
            m = self.nc.tensor.matmul(bank, l, r, start=k == 0, stop=k == len(pairs) - 1)
        return self.pe.mark(m)

    def rows(self, scope, names, tag):
        tile = self.sb(scope, f"rows_{tag}", [P, len(names), C])
        landed = self.arrivals(f"rows_{tag}_landed")
        for i, n in enumerate(names):
            landed.load(self.sp, tile[:, i, :], self.a[n].rearrange("(o c) -> o c", o=1).to_broadcast([P, C]))
        return {n: tile[:, i, :] for i, n in enumerate(names)}, landed.token()

    def weight(self, scope, landed, name, shape):
        tile = self.sb(scope, f"w_{name}", shape)
        landed.load(self.sp, tile[:], self.a[name])
        return tile

    def linear_attention(self, scope):
        nc, pe, act, dve, pool = self.nc, self.pe, self.act, self.dve, self.pool
        sb = lambda n, s, d=F32: self.sb(scope, "la_" + n, s, d)
        landed = self.arrivals("la_weights")
        wqkv = self.weight(scope, landed, "L0_attn_w_qkv", [P, KC, 3 * C])
        wg = self.weight(scope, landed, "L0_attn_w_gate", [P, KC, C])
        wp = self.weight(scope, landed, "L0_attn_w_proj", [P, KC, C])
        row, rows_in = self.rows(scope, ["L0_attn_bv", "L0_attn_b_proj"], "la")
        mask = sb("mask", [P, P])
        nbg = sb("nbg", [P, KC])
        t = pool.mark(nc.gpsimd.memset(mask[:, :], 1.0))
        pool.wait(t)
        mask_t = pool.mark(nc.gpsimd.affine_select(out=mask[:, :], in_=mask[:, :], compare_op=ALU.is_ge, fill=0.0,
                                                   base=0, pattern=[[1, P]], channel_multiplier=-1))
        at, n = COL_AT["L0_attn_b_gate"]
        nbg_t = dve.mark(nc.vector.tensor_scalar(nbg[:, :], self.cols[:, at:at + n], -1.0, None, ALU.mult))
        act.wait(nbg_t)
        dve.wait(mask_t, rows_in)
        pool.wait(rows_in)
        pe.wait(landed.token())
        psum = Ring(self.banks)
        sets = [dict(xh=sb(f"xh{i}", [P, TB, C]), xn=sb(f"xn{i}", [P, KC, T]), q=sb(f"q{i}", [P, KC, T]),
                     k=sb(f"k{i}", [P, KC, T]), v=sb(f"v{i}", [P, TB, C]), s=sb(f"s{i}", [P, TB, T]),
                     rd=sb(f"rd{i}", [P, T]), o=sb(f"o{i}", [P, KC, T]), xb=sb(f"xb{i}", [P, TB, C]),
                     done=[]) for i in range(2)]
        exps = Ring([Slot(sb(f"e{i}", [P, T])) for i in range(3)])
        relus = Ring([Slot(sb(f"r{i}", [P, T])) for i in range(3)])
        gates = Ring([Slot(sb(f"g{i}", [P, T])) for i in range(3)])

        def elu1(src, src_t, bias, dst):
            e, r = exps.take(act), relus.take(dve)
            act.wait(src_t)
            et = act.mark(nc.scalar.activation(e.tile[:, :], src, ACT.Exp, bias=bias))
            dve.wait(src_t, et)
            rt = dve.mark(nc.vector.tensor_scalar(r.tile[:, :], src, bias, 0.0, ALU.add, ALU.max))
            dve.wait(rt)
            t = dve.mark(nc.vector.scalar_tensor_tensor(out=dst, in0=e.tile[:, :], scalar=1.0, in1=r.tile[:, :],
                                                        op0=ALU.min, op1=ALU.add))
            e.free, r.free = [t], [t]
            return t

        def batch(b):
            u = sets[b % 2]
            x = self.X[:, TB * b:TB * b + TB, :]
            for lane in (dve, act, pool):
                lane.wait(u["done"])
            xb_t = [pool.mark(nc.gpsimd.tensor_tensor(u["xb"][:, i, :], x[:, i, :], row["L0_attn_b_proj"], ALU.add))
                    for i in range(TB)]
            slot, t = self.stats(lambda i: x[:, i, :], TB, [None] * TB)
            yield
            xh_t = self.normalize(slot, t, lambda i: u["xh"][:, i, :], lambda i: x[:, i, :], TB)
            xn_t = []

            def evac(c, bank, t):
                act.wait(t)
                xn_t.append(act.mark(nc.scalar.activation(u["xn"][:, c, :], bank[:, :], ACT.Identity,
                                                          scale=self.col("L0_attn_ln_g", c),
                                                          bias=self.col("L0_attn_ln_b", c))))
                return xn_t[-1]
            self.turn(psum, u["xh"], xh_t, evac)
            yield
            xn = lambda k: u["xn"][:, k, :]
            k_t = []
            for c in range(KC):
                cs = slice(P * c, P * c + P)
                bank = psum.take(pe)
                t = self.product(bank.tile[:, :], [(wg[:, k, cs], xn(k)) for k in range(KC)], xn_t)
                g = gates.take(act)
                act.wait(t)
                t = act.mark(nc.scalar.activation(g.tile[:, :], bank.tile[:, :], ACT.Exp, scale=-1.0,
                                                  bias=nbg[:, c:c + 1]))
                bank.free = [t]
                dve.wait(t)
                t = dve.mark(nc.vector.tensor_scalar(g.tile[:, :], g.tile[:, :], 1.0, None, ALU.add))
                dve.wait(t)
                gt = dve.mark(nc.vector.reciprocal(g.tile[:, :], g.tile[:, :]))
                bank = psum.take(pe)
                t = self.product(bank.tile[:, :], [(wqkv[:, k, C + P * c:C + P * c + P], xn(k)) for k in range(KC)], xn_t)
                dve.wait(t, gt)
                t = dve.mark(nc.vector.scalar_tensor_tensor(out=g.tile[:, :], in0=bank.tile[:, :],
                                                            scalar=self.col("L0_attn_bk", c), in1=g.tile[:, :],
                                                            op0=ALU.add, op1=ALU.mult))
                bank.free = [t]
                k_t.append(elu1(g.tile[:, :], t, 0.0, u["k"][:, c, :]))
                g.free = [k_t[-1]]
                yield
            q_t = []
            for c in range(KC):
                bank = psum.take(pe)
                t = self.product(bank.tile[:, :], [(wqkv[:, k, P * c:P * c + P], xn(k)) for k in range(KC)], xn_t)
                q_t.append(elu1(bank.tile[:, :], t, self.col("L0_attn_bq", c), u["q"][:, c, :]))
                bank.free = [q_t[-1]]
                yield
            v_t = []
            for i in range(TB):
                bank = psum.take(pe)
                t = self.product(bank.tile[:, 0:C], [(u["xn"][:, k, P * i:P * i + P], wqkv[:, k, 2 * C:3 * C])
                                                     for k in range(KC)], xn_t)
                dve.wait(t)
                v_t.append(dve.mark(nc.vector.tensor_tensor(u["v"][:, i, :], bank.tile[:, 0:C], row["L0_attn_bv"], ALU.add)))
                bank.free = [v_t[-1]]
            yield
            s_t = []
            for j in range(TB):
                w = T - P * j
                bank = psum.take(pe)
                t = self.product(bank.tile[:, 0:w], [(u["k"][:, k, P * j:P * j + P], u["q"][:, k, P * j:T])
                                                     for k in range(KC)], k_t + q_t)
                dve.wait(t)
                s_t.append(dve.mark(nc.vector.tensor_tensor(u["s"][:, j, P * j:P * j + P], bank.tile[:, 0:P],
                                                            mask[:, :], ALU.mult)))
                bank.free = [s_t[-1]]
                if w > P:
                    act.wait(s_t[-1])
                    s_t.append(act.mark(nc.scalar.activation(u["s"][:, j, P * j + P:T], bank.tile[:, P:w], ACT.Copy)))
                    bank.free = [s_t[-1], s_t[-2]]
            yield
            bank = psum.take(pe)
            pe.wait(s_t)
            for j in range(TB):
                m = nc.tensor.matmul(bank.tile[:, P * j:T], self.ones[:, :], u["s"][:, j, P * j:T], start=j == 0,
                                     stop=j == TB - 1, skip_group_check=True)
            t = pe.mark(m)
            dve.wait(t)
            t = dve.mark(nc.vector.tensor_scalar(u["rd"][:, :], bank.tile[:, :], DEN_EPS, None, ALU.add))
            bank.free = [t]
            dve.wait(t)
            rd_t = dve.mark(nc.vector.reciprocal(u["rd"][:, :], u["rd"][:, :]))
            o_t = []
            for c in range(KC):
                bank = psum.take(pe)
                pe.wait(v_t)
                for j in range(TB):
                    m = nc.tensor.matmul(bank.tile[:, P * j:T], u["v"][:, j, P * c:P * c + P], u["s"][:, j, P * j:T],
                                         start=j == 0, stop=j == TB - 1, skip_group_check=True)
                t = pe.mark(m)
                dve.wait(t, rd_t)
                o_t.append(dve.mark(nc.vector.tensor_tensor(u["o"][:, c, :], bank.tile[:, :], u["rd"][:, :], ALU.mult)))
                bank.free = [o_t[-1]]
                yield
            yield from self.finish_tokens(b, psum, u["xb"], xb_t, u["xb"], [
                [(u["o"][:, k, P * i:P * i + P], wp[:, k, :]) for k in range(KC)] for i in range(TB)], o_t)
            u["done"] = [self.done_token]

        drive([batch(b) for b in range(NB)], 2)

    def finish_tokens(self, b, psum, xb, xb_t, r, pairs, after):
        nc, dve = self.nc, self.dve
        r_t = []
        for i in range(TB):
            bank = psum.take(self.pe)
            t = self.product(bank.tile[:, 0:C], pairs[i], after)
            dve.wait(t, xb_t[i])
            r_t.append(dve.mark(nc.vector.tensor_tensor(r[:, i, :], bank.tile[:, 0:C], xb[:, i, :], ALU.add)))
            bank.free = [r_t[-1]]
        yield
        slot, t = self.stats(lambda i: r[:, i, :], TB, r_t)
        yield
        done = self.normalize(slot, t, lambda i: self.X[:, TB * b + i, :], lambda i: r[:, i, :], TB)
        self.done_token = done[-1]


    def softmax_attention(self, scope, tag, D, scale, jobs, cut_room, y, raw_den):
        nc, pe, act, dve, pool, sp = self.nc, self.pe, self.act, self.dve, self.pool, self.sp
        sb = lambda n, s, d=F32: self.sb(scope, f"{tag}_" + n, s, d)
        STK = MAXROW + 2
        rows_ = lambda t: t.bitcast(F32)
        kst = Ring([Slot(sb(f"ks{i}", [STK, HG, max(cut_room)], F32R), self.arrivals(f"{tag}_ks{i}")) for i in range(6)])
        qst = Ring([Slot(sb(f"qs{i}", [STK, HG, T], F32R), self.arrivals(f"{tag}_qs{i}")) for i in range(3)])
        peaks = [self.arrivals(f"{tag}_peak{i}") for i in range(3)]
        for slot in kst.slots + qst.slots:
            slot.busy = False
        if 3 * D < MAXROW:
            for slot in qst.slots:
                slot.free = [dve.mark(nc.vector.memset(slot.tile[0:96].bitcast(F32), 0.0))]
        for n, slot in enumerate(kst.slots):
            eng, lane = ((nc.vector, dve), (nc.gpsimd, pool))[n % 2]
            if 3 * D < MAXROW:
                lane.wait(lane.mark(eng.memset(slot.tile[0:96].bitcast(F32), 0.0)))
            slot.free = [lane.mark(eng.memset(slot.tile[96:STK].bitcast(F32), -1.0))]
            lane.wait(slot.free)
        kparts = [Slot((sb(f"kh{i}", [P, w], F32R), sb(f"kl{i}", [P, w], F32R))) for i, w in enumerate(cut_room)]
        qh, ql = sb("qh", [P, T], F32R), sb("ql", [P, T], F32R)
        q_free = []
        probs = Ring([Slot(sb(f"p{i}", [P, T])) for i in range(8)])
        rec = Ring([Slot(sb(f"rec{i}", [P, T])) for i in range(1)])
        mp = Ring([Slot((sb(f"mp{i}", [P, HG, TB, 4]), sb(f"top{i}", [P, HG, TB]))) for i in range(2)])
        mm = Ring([Slot(sb(f"mm{i}", [P, TB, 2, HG], F32R)) for i in range(2)])
        mt = Ring([Slot(sb(f"mt{i}", [2 * HG, T], F32R)) for i in range(1)])
        a_banks = Ring(self.banks[0:3])
        b_banks = Ring(self.banks[3:5] if raw_den else self.banks[3:6])
        d_banks = Ring(self.banks[5:6])
        n_banks = Ring(self.banks[6:7])
        misc = Ring(self.banks[7:8])
        per_chunk = P // D // HG
        if any(j["mask"] == "causal" for j in jobs):
            neg_a, neg_b = sb("neg_a", [P, P], BF16), sb("neg_b", [P, P], BF16)
            for m in (neg_a, neg_b):
                t = pool.mark(nc.gpsimd.memset(m[:, :], 0.0))
            pool.wait(t)
            pool.mark(nc.gpsimd.affine_select(out=neg_a[:, :], in_=neg_a[:, :], compare_op=ALU.is_ge, fill=NEG,
                                              base=0, pattern=[[-1, P]], channel_multiplier=1))
            t = pool.mark(nc.gpsimd.affine_select(out=neg_b[:, :], in_=neg_b[:, :], compare_op=ALU.is_ge, fill=NEG,
                                                  base=0, pattern=[[1, P]], channel_multiplier=-1))
            pe.wait(t)
        if any(j["mask"] == "upper" for j in jobs):
            upper = sb("upper", [P, P])
            cut = Ring([Slot(sb(f"cut{i}", [P, P])) for i in range(8)])
            t = pool.mark(nc.gpsimd.memset(upper[:, :], 1.0))
            pool.wait(t)
            t = pool.mark(nc.gpsimd.affine_select(out=upper[:, :], in_=upper[:, :], compare_op=ALU.is_gt, fill=0.0,
                                                  base=0, pattern=[[-1, P]], channel_multiplier=1))
            pool.wait(t)
        if not raw_den:
            spread = sb("spread", [P, P])
            raw = Ring([Slot(sb(f"raw{i}", [P, T])) for i in range(2)])
            t = pool.mark(nc.gpsimd.memset(spread[:, :], 0.0))
            pool.wait(t)
            sv = spread[:, :].rearrange("p (g r) -> p g r", g=HG)
            t = pool.mark(nc.gpsimd.affine_select(out=sv, in_=sv, compare_op=ALU.not_equal, fill=1.0, base=-D,
                                                  pattern=[[-P // HG, HG], [0, P // HG]], channel_multiplier=1))
            pe.wait(t)
            t = dve.mark(nc.vector.memset(n_banks.slots[0].tile[:, :], 0.0))
            n_banks.slots[0].free = [t]

        def stack(job, ci):
            nonlocal q_free
            c = job["chunk"]
            k0, n = c["cuts"][ci]
            if ci == 0:
                job["n"] = stack.jobs
                stack.jobs += 1
                job["ks"], job["stacked"] = [], []
                if job["first"]:
                    bank = misc.take(pe)
                    t = self.product(bank.tile[:, :], c["q"], c["q_after"]())
                    act.wait(t, q_free)
                    dve.wait(q_free)
                    ht = act.mark(nc.scalar.activation(qh[:, :], bank.tile[:, :], ACT.Identity, bias=c["qb"]))
                    dve.wait(ht)
                    t = dve.mark(nc.vector.scalar_tensor_tensor(
                        out=ql[:, :], in0=bank.tile[:, :], scalar=c["qb"], in1=qh[:, :].bitcast(F32),
                        op0=ALU.add, op1=ALU.subtract))
                    bank.free = [t]
                    c["q_parts"] = [ht, t]
                    c["k_parts"] = {}
                    q_free = []
            src = slice(D * HG * job["sub"], D * HG * (job["sub"] + 1))
            parts = kparts[ci % len(kparts)]
            kh, kl = parts.tile
            if job["first"]:
                bank = misc.take(pe)
                t = self.product(bank.tile[:, 0:n], c["k"](k0, n), c["k_after"]())
                act.wait(t, parts.free)
                dve.wait(parts.free)
                ht = act.mark(nc.scalar.activation(kh[:, 0:n], bank.tile[:, 0:n], ACT.Identity, bias=c["kb"]))
                dve.wait(ht)
                t = dve.mark(nc.vector.scalar_tensor_tensor(
                    out=kl[:, 0:n], in0=bank.tile[:, 0:n], scalar=c["kb"], in1=kh[:, 0:n].bitcast(F32),
                    op0=ALU.add, op1=ALU.subtract))
                bank.free, parts.free = [t], []
                c["k_parts"][ci] = [ht, t]
            if ci == 0:
                qs = qst.take(sp)
                qs.busy = True
                sp.wait(c["q_parts"])
                for r, part in enumerate((qh, ql, qh)):
                    qs.landed.load(sp, qs.tile[D * r:D * r + D, :, :].bitcast(F32), part[src, :].bitcast(F32))
                job["qs"] = qs
                job["q_stacked"] = qs.landed.token()
                q_free = q_free + [job["q_stacked"]]
            ks = kst.take(sp)
            ks.busy = True
            sp.wait(c["k_parts"][ci])
            for r, part in enumerate((kh, kh, kl)):
                ks.landed.load(sp, ks.tile[D * r:D * r + D, :, 0:n].bitcast(F32), part[src, 0:n].bitcast(F32))
            job["ks"].append(ks)
            job["stacked"].append(ks.landed.token())
            parts.free = parts.free + [ks.landed.token()]
        stack.jobs = 0

        to_stack = [(job, ci) for job in jobs for ci in range(len(job["chunk"]["cuts"]))]

        def feed(most=1):
            while to_stack and most:
                job, ci = to_stack[0]
                free = not kst.slots[kst.at % len(kst.slots)].busy
                if ci == 0:
                    free = free and not qst.slots[qst.at % len(qst.slots)].busy
                if not free or not job["ready"]():
                    return
                to_stack.pop(0)
                most -= 1
                stack(job, ci)

        def peak(n, job):
            causal = job["mask"] == "causal"
            peaks_of = mp.take(dve)
            part, best = peaks_of.tile
            cuts = job["chunk"]["cuts"]
            for ci, (_, cw) in enumerate(cuts):
                while len(job.get("ks", ())) <= ci:
                    before = len(to_stack)
                    feed()
                    if len(to_stack) == before:
                        yield HELD
                qs, ks = job["qs"].tile, job["ks"][ci].tile
                pe.wait(job["q_stacked"], job["stacked"][ci])
                for g in range(HG):
                    for i in range(TB):
                        w = P * (i + 1) if causal else cw
                        bank = a_banks.take(pe)
                        m = nc.tensor.matmul(bank.tile[:, 0:w], qs[0:MAXROW, g, P * i:P * i + P],
                                             ks[0:MAXROW, g, 0:w], start=True, stop=not causal)
                        if causal:
                            m = nc.tensor.matmul(bank.tile[:, P * i:P * i + P], self.identb[:, :], neg_a[:, :],
                                                 start=False, stop=True)
                        t = pe.mark(m)
                        dve.wait(t)
                        t = dve.mark(nc.vector.tensor_reduce(part[:, g, i, ci:ci + 1], bank.tile[:, 0:w], AX.X, ALU.max))
                        bank.free = [t]
                        yield
            dve.wait(t)
            if len(cuts) > 1:
                t = dve.mark(nc.vector.tensor_reduce(best[:, :, :], part[:, :, :, 0:len(cuts)], AX.X, ALU.max))
                dve.wait(t)
            both = mm.take(dve)
            top = (best[:, :, :] if len(cuts) > 1 else part[:, :, :, 0]).rearrange("p g i -> p i g")
            t = dve.mark(nc.vector.tensor_copy(both.tile[:, :, 0, :], top))
            dve.wait(t)
            t = dve.mark(nc.vector.tensor_tensor(both.tile[:, :, 1, :], top, both.tile[:, :, 0, :].bitcast(F32), ALU.subtract))
            peaks_of.free = [t]
            bank = misc.take(pe)
            pe.wait(t)
            for i in range(TB):
                m = nc.tensor.transpose(bank.tile[0:2 * HG, P * i:P * i + P],
                                        both.tile[:, i].rearrange("p s g -> p (s g)").bitcast(F32), self.ident[:, :])
            t = pe.mark(m)
            both.free = [t]
            turned = mt.take(dve)
            dve.wait(t)
            t = dve.mark(nc.vector.tensor_copy(turned.tile[:, :], bank.tile[0:2 * HG, :]))
            bank.free = [t]
            sp.wait(t)
            peaks[n % 3].load(sp, qs[MAXROW:STK, :, :].bitcast(F32), turned.tile[:, :].bitcast(F32))
            turned.free = [peaks[n % 3].token()]
            job["peaked"] = peaks[n % 3].token()
            yield

        def weigh(n, job):
            qs, mask = job["qs"].tile, job["mask"]
            nkb = (job["nk"] + P - 1) // P
            num = n_banks.take(pe)
            den = d_banks.take(pe) if raw_den else None
            pe.wait(job["peaked"], job["values_after"]())
            behind = None

            def values(kb, kp, q0, tiles):
                first, last = kb == 0, kb == nkb - 1
                for g, (p, t) in enumerate(tiles):
                    pe.wait(t)
                    rows = slice(32 * g, 32 * g + job["vw"])
                    v = job["values"](kb, kp, g)
                    if mask == "upper":
                        p2, t2 = job["cut"][g]
                        if kb:
                            nc.tensor.matmul(num.tile[rows, 0:P * kb], v, p.tile[0:kp, 0:P * kb], start=False, stop=False,
                                             skip_group_check=True)
                        pe.wait(t2)
                        m = nc.tensor.matmul(num.tile[rows, P * kb:P * kb + P], v, p2.tile[:, :], start=first,
                                             stop=last, skip_group_check=True)
                    else:
                        m = nc.tensor.matmul(num.tile[rows, q0:T], v, p.tile[0:kp, q0:T], start=first, stop=last,
                                             skip_group_check=True)
                if raw_den:
                    for g, (p, t) in enumerate(tiles):
                        m = nc.tensor.matmul(den.tile[32 * g:32 * g + 32, q0:T], self.ones[0:kp, 0:32],
                                             p.tile[0:kp, q0:T], start=first, stop=last, skip_group_check=True)
                t = pe.mark(m)
                for g, (p, _) in enumerate(tiles):
                    p.free = [t]
                    if mask == "upper":
                        job["cut"][g][0].free = [t]
                return t

            cuts_of = job["chunk"]["cuts"]
            for kb in range(nkb):
                kp = min(P, job["nk"] - P * kb)
                ci = max(c for c, (k0, _) in enumerate(cuts_of) if k0 <= P * kb)
                ks, k0 = job["ks"][ci], P * kb - cuts_of[ci][0]
                last_of_cut = kb == nkb - 1 or ci + 1 < len(cuts_of) and P * (kb + 1) >= cuts_of[ci + 1][0]
                q0 = P * kb if mask == "causal" else 0
                tiles, cuts = [], []
                for g in range(HG):
                    bank = b_banks.take(pe)
                    m = nc.tensor.matmul(bank.tile[0:kp, q0:T], ks.tile[0:STK, g, k0:k0 + kp], qs[0:STK, g, q0:T],
                                         start=True, stop=mask != "causal")
                    if mask == "causal":
                        m = nc.tensor.matmul(bank.tile[:, q0:q0 + P], self.identb[:, :], neg_b[:, :], start=False, stop=True)
                    t = pe.mark(m)
                    if last_of_cut and g == HG - 1:
                        ks.free, ks.busy = [t], False
                        if kb == nkb - 1:
                            job["qs"].free, job["qs"].busy = [t], False
                    p = probs.take(act)
                    act.wait(t)
                    t = act.mark(nc.scalar.activation(p.tile[0:kp, q0:T], bank.tile[0:kp, q0:T], ACT.Exp, scale=scale))
                    bank.free = [t]
                    tiles.append((p, t))
                    if mask == "upper":
                        p2 = cut.take(pool)
                        pool.wait(t)
                        t = pool.mark(nc.gpsimd.tensor_tensor(p2.tile[:, :], p.tile[:, P * kb:P * kb + P], upper[:, :], ALU.mult))
                        cuts.append((p2, t))
                    if g == 1 and behind:
                        values(*behind)
                        behind = None
                    yield
                job["cut"] = cuts
                behind = (kb, kp, q0, tiles)
            t = values(*behind)
            job["values_done"](t)
            r = rec.take(dve)
            if raw_den:
                dve.wait(t)
                t = dve.mark(nc.vector.reciprocal(r.tile[:, :], den.tile[:, :]))
                den.free = [t]
                dve.wait(t, job["y_free"]())
                t = dve.mark(nc.vector.tensor_tensor(job["y"], num.tile[:, :], r.tile[:, :], ALU.mult))
                num.free, r.free = [t], [t]
            else:
                w = raw.take(dve)
                dve.wait(t)
                wt = dve.mark(nc.vector.tensor_copy(w.tile[:, :], num.tile[:, :]))
                num.free = [wt]
                bank = misc.take(pe)
                t = self.product(bank.tile[:, :], [(spread[:, :], w.tile[:, :])], [wt])
                dve.wait(t)
                t = dve.mark(nc.vector.reciprocal(r.tile[:, :], bank.tile[:, :]))
                bank.free = [t]
                dve.wait(t, job["y_free"]())
                if job["add"]:
                    t = dve.mark(nc.vector.tensor_tensor(w.tile[:, :], w.tile[:, :], r.tile[:, :], ALU.mult))
                    r.free = [t]
                    dve.wait(t)
                    t = dve.mark(nc.vector.tensor_tensor(job["y"], job["y"], w.tile[:, :], ALU.add))
                else:
                    t = dve.mark(nc.vector.tensor_tensor(job["y"], w.tile[:, :], r.tile[:, :], ALU.mult))
                    r.free = [t]
                w.free = [t]
            job["y_done"](t)
            yield

        def run(before, beside_job, between=lambda n: ()):
            def early(n):
                for g in beside_job(n):
                    yield from g

            def main(n):
                for _ in weigh(n, jobs[n]):
                    feed()
                    yield
            for g in before:
                for _ in g:
                    pass
            for _ in peak(0, jobs[0]):
                feed()
            for n, job in enumerate(jobs):
                nkb = (job["nk"] + P - 1) // P
                sides = [(early(n), 20, 0.0, EARLY_TO)]
                if n + 1 < len(jobs):
                    nxt = jobs[n + 1]
                    tiles = HG * TB * len(nxt["chunk"]["cuts"])
                    sides.append((peak(n + 1, nxt), tiles + 1, A_FROM, A_TO))
                for _ in between(n):
                    pass
                beside(main(n), HG * nkb, sides)

        return run, misc

    def mixed_attention(self, scope):
        nc, pe, act, dve, pool, sp = self.nc, self.pe, self.act, self.dve, self.pool, self.sp
        sb = lambda n, s, d=F32: self.sb(scope, "mx_" + n, s, d)
        D = C // H
        landed = self.arrivals("mx_weights")
        W = {n: self.weight(scope, landed, f"L0_xattn_{n}", [P, KC, C]) for n in ("Wq", "Wk", "Wv", "Wcq")}
        W.update({n: self.weight(scope, landed, f"L0_xattn_{n}", [P, 1, C]) for n in ("Wck", "Wcv")})
        wp = self.weight(scope, landed, "L0_xattn_Wp", [P, NG, C])
        row, rows_in = self.rows(scope, ["L0_xattn_bv", "L0_xattn_bcv", "L0_xattn_bp"], "mx")
        xts = [sb(f"xt{i}", [P, KC, T]) for i in range(2)]
        ctx = Slot(sb("ctx", [P, CTXE]), self.arrivals("mx_ctx"))
        VW = D + 2
        vs = [sb(f"vs{i}", [P, TB, H, VW]) for i in range(2)]
        vc = sb("vc", [P, CB, H, VW])
        y = sb("y", [P, NG, T])
        xb, r = sb("xb", [P, TB, C]), sb("r", [P, TB, C])
        for v in vs + [vc]:
            t = dve.mark(nc.vector.memset(v[:, :, :, D:D + 1], 1.0))
        dve.wait(rows_in)
        pool.wait(rows_in)
        pe.wait(landed.token(), t)
        st = dict(xt={}, vs={}, vc={}, ctx={}, y=[], y_free=[], vc_free=[], xt_free=[[], []], xb_free=[])

        cuts_self = [(0, T)]
        jobs = []
        for b in range(NB):
            for kind in ("self", "cross"):
                chunks = []
                for c in range(KC):
                    cs = slice(P * c, P * c + P)
                    xt = xts[b % 2]
                    if kind == "self":
                        chunks.append(dict(
                            q=[(W["Wq"][:, k, cs], xt[:, k, :]) for k in range(KC)], qb=self.col("L0_xattn_bq", c),
                            k=lambda k0, n, cs=cs, xt=xt: [(W["Wk"][:, k, cs], xt[:, k, k0:k0 + n]) for k in range(KC)],
                            kb=self.col("L0_xattn_bk", c), q_after=lambda b=b: st["xt"][b], k_after=lambda b=b: st["xt"][b],
                            cuts=cuts_self, nk2=T))
                    else:
                        chunks.append(dict(
                            q=[(W["Wcq"][:, k, cs], xt[:, k, :]) for k in range(KC)], qb=self.col("L0_xattn_bcq", c),
                            k=lambda k0, n, cs=cs: [(W["Wck"][:, 0, cs], ctx.tile[:, k0:k0 + n])],
                            kb=self.col("L0_xattn_bck", c), q_after=lambda b=b: st["xt"][b], k_after=lambda b=b: st["ctx"][b],
                            cuts=KEY_CUTS, nk2=CTXE))
                for g in range(NG):
                    per = NG // KC
                    job = dict(b=b, g=g, kind=kind, chunk=chunks[g // per], first=g % per == 0, sub=g % per,
                               mask="causal" if kind == "self" else None, nk=T if kind == "self" else CTX,
                               add=kind == "cross", y=y[:, g, :], vw=D + 1)
                    tile = vs[b % 2] if kind == "self" else vc
                    job["values"] = lambda kb, kp, h, tile=tile, g=g: tile[0:kp, kb, HG * g + h, 0:D + 1]
                    which = "vs" if kind == "self" else "vc"
                    job["values_after"] = lambda b=b, which=which: st[which][b]
                    job["values_done"] = (lambda t: None) if kind == "self" else (lambda t: st.update(vc_free=[t]))
                    job["y_free"] = lambda: st["y_free"] + st["y"]
                    job["y_done"] = lambda t: st.update(y=[t])
                    job["ready"] = lambda b=b, what="xt" if kind == "self" else "ctx": len(st[what].get(b, ())) > 0
                    jobs.append(job)
        run, misc = self.softmax_attention(scope, "mx", D, float(np.float32(1.0 / np.sqrt(D))), jobs, [T, 384, 384, 450], y, False)

        def own(b):
            xt, x = xts[b % 2], self.X[:, TB * b:TB * b + TB, :]
            st["xt"][b] = []
            dve.wait(st["vs"].get(b - 2, []))

            def evac(c, bank, t):
                dve.wait(t)
                t = dve.mark(nc.vector.tensor_copy(xt[:, c, :], bank[:, :]))
                st["xt"][b].append(t)
                return t
            dve.wait((pe.sem, pe.count) if pe.count else None)
            self.turn(misc, x, [None] * TB, evac)
            yield
            st["vs"][b] = []
            for i in range(TB):
                bank = misc.take(pe)
                t = self.product(bank.tile[:, 0:C], [(xt[:, k, P * i:P * i + P], W["Wv"][:, k, :]) for k in range(KC)],
                                 st["xt"][b])
                dve.wait(t)
                t = dve.mark(nc.vector.tensor_tensor(
                    vs[b % 2][:, i, :, 0:D], bank.tile[:, 0:C].rearrange("p (h d) -> p h d", h=H),
                    row["L0_xattn_bv"].rearrange("p (h d) -> p h d", h=H), ALU.add))
                bank.free = [t]
                st["vs"][b].append(t)
                yield

        def context(b):
            sp.wait(ctx.free)
            ctx.landed.load(sp, ctx.tile[:, :], self.a["ctx_t"][b])
            st["ctx"][b] = [ctx.landed.token()]
            st["vc"][b] = []
            yield
            dve.wait(st["vc_free"])
            for i in range(CB):
                kp = min(P, CTX - P * i)
                bank = misc.take(pe)
                t = self.product(bank.tile[0:kp, 0:C], [(ctx.tile[:, P * i:P * i + kp], W["Wcv"][:, 0, :])], st["ctx"][b])
                dve.wait(t)
                t = dve.mark(nc.vector.tensor_tensor(
                    vc[0:kp, i, :, 0:D], bank.tile[0:kp, 0:C].rearrange("p (h d) -> p h d", h=H),
                    row["L0_xattn_bcv"][0:kp].rearrange("p (h d) -> p h d", h=H), ALU.add))
                bank.free = [t]
                st["vc"][b].append(t)
                yield

        def finish(b):
            pool.wait(st["xb_free"])
            xb_t = [pool.mark(nc.gpsimd.tensor_tensor(xb[:, i, :], self.X[:, TB * b + i, :], row["L0_xattn_bp"], ALU.add))
                    for i in range(TB)]
            yield
            yield from self.finish_tokens(b, misc, xb, xb_t, r, [
                [(y[:, k, P * i:P * i + P], wp[:, k, :]) for k in range(NG)] for i in range(TB)], st["y"])
            st["y_free"] = [(pe.sem, pe.count)]
            st["xb_free"] = [self.done_token]

        def beside_job(n):
            job = jobs[n]
            b, out = job["b"], []
            if job["kind"] == "self" and job["g"] == 0 and b:
                out.append(finish(b - 1))
            if job["kind"] == "self" and job["g"] == 1:
                out.append(context(b))
            if job["kind"] == "cross" and job["g"] == NG - 2:
                ctx.free = [(pe.sem, pe.count)]
                if b + 1 < NB:
                    out.append(own(b + 1))
            return out
        run([own(0)], beside_job)
        for _ in finish(NB - 1):
            pass

    def experts(self, scope):
        nc, pe, act, dve, pool, sp = self.nc, self.pe, self.act, self.dve, self.pool, self.sp
        sb = lambda n, s, d=F32: self.sb(scope, "ex_" + n, s, d)
        landed = self.arrivals("ex_weights")
        wa = self.weight(scope, landed, "L0_ffn_attn_w", [P, KC, C])
        wn = self.weight(scope, landed, "L0_ffn_next_w", [P, KC, C])
        row, rows_in = self.rows(scope, ["L0_ffn_next_b"], "ex")
        FC = FF // P
        up = Ring([Slot(sb(f"w1_{i}", [P, KC, FF]), self.arrivals(f"ex_w1_{i}")) for i in range(3)])
        down = Ring([Slot(sb(f"w2_{i}", [P, FC, C]), self.arrivals(f"ex_w2_{i}")) for i in range(3)])
        w = {}

        def fetch(e):
            u, d = up.take(sp), down.take(sp)
            w[e] = (u, d, u.landed.load(sp, u.tile[:, :, :], self.a["L0_ffn_w1"][e]),
                    d.landed.load(sp, d.tile[:, :, :], self.a["L0_ffn_w2"][e]))
        for e in range(3):
            fetch(e)
        dve.wait(rows_in)
        pe.wait(landed.token())
        psum = Ring(self.banks)
        N = 2 * P
        sets = [dict(xh=sb(f"xh{i}", [P, 2, C]), xn=sb(f"xn{i}", [P, KC, N]), xt=sb(f"xt{i}", [P, KC, N]),
                     xa=sb(f"xa{i}", [P, KC, N]), h=sb(f"h{i}", [P, FC, N]), y=sb(f"y{i}", [P, KC, N]),
                     g=sb(f"g{i}", [P, 2, C]), done=[]) for i in range(3)]

        def expert(e):
            u = sets[e % 3]
            x = self.X[:, e:e + E + 1:E, :]
            for lane in (dve, act):
                lane.wait(u["done"])
            w1, w2, w1_t, w2_t = w[e]
            slot, t = self.stats(lambda i: x[:, i, :], 2, [None] * 2)
            yield
            xh_t = self.normalize(slot, t, lambda i: u["xh"][:, i, :], lambda i: x[:, i, :], 2)
            banks = []
            for src, after in ((x, []), (u["xh"], xh_t)):
                bank = psum.take(pe)
                pe.wait(after)
                for c in range(KC):
                    for i in range(2):
                        m = nc.tensor.transpose(bank.tile[:, N * c + P * i:N * c + P * i + P],
                                                src[:, i, P * c:P * c + P], self.ident[:, :])
                banks.append((bank, pe.mark(m)))
            bank, t = banks[0]
            act.wait(t)
            xt_t = act.mark(nc.scalar.activation(u["xt"].rearrange("p c n -> p (c n)"), bank.tile[:, :], ACT.Copy))
            bank.free = [xt_t]
            bank, t = banks[1]
            act.wait(t)
            for c in range(KC):
                xn_t = act.mark(nc.scalar.activation(u["xn"][:, c, :], bank.tile[:, N * c:N * c + N], ACT.Identity,
                                                     scale=self.col("L0_ffn_ln_g", c), bias=self.col("L0_ffn_ln_b", c)))
            bank.free = [xn_t]
            yield
            bank = psum.take(pe)
            for c in range(KC):
                t = self.product(bank.tile[:, N * c:N * c + N],
                                 [(wa[:, k, P * c:P * c + P], u["xn"][:, k, :]) for k in range(KC)], [xn_t])
            dve.wait(t, xt_t)
            for c in range(KC):
                xa_t = dve.mark(nc.vector.scalar_tensor_tensor(
                    out=u["xa"][:, c, :], in0=bank.tile[:, N * c:N * c + N], scalar=self.col("L0_ffn_attn_b", c),
                    in1=u["xt"][:, c, :], op0=ALU.add, op1=ALU.add))
            bank.free = [xa_t]
            yield
            pe.wait(w1_t)
            for f in range(0, FC, 2):
                bank = psum.take(pe)
                for j in range(2):
                    t = self.product(bank.tile[:, N * j:N * j + N],
                                     [(w1.tile[:, k, P * (f + j):P * (f + j) + P], u["xa"][:, k, :]) for k in range(KC)],
                                     [xa_t])
                act.wait(t)
                for j in range(2):
                    h_t = act.mark(nc.scalar.activation(u["h"][:, f + j, :], bank.tile[:, N * j:N * j + N], ACT.Gelu,
                                                        bias=self.col("L0_ffn_b1", FC * e + f + j)))
                bank.free = [h_t]
                yield
            w1.free = [t]
            pe.wait(w2_t)
            bank = psum.take(pe)
            for c in range(KC):
                t = self.product(bank.tile[:, N * c:N * c + N],
                                 [(w2.tile[:, f, P * c:P * c + P], u["h"][:, f, :]) for f in range(FC)], [h_t])
            w2.free = [t]
            if e + 3 < E:
                fetch(e + 3)
            dve.wait(t)
            for c in range(KC):
                y_t = dve.mark(nc.vector.tensor_scalar(u["y"][:, c, :], bank.tile[:, N * c:N * c + N],
                                                       self.col("L0_ffn_b2", KC * e + c), None, ALU.add))
            bank.free = [y_t]
            yield
            bank = psum.take(pe)
            for i in range(2):
                t = self.product(bank.tile[:, C * i:C * i + C],
                                 [(u["y"][:, k, P * i:P * i + P], wn[:, k, :]) for k in range(KC)], [y_t])
            dve.wait(t)
            for i in range(2):
                t = dve.mark(nc.vector.tensor_tensor(u["g"][:, i, :], bank.tile[:, C * i:C * i + C],
                                                     row["L0_ffn_next_b"], ALU.add))
            bank.free = [t]
            act.wait(t)
            t = act.mark(nc.scalar.activation(u["g"][:, :, :], u["g"][:, :, :], ACT.Gelu))
            dve.wait(t)
            t = dve.mark(nc.vector.tensor_tensor(u["g"][:, :, :], u["g"][:, :, :], x, ALU.add))
            yield
            slot, t = self.stats(lambda i: u["g"][:, i, :], 2, [t, t])
            yield
            u["done"] = self.normalize(slot, t, lambda i: x[:, i, :], lambda i: u["g"][:, i, :], 2)

        drive([expert(e) for e in range(E)], 3)

    def state_space(self, scope):
        nc, pe, act, dve, pool = self.nc, self.pe, self.act, self.dve, self.pool
        v = nc.vector
        sb = lambda n, s, d=F32: self.sb(scope, "ss_" + n, s, d)
        landed = self.arrivals("ss_weights")
        wi = self.weight(scope, landed, "ssm_in", [P, KC, 5 * SS])
        wo = self.weight(scope, landed, "ssm_out", [P, C])
        row, rows_in = self.rows(scope, ["L1_attn_out_proj_b"], "ss")
        EPS = 1e-4
        k = sb("k", [P, 8])
        expa, A, small, inv, bb, bc, am, ns = [k[:, i:i + 1] for i in range(8)]
        t = act.mark(nc.scalar.activation(expa, self.col("ssm_alog"), ACT.Exp))
        dve.wait(t)
        dve.mark(v.tensor_scalar(A, expa, -1.0, None, ALU.mult))
        dve.mark(v.tensor_tensor(bb, self.col("ssm_bb0"), self.col("ssm_bb1"), ALU.add))
        dve.mark(v.tensor_tensor(bc, self.col("ssm_bc0"), self.col("ssm_bc1"), ALU.add))
        t = dve.mark(v.tensor_scalar(small, expa, EPS, None, ALU.is_lt))
        dve.wait(t)
        dve.mark(v.tensor_tensor(am, A, small, ALU.subtract))
        t = dve.mark(v.tensor_scalar(ns, small, -1.0, 1.0, ALU.mult, ALU.add))
        dve.wait(t)
        t = dve.mark(v.reciprocal(inv, am))
        dve.wait(t)
        t = dve.mark(v.tensor_tensor(inv, inv, ns, ALU.mult))
        dve.wait(t)
        pool.wait(rows_in)
        pe.wait(landed.token())
        psum = Ring(self.banks[6:8])
        names = ("z", "l", "d", "ab", "sc", "b", "h", "c")
        sets = []
        for i in range(2):
            s = dict(xp=sb(f"xp{i}", [P, 2, KC, T + 2]), xc=sb(f"xc{i}", [P, 2, KC, T]), xb=sb(f"xb{i}", [P, 2, TB, C]))
            s.update({n: sb(f"{n}{i}", [P, T]) for n in names})
            pool.mark(nc.gpsimd.memset(s["xp"][:, :, :, 0:1], 0.0))
            pool.mark(nc.gpsimd.memset(s["xp"][:, :, :, T + 1:T + 2], 0.0))
            s["clear"] = pool.mark(nc.gpsimd.memset(s["xc"][:, :, :, T - 1:T], 0.0))
            sets.append(s)

        def pair(n):
            u = sets[n]
            dve.wait(u["clear"])
            xb_t = [[pool.mark(nc.gpsimd.tensor_tensor(u["xb"][:, s, i, :], self.X[:, TB * (2 * n + s) + i, :],
                                                       row["L1_attn_out_proj_b"], ALU.add)) for i in range(TB)]
                    for s in range(2)]
            banks = self.banks[3 * n:3 * n + 3]
            for s in range(2):
                b = 2 * n + s
                xp_t = []

                def evac(c, bank, t):
                    act.wait(t)
                    xp_t.append(act.mark(nc.scalar.activation(u["xp"][:, s, c, 1:T + 1], bank[:, :], ACT.Copy)))
                    return xp_t[-1]
                self.turn(psum, self.X[:, TB * b:TB * b + TB, :], [None] * TB, evac)
                yield
                for c in range(KC):
                    dst = u["xc"][:, s, c, 0:T - 1]
                    dve.wait(xp_t[c])
                    xc_t = dve.mark(v.tensor_scalar(dst, u["xp"][:, s, c, 0:T - 1], self.col("conv0", c),
                                                    self.col("L1_attn_conv_b", c), ALU.mult, ALU.add))
                    for j in range(1, 4):
                        dve.wait(xc_t)
                        xc_t = dve.mark(v.scalar_tensor_tensor(out=dst, in0=u["xp"][:, s, c, j:j + T - 1],
                                                               scalar=self.col(f"conv{j}", c), in1=dst,
                                                               op0=ALU.mult, op1=ALU.add))
                    yield
                pe.wait(u["clear"])
                half = slice(SS * s, SS * s + SS)
                for bank, parts in zip(banks, ((0,), (1, 2), (3, 4))):
                    prod_t = self.product(bank.tile[half, :], [(wi[:, kk, SS * p:SS * p + SS], u["xc"][:, s, kk, :])
                                                               for p in parts for kk in range(KC)], [xc_t])
                yield

            def step(ins):
                t = dve.mark(ins)
                dve.wait(t)
                return t
            bd, bB, bC = [x.tile[:, :] for x in banks]
            dve.wait(prod_t)
            z, l, d, ab, sc, bt, h, c = [u[x][:, :] for x in names]
            t = step(v.tensor_scalar(z, bd, self.col("ssm_bd"), None, ALU.add))
            banks[0].free = [t]
            t = step(v.scalar_tensor_tensor(out=l, in0=z, scalar=-1.0, in1=z, op0=ALU.mult, op1=ALU.max))
            act.wait(t)
            t = act.mark(nc.scalar.activation(l, l, ACT.Exp, scale=-1.0))
            act.wait(t)
            t = act.mark(nc.scalar.activation(l, l, ACT.Ln, bias=1.0))
            b_t = dve.mark(v.tensor_scalar(bt, bB, bb, 0.5, ALU.add, ALU.mult))
            banks[1].free = [b_t]
            c_t = dve.mark(v.tensor_scalar(c, bC, bc, 0.5, ALU.add, ALU.mult))
            banks[2].free = [c_t]
            yield
            dve.wait(t)
            step(v.scalar_tensor_tensor(out=d, in0=z, scalar=0.0, in1=l, op0=ALU.max, op1=ALU.add))
            t = step(v.tensor_scalar(d, d, A, None, ALU.mult))
            act.wait(t)
            ab_t = act.mark(nc.scalar.activation(ab, d, ACT.Exp))
            step(v.tensor_scalar(z, d, small, None, ALU.mult))
            step(v.tensor_scalar(l, z, 1.0 / 6.0, 0.5, ALU.mult, ALU.add))
            step(v.tensor_tensor(l, l, z, ALU.mult))
            step(v.tensor_scalar(l, l, 1.0, small, ALU.add, ALU.mult))
            yield
            dve.wait(ab_t)
            step(v.tensor_scalar(sc, ab, 1.0, inv, ALU.subtract, ALU.mult))
            step(v.tensor_tensor(sc, sc, l, ALU.add))
            step(v.tensor_tensor(sc, sc, bt, ALU.mult))
            step(v.tensor_tensor_scan(h, ab, sc, 0.0, ALU.mult, ALU.add))
            y_t = step(v.tensor_tensor(h, h, c, ALU.mult))
            yield
            for s in range(2):
                half = slice(SS * s, SS * s + SS)
                yield from self.finish_tokens(2 * n + s, psum, u["xb"][:, s], xb_t[s], u["xb"][:, s], [
                    [(u["h"][half, P * i:P * i + P], wo[half, :])] for i in range(TB)], [y_t])

        drive([pair(n) for n in range(NB // 2)], 2)

    def mlp(self, scope, tag, xo, more, then):
        nc, pe, act, dve, pool = self.nc, self.pe, self.act, self.dve, self.pool
        sb = lambda n, s, d=F32: self.sb(scope, f"m{tag}_" + n, s, d)
        landed = self.arrivals(f"m{tag}_weights")
        FC = FF // P
        w2 = self.weight(scope, landed, f"{tag}_li2_w", [P, KC, FF])
        w3 = self.weight(scope, landed, f"{tag}_li3_w", [P, FC, C])
        row, rows_in = self.rows(scope, [f"L1_xattn_{tag}_li3_b"], "m" + tag)
        pool.wait(rows_in)
        pe.wait(landed.token())
        psum = Ring(self.banks)
        sets = [dict(xh=sb(f"xh{i}", [P, TB, C]), xn=sb(f"xn{i}", [P, KC, T]), h=sb(f"h{i}", [P, FC, T]),
                     xb=sb(f"xb{i}", [P, TB, C]), done=[]) for i in range(2)]

        def batch(b):
            u = sets[b % 2]
            for lane in (dve, act, pool):
                lane.wait(u["done"])
            x = xo[:, TB * b:TB * b + TB, :]
            t = [pool.mark(nc.gpsimd.tensor_tensor(u["xb"][:, i, :], x[:, i, :], row[f"L1_xattn_{tag}_li3_b"], ALU.add))
                 for i in range(TB)]
            for src, src_t in more(b):
                pool.wait(t[-1], src_t)
                t = [pool.mark(nc.gpsimd.tensor_tensor(u["xb"][:, :, :], u["xb"][:, :, :], src, ALU.add))]
            xb_t = t[-1]
            slot, t = self.stats(lambda i: x[:, i, :], TB, [None] * TB)
            yield
            xh_t = self.normalize(slot, t, lambda i: u["xh"][:, i, :], lambda i: x[:, i, :], TB)
            xn_t = []

            def evac(c, bank, t):
                dve.wait(t)
                xn_t.append(dve.mark(nc.vector.tensor_scalar(u["xn"][:, c, :], bank[:, :], self.col(f"{tag}_ln3_g", c),
                                                             self.col(f"{tag}_ln3_b", c), ALU.mult, ALU.add)))
                return xn_t[-1]
            self.turn(psum, u["xh"], xh_t, evac)
            yield
            for f in range(FC):
                bank = psum.take(pe)
                t = self.product(bank.tile[:, :], [(w2[:, k, P * f:P * f + P], u["xn"][:, k, :]) for k in range(KC)], xn_t)
                act.wait(t)
                h_t = act.mark(nc.scalar.activation(u["h"][:, f, :], bank.tile[:, :], ACT.Gelu,
                                                    bias=self.col(f"{tag}_li2_b", f)))
                bank.free = [h_t]
                yield
            r_t = []
            for i in range(TB):
                bank = psum.take(pe)
                t = self.product(bank.tile[:, 0:C], [(u["h"][:, f, P * i:P * i + P], w3[:, f, :]) for f in range(FC)], [h_t])
                dve.wait(t, xb_t)
                r_t.append(dve.mark(nc.vector.tensor_tensor(u["xb"][:, i, :], bank.tile[:, 0:C], u["xb"][:, i, :], ALU.add)))
                bank.free = [r_t[-1]]
                yield
            yield from then(b, u["xb"], r_t)
            u["done"] = [self.done_token]

        drive([batch(b) for b in range(NB)], 2)

    def norm_to(self, dst):
        def then(b, r, r_t):
            slot, t = self.stats(lambda i: r[:, i, :], TB, r_t)
            yield
            done = self.normalize(slot, t, lambda i: dst[:, TB * b + i, :], lambda i: r[:, i, :], TB)
            self.done_token = done[-1]
        return then

    def block_attention(self, scope, tag, x1, xo, cross):
        nc, pe, act, dve, pool, sp = self.nc, self.pe, self.act, self.dve, self.pool, self.sp
        sb = lambda n, s, d=F32: self.sb(scope, f"{tag}_" + n, s, d)
        D, HD = 32, 32 * H
        YC = 1 if cross else KC
        landed = self.arrivals(f"{tag}_weights")
        wq = self.weight(scope, landed, f"{tag}_wq", [P, KC, HD])
        wk = self.weight(scope, landed, f"{tag}_wk", [P, YC, HD])
        wv = self.weight(scope, landed, f"{tag}_wv", [P, YC, HD])
        wo = self.weight(scope, landed, f"{tag}_li1_w", [P, NG, C])
        bias = f"L1_xattn_{tag}_li1_b"
        row, rows_in = self.rows(scope, [bias], tag)
        nkb = CB if cross else TB
        n_xn = 1 if cross else 2
        xn = [sb(f"xn{i}", [P, KC, T]) for i in range(n_xn)]
        yn = [sb("yn0", [P, 1, CTXE])] if cross else [sb(f"yn{i}", [P, KC, T]) for i in range(2)]
        vals = [sb(f"v{i}", [P, nkb, HD]) for i in range(1 if cross else 2)]
        y = sb("y", [P, NG, T])
        xb = sb("xb", [P, TB, C])
        if cross:
            raw = Ring([Slot(sb(f"ct{i}", [P, 4, CC]), self.arrivals(f"{tag}_ct{i}")) for i in range(2)])
        pool.wait(rows_in)
        pe.wait(landed.token())
        st = dict(xn={}, yn={}, v={}, y=[], y_free=[], v_free=[[], []], xb_free=[])
        jobs = []
        for b in range(NB):
            xt, yt, v = xn[b % len(xn)], yn[b % len(yn)], vals[b % len(vals)]
            for g in range(NG):
                cs = slice(P * g, P * g + P)
                chunk = dict(q=[(wq[:, k, cs], xt[:, k, :]) for k in range(KC)], qb=0.0, kb=0.0,
                             k=lambda k0, n, cs=cs, yt=yt: [(wk[:, k, cs], yt[:, k, k0:k0 + n]) for k in range(YC)],
                             q_after=lambda b=b: st["xn"][b], k_after=lambda b=b: st["yn"][b],
                             cuts=KEY_CUTS if cross else [(0, T)], nk2=CTXE if cross else T)
                jobs.append(dict(
                    b=b, g=g, chunk=chunk, first=True, sub=0, mask=None if cross else "upper", nk=CTX if cross else T,
                    add=False, y=y[:, g, :], vw=D, values=lambda kb, kp, h, v=v, g=g: v[0:kp, kb, P * g + D * h:P * g + D * h + D],
                    values_after=lambda b=b: st["v"][b], values_done=lambda t, b=b: st.update(v_last=t),
                    y_free=lambda: st["y_free"] + st["y"], y_done=lambda t: st.update(y=[t]),
                    ready=lambda b=b: b in st["xn"] and len(st["xn"][b]) == KC and len(st["yn"].get(b, ())) > 0))
        run, misc = self.softmax_attention(scope, tag, D, float(D) ** -0.5, jobs,
                                           [450, 450] if cross else [T, T], y, True)

        def own(b):
            x = x1[:, TB * b:TB * b + TB, :]
            dve.wait(st["xb_free"])
            slot, t = self.stats(lambda i: x[:, i, :], TB, [None] * TB)
            yield
            xh_t = self.normalize(slot, t, lambda i: xb[:, i, :], lambda i: x[:, i, :], TB)
            xt, yt = xn[b % len(xn)], yn[b % len(yn)]
            st["xn"][b] = []
            if not cross:
                st["yn"][b] = []
            dve.wait((pe.sem, pe.count))

            def evac(c, bank, t):
                dve.wait(t)
                t = dve.mark(nc.vector.tensor_scalar(xt[:, c, :], bank[:, :], self.col(f"{tag}_lnx_g", c),
                                                     self.col(f"{tag}_lnx_b", c), ALU.mult, ALU.add))
                st["xn"][b].append(t)
                if not cross:
                    t = dve.mark(nc.vector.tensor_scalar(yt[:, c, :], bank[:, :], self.col(f"{tag}_lny_g", c),
                                                         self.col(f"{tag}_lny_b", c), ALU.mult, ALU.add))
                    st["yn"][b].append(t)
                return t
            self.turn(misc, xb, xh_t, evac)
            st["xb_free"] = [(pe.sem, pe.count)]
            yield
            if not cross:
                yield from values(b)

        def context(b):
            st["yn"][b] = []
            tile = yn[0]
            cv = self.a["ctx"][b]
            dve.wait((pe.sem, pe.count))
            for i0 in range(0, CB, 4):
                n = min(4, CB - i0)
                kp = P if n == 4 else CTX - P * i0
                slot = raw.take(sp)
                t = slot.landed.load(sp, slot.tile[0:kp, 0:n, :],
                                     cv[P * i0:P * i0 + (P * n if n == 4 else kp)].rearrange("(t p) c -> p t c", p=kp))
                s, st_t = self.stats(lambda i: slot.tile[0:kp, i, :], n, [t] * n, kp)
                yield
                xh_t = self.normalize(s, st_t, lambda i: slot.tile[0:kp, i, :], lambda i: slot.tile[0:kp, i, :], n, kp)
                bank = misc.take(pe)
                for i in range(n):
                    pe.wait(xh_t[i])
                    m = nc.tensor.transpose(bank.tile[:, P * i:P * i + kp], slot.tile[0:kp, i, :], self.ident[0:kp, 0:kp])
                t = pe.mark(m)
                slot.free = [t]
                dve.wait(t)
                w = P * (n - 1) + kp
                t = dve.mark(nc.vector.tensor_scalar(tile[:, 0, P * i0:P * i0 + w], bank.tile[:, 0:w],
                                                     self.col(f"{tag}_lny_g"), self.col(f"{tag}_lny_b"), ALU.mult, ALU.add))
                bank.free = [t]
                yield
            dve.wait(t)
            st["yn"][b] = [dve.mark(nc.vector.tensor_copy(tile[:, 0, CTX:CTXE], tile[:, 0, CTX - 1:CTX]))]
            yield

        def values(b):
            v, yt = vals[b % len(vals)], yn[b % len(yn)]
            act.wait(st.get("v_last"))
            st["v"][b] = []
            for i in range(nkb):
                kp = min(P, (CTX if cross else T) - P * i)
                bank = misc.take(pe)
                t = self.product(bank.tile[0:kp, :], [(yt[:, k, P * i:P * i + kp], wv[:, k, :]) for k in range(YC)],
                                 st["yn"][b])
                act.wait(t)
                t = act.mark(nc.scalar.activation(v[0:kp, i, :], bank.tile[0:kp, :], ACT.Copy))
                bank.free = [t]
                st["v"][b].append(t)
                yield

        def finish(b):
            pool.wait(st["xb_free"])
            xb_t = [pool.mark(nc.gpsimd.tensor_tensor(xb[:, i, :], x1[:, TB * b + i, :], row[bias], ALU.add))
                    for i in range(TB)]
            yield
            for i in range(TB):
                bank = misc.take(pe)
                t = self.product(bank.tile[:, 0:C], [(y[:, k, P * i:P * i + P], wo[:, k, :]) for k in range(NG)], st["y"])
                dve.wait(t, xb_t[i])
                t = dve.mark(nc.vector.tensor_tensor(xo[:, TB * b + i, :], bank.tile[:, 0:C], xb[:, i, :], ALU.add))
                bank.free = [t]
                yield
            st["y_free"] = [(pe.sem, pe.count)]
            st["xb_free"] = [t]

        def beside_job(n):
            b, g = jobs[n]["b"], jobs[n]["g"]
            out = []
            if g == 0 and b:
                out.append(finish(b - 1))
            if g == (NG - 1 if cross else 1) and b + 1 < NB:
                out.append(own(b + 1))
                if cross:
                    out.append(context(b + 1))
            return out

        def between(n):
            if cross and jobs[n]["g"] == 0:
                yield from values(jobs[n]["b"])
        run([own(0)] + ([context(0)] if cross else []), beside_job, between)
        for _ in finish(NB - 1):
            pass

    def attention_blocks(self, scope):
        nc, dve, pool, sp = self.nc, self.dve, self.pool, self.sp
        x1 = self.sb(scope, "x1", [P, NT, C])
        aside = nc.dram_tensor("x_aside", (P, NT, C), F32, kind="Internal").ap()
        parked = self.arrivals("x_parked")
        parked.load(sp, aside, self.X[:, :, :])

        def affine(tag, dst, src, src_t, row):
            for i in range(TB):
                pool.wait(src_t[i])
                t = pool.mark(nc.gpsimd.tensor_tensor(dst(i), src(i), row[f"L1_xattn_{tag}_g"], ALU.mult))
                pool.wait(t)
                t = pool.mark(nc.gpsimd.tensor_tensor(dst(i), dst(i), row[f"L1_xattn_{tag}_b"], ALU.add))
            return t

        with ExitStack() as sc:
            row, rows_in = self.rows(sc, ["L1_xattn_ln1_g", "L1_xattn_ln1_b"], "n1")
            pool.wait(rows_in)
            for b in range(NB):
                at = lambda t, i, b=b: t[:, TB * b + i, :]
                slot, t = self.stats(lambda i: at(self.X, i), TB, [None] * TB)
                h_t = self.normalize(slot, t, lambda i: at(x1, i), lambda i: at(self.X, i), TB)
                affine("ln1", lambda i: at(x1, i), lambda i: at(x1, i), h_t, row)
        self.fence()
        with ExitStack() as sc:
            self.block_attention(sc, "a1", x1, self.X, False)
        self.fence()
        with ExitStack() as sc:
            row, rows_in = self.rows(sc, ["L1_xattn_ln2_g", "L1_xattn_ln2_b"], "n2")
            pool.wait(rows_in)

            def then(b, r, r_t):
                at = lambda i: x1[:, TB * b + i, :]
                slot, t = self.stats(lambda i: r[:, i, :], TB, r_t)
                yield
                h_t = self.normalize(slot, t, at, lambda i: r[:, i, :], TB)
                yield
                self.done_token = affine("ln2", at, at, h_t, row)
            self.mlp(sc, "a1", self.X, lambda b: [(x1[:, TB * b:TB * b + TB, :], None)], then)
        self.fence()
        with ExitStack() as sc:
            self.block_attention(sc, "a2", x1, self.X, True)
        self.fence()
        with ExitStack() as sc:
            back = [Slot(self.sb(sc, f"back{i}", [P, TB, C]), self.arrivals(f"back{i}")) for i in range(2)]
            tokens = {}

            def fetch(b):
                sp.wait(back[b % 2].free)
                tokens[b] = back[b % 2].landed.load(sp, back[b % 2].tile[:, :, :], aside[:, TB * b:TB * b + TB, :])
            fetch(0)
            fetch(1)

            def more(b):
                yield x1[:, TB * b:TB * b + TB, :], None
                yield back[b % 2].tile[:, :, :], tokens[b]

            def then(b, r, r_t):
                back[b % 2].free = [(pool.sem, pool.count)]
                if b + 2 < NB:
                    fetch(b + 2)
                yield from self.norm_to(self.X)(b, r, r_t)
            self.mlp(sc, "a2", self.X, more, then)

    def scaled_ffn(self, scope):
        nc, pe, act, dve, pool = self.nc, self.pe, self.act, self.dve, self.pool
        sb = lambda n, s, d=F32: self.sb(scope, "sf_" + n, s, d)
        FC = FF // P
        w = {}
        for n, shape in (("w1_w", [P, KC, FF]), ("w2_w", [P, KC, FF]), ("h1_w", [P, FC, FF]), ("h2_w", [P, FC, FF]),
                         ("w3_w", [P, FC, C])):
            landed = self.arrivals("sf_" + n)
            w[n] = (self.weight(scope, landed, n, shape), landed.token())
        row, rows_in = self.rows(scope, ["w3_s"], "sf")
        dve.wait(rows_in)
        psum = Ring(self.banks)
        sets = [dict(xt=sb(f"xt{i}", [P, KC, T]), h=sb(f"h{i}", [P, FC, T]), g=sb(f"g{i}", [P, FC, T]),
                     r=sb(f"r{i}", [P, TB, C]), done=[]) for i in range(2)]
        gates = Ring([Slot(sb(f"s{i}", [P, T])) for i in range(2)])

        def batch(b):
            u = sets[b % 2]
            for lane in (dve, act):
                lane.wait(u["done"])
            x = self.X[:, TB * b:TB * b + TB, :]
            xt_t = []

            def evac(c, bank, t):
                act.wait(t)
                xt_t.append(act.mark(nc.scalar.activation(u["xt"][:, c, :], bank[:, :], ACT.Copy)))
                return xt_t[-1]
            self.turn(psum, x, [None] * TB, evac)
            yield
            for f in range(FC):
                fs = slice(P * f, P * f + P)
                pe.wait(w["w1_w"][1])
                bank = psum.take(pe)
                t = self.product(bank.tile[:, :], [(w["w1_w"][0][:, k, fs], u["xt"][:, k, :]) for k in range(KC)], xt_t)
                s = gates.take(act)
                act.wait(t)
                st = act.mark(nc.scalar.activation(s.tile[:, :], bank.tile[:, :], ACT.Silu, scale=self.col("w1_s", f)))
                bank.free = [st]
                pe.wait(w["w2_w"][1])
                bank = psum.take(pe)
                t = self.product(bank.tile[:, :], [(w["w2_w"][0][:, k, fs], u["xt"][:, k, :]) for k in range(KC)], xt_t)
                dve.wait(t, st)
                t = dve.mark(nc.vector.scalar_tensor_tensor(out=u["h"][:, f, :], in0=bank.tile[:, :],
                                                            scalar=self.col("w2_s", f), in1=s.tile[:, :],
                                                            op0=ALU.mult, op1=ALU.mult))
                bank.free, s.free = [t], [t]
                yield
            for n, src, dst in (("h1", "h", "g"), ("h2", "g", "h")):
                pe.wait(w[n + "_w"][1])
                src_t = t
                for f in range(FC):
                    bank = psum.take(pe)
                    t = self.product(bank.tile[:, :], [(w[n + "_w"][0][:, k, P * f:P * f + P], u[src][:, k, :])
                                                       for k in range(FC)], [src_t])
                    act.wait(t)
                    t = act.mark(nc.scalar.activation(u[dst][:, f, :], bank.tile[:, :], ACT.Gelu,
                                                      scale=self.col(n + "_s", f)))
                    bank.free = [t]
                    yield
            pe.wait(w["w3_w"][1])
            r_t = []
            for i in range(TB):
                bank = psum.take(pe)
                mt = self.product(bank.tile[:, 0:C], [(u["h"][:, f, P * i:P * i + P], w["w3_w"][0][:, f, :])
                                                      for f in range(FC)], [t])
                dve.wait(mt)
                rt = dve.mark(nc.vector.tensor_tensor(u["r"][:, i, :], bank.tile[:, 0:C], row["w3_s"], ALU.mult))
                bank.free = [rt]
                dve.wait(rt)
                r_t.append(dve.mark(nc.vector.tensor_tensor(u["r"][:, i, :], u["r"][:, i, :], x[:, i, :], ALU.add)))
                yield
            slot, t = self.stats(lambda i: u["r"][:, i, :], TB, r_t)
            yield
            u["done"] = self.normalize(slot, t, lambda i: x[:, i, :], lambda i: u["r"][:, i, :], TB)

        drive([batch(b) for b in range(NB)], 2)


def build(nc, a, out, last_stage=99, first_stage=0):
    with ExitStack() as ctx:
        d = Decoder(nc, ctx, a, out, last_stage)
        d.constants()
        if first_stage:
            d.fence()
        stages = [d.linear_attention, d.mixed_attention, d.experts, d.state_space, d.attention_blocks, d.scaled_ffn]
        for i, stage in enumerate(stages[:last_stage]):
            if i < first_stage:
                continue
            with ExitStack() as scope:
                stage(scope)
            d.fence()
        stored = d.arrivals("stored")
        ov = out.rearrange("b (t p) c -> p (b t) c", p=P)
        stored.load(d.sp, ov, d.X[:, :, :])
        d.sp.wait(stored.token())


def by_channel(m, D):
    m = np.asarray(m)
    lead = m.shape[:-1]
    return m.reshape(*lead, NG, HG, D).swapaxes(-1, -2).reshape(*lead, -1)


def lay_out(inp):
    f = {k: np.asarray(v) for k, v in inp.items()}
    a = {"x": f["x"]}

    def w(name, m, rows=P):
        m = np.asarray(m)
        a[name] = np.ascontiguousarray(m.reshape(m.shape[0] // rows, rows, -1).transpose(1, 0, 2))
    w("L0_attn_w_qkv", f["L0_attn_w_qkv"])
    w("L0_attn_w_gate", f["L0_attn_w_gate"])
    w("L0_attn_w_proj", f["L0_attn_w_proj"])
    for n in ("Wv", "Wcv"):
        w("L0_xattn_" + n, f["L0_xattn_" + n])
    for n in ("Wq", "Wk", "Wcq", "Wck"):
        w("L0_xattn_" + n, by_channel(f["L0_xattn_" + n], C // H))
    wp = np.zeros((NG, HG, 32, C), np.float32)
    wp[:, :, :C // H] = f["L0_xattn_Wp"].reshape(NG, HG, C // H, C)
    w("L0_xattn_Wp", wp.reshape(NG * P, C))
    for n in ("bv", "bcv", "bp"):
        a["L0_xattn_" + n] = f["L0_xattn_" + n]
    a["ctx"] = f["ctx_512"]
    t = f["ctx_512"].transpose(0, 2, 1)
    a["ctx_t"] = np.concatenate([t, t[:, :, CTX - 1:]], axis=2)
    w("L0_ffn_attn_w", f["L0_ffn_attn_w"])
    w("L0_ffn_next_w", f["L0_ffn_next_w"])
    a["L0_ffn_next_b"] = f["L0_ffn_next_b"]
    for n in ("L0_ffn_w1", "L0_ffn_w2"):
        m = f[n]
        a[n] = np.ascontiguousarray(m.reshape(E, m.shape[1] // P, P, -1).transpose(0, 2, 1, 3))
    m = f["L1_attn_in_proj_w"]
    w("ssm_in", np.concatenate([m[:SS], m[SS:3 * SS:2], m[SS + 1:3 * SS:2], m[3 * SS::2], m[3 * SS + 1::2]]).T)
    a["ssm_out"] = np.concatenate([f["L1_attn_out_proj_w"].T] * 2)
    a["L1_attn_out_proj_b"] = f["L1_attn_out_proj_b"]
    for n in ("w1_w", "w2_w", "h1_w", "h2_w", "w3_w"):
        w(n, f["L1_ffn_" + n].T)
    a["w3_s"] = f["L1_ffn_w3_s"]
    for n in ("ln1_g", "ln1_b", "ln2_g", "ln2_b"):
        a["L1_xattn_" + n] = f["L1_xattn_" + n]
    for tag in ("a1", "a2"):
        for n in ("wq", "wk", "wv"):
            m = f[f"L1_xattn_{tag}_{n}"].transpose(1, 0, 2)
            m = m.reshape(m.shape[0], -1)
            w(f"{tag}_{n}", m if n == "wv" else by_channel(m, 32))
        a[f"L1_xattn_{tag}_li1_b"] = f[f"L1_xattn_{tag}_li1_b"]
        for n in ("li1_w", "li2_w", "li3_w"):
            w(f"{tag}_{n}", f[f"L1_xattn_{tag}_{n}"])
        a[f"L1_xattn_{tag}_li3_b"] = f[f"L1_xattn_{tag}_li3_b"]
    b = f["L0_attn_b_qkv"]
    a["L0_attn_bv"] = b[2 * C:]
    a["L0_attn_b_proj"] = f["L0_attn_b_proj"]
    v = {k[len("L1_xattn_"):] if k.startswith("L1_xattn_") else k[len("L1_ffn_"):] if k.startswith("L1_ffn_") else k: x
         for k, x in f.items()}
    for n in ("bq", "bk", "bcq", "bck"):
        v["L0_xattn_" + n] = by_channel(v["L0_xattn_" + n], C // H)
    v["L0_attn_bq"], v["L0_attn_bk"] = b[:C], b[C:2 * C]
    for j in range(4):
        v[f"conv{j}"] = f["L1_attn_conv_w"][:, 0, j]
    ib = f["L1_attn_in_proj_b"]
    two = lambda z: np.concatenate([z, z])
    v["ssm_bd"] = two(ib[:SS])
    v["ssm_bb0"], v["ssm_bb1"] = two(ib[SS:3 * SS:2]), two(ib[SS + 1:3 * SS:2])
    v["ssm_bc0"], v["ssm_bc1"] = two(ib[3 * SS::2]), two(ib[3 * SS + 1::2])
    v["ssm_alog"] = two(f["L1_attn_A_log"])
    a["cols"] = np.ascontiguousarray(np.concatenate([v[n].reshape(-1, P) for n, _ in COLS]).T)
    return a


def kernel(**inputs):
    import concourse.bacc as bacc
    from concourse.bass_utils import run_bass_kernel_spmd

    nc = bacc.Bacc("TRN2", target_bir_lowering=False, num_devices=1)
    arrays = {f"in_{k}": np.ascontiguousarray(v) for k, v in lay_out(inputs).items()}
    aps = {k[3:]: nc.dram_tensor(k, v.shape, mybir.dt.from_np(v.dtype), kind="ExternalInput").ap()
           for k, v in arrays.items()}
    out = nc.dram_tensor("out", (NB, T, C), F32, kind="ExternalOutput").ap()
    build(nc, aps, out)
    return run_bass_kernel_spmd(nc, [arrays], core_ids=[0]).results[0]["out"]
```

```python
from contextlib import ExitStack

import numpy as np

from concourse import mybir

F32 = mybir.dt.float32
F32R = mybir.dt.float32r
BF16 = mybir.dt.bfloat16
ALU = mybir.AluOpType
ACT = mybir.ActivationFunctionType
AX = mybir.AxisListType

P = 128
NB, T, C = 4, 512, 256
TB = T // P
NT = NB * TB
KC = C // P
H, HG = 16, 4
NG = H // HG
CTX, CC = 1601, 128
CTXE = CTX + 1
CB = (CTX + P - 1) // P
KEY_CUTS = [(0, 384), (384, 384), (768, 384), (1152, 450)]
E = 8
LN_EPS = 1e-5
DEN_EPS = 1e-6
MAXROW = 96
NEG = -1e30
LA_SETS, LA_APART = 3, 6
EX_SETS, EX_APART = 3, 5
MLP_SETS, MLP_APART = 2, 11
PAIRS_ON_DVE = (3,)
SS = 64
FF = 4 * C

COLS = [
    ("L0_attn_ln_g", 256), ("L0_attn_ln_b", 256), ("L0_attn_bq", 256), ("L0_attn_bk", 256),
    ("L0_attn_b_gate", 256),
    ("L0_xattn_bq", 256), ("L0_xattn_bk", 256), ("L0_xattn_bcq", 256), ("L0_xattn_bck", 256),
    ("L0_ffn_ln_g", 256), ("L0_ffn_ln_b", 256), ("L0_ffn_attn_b", 256),
    ("L0_ffn_b1", 8 * 1024), ("L0_ffn_b2", 8 * 256),
    ("conv0", 256), ("conv1", 256), ("conv2", 256), ("conv3", 256), ("L1_attn_conv_b", 256),
    ("ssm_bd", 128), ("ssm_bb0", 128), ("ssm_bb1", 128), ("ssm_bc0", 128), ("ssm_bc1", 128),
    ("ssm_alog", 128),
    ("a1_lnx_g", 256), ("a1_lnx_b", 256), ("a1_lny_g", 256), ("a1_lny_b", 256),
    ("a1_ln3_g", 256), ("a1_ln3_b", 256), ("a1_li2_b", 1024),
    ("a2_lnx_g", 256), ("a2_lnx_b", 256), ("a2_lny_g", 128), ("a2_lny_b", 128),
    ("a2_ln3_g", 256), ("a2_ln3_b", 256), ("a2_li2_b", 1024),
    ("w1_s", 1024), ("w2_s", 1024), ("h1_s", 1024), ("h2_s", 1024),
]
COL_AT = {}
for _name, _n in COLS:
    COL_AT[_name] = (sum(n // P for _, n in COLS[:len(COL_AT)]), _n // P)
NCOLS = sum(n // P for _, n in COLS)


class Lane:

    def __init__(self, nc, ctx, name, eng):
        self.eng, self.sem, self.count, self.seen = eng, ctx.enter_context(nc.semaphore(f"{name}_done")), 0, {}

    def mark(self, ins):
        ins.then_inc(self.sem, 1)
        self.count += 1
        return (self.sem, self.count)

    def wait(self, *tokens):
        for token in tokens:
            if token is None:
                continue
            if isinstance(token, list):
                self.wait(*token)
                continue
            sem, value = token
            if self.seen.get(sem.name, 0) < value:
                self.seen[sem.name] = value
                self.eng.wait_ge(sem, value)


class Arrivals:

    def __init__(self, nc, ctx, name):
        self.sem, self.count = ctx.enter_context(nc.semaphore(name)), 0

    def load(self, lane, out, in_):
        lane.eng.dma_start(out, in_).then_inc(self.sem, 16)
        self.count += 16
        return self.token()

    def token(self):
        return (self.sem, self.count)


class Slot:

    def __init__(self, tile, landed=None):
        self.tile, self.free, self.landed = tile, [], landed


class Ring:
    def __init__(self, slots):
        self.slots, self.at = slots, 0

    def take(self, lane=None):
        slot = self.slots[self.at % len(self.slots)]
        self.at += 1
        if lane is not None:
            lane.wait(slot.free)
        return slot


def drive(gens, width, apart=0):
    waiting, running, steps = list(gens), [], apart
    while waiting or running:
        while waiting and len(running) < width and (steps >= apart or not running):
            running.append(waiting.pop(0))
            steps = 0
        steps += 1
        for g in list(running):
            try:
                next(g)
            except StopIteration:
                running.remove(g)


HELD = "held"


class Decoder:
    def __init__(self, nc, ctx, a, out):
        self.nc, self.a, self.out = nc, a, out
        self.pe = Lane(nc, ctx, "pe", nc.tensor)
        self.act = Lane(nc, ctx, "act", nc.scalar)
        self.dve = Lane(nc, ctx, "dve", nc.vector)
        self.pool = Lane(nc, ctx, "pool", nc.gpsimd)
        self.sp = Lane(nc, ctx, "sp", nc.sync)
        self.ctx = ctx
        self.banks = [Slot(ctx.enter_context(nc.psum_tensor(f"bank{i}", [P, 512], F32))) for i in range(8)]
        self.dma_sems = []
        self.fences = 0

    def sb(self, scope, name, shape, dt=F32):
        return scope.enter_context(self.nc.sbuf_tensor(name, shape, dt))

    def arrivals(self, name):
        a = Arrivals(self.nc, self.ctx, name)
        self.dma_sems.append(a)
        return a

    def fence(self):
        lanes = [self.pe, self.act, self.dve, self.pool]
        last = [(l.sem, l.count) for l in lanes if l.count] + [d.token() for d in self.dma_sems if d.count]
        for lane in lanes + [self.sp]:
            lane.wait(last)
        for b in self.banks:
            b.free = []

    def col(self, name, i=0, rows=P):
        at, n = COL_AT[name]
        return self.cols[0:rows, at + i:at + i + 1]

    def constants(self):
        sb, pool, dve = self.sb, self.pool, self.dve
        ctx = self.ctx
        self.cols = sb(ctx, "cols", [P, NCOLS])
        self.X = sb(ctx, "X", [P, NT, C])
        self.ident = sb(ctx, "ident", [P, P])
        self.identb = sb(ctx, "identb", [P, P], BF16)
        self.ones = sb(ctx, "ones", [P, P])
        self.neghalf = sb(ctx, "neghalf", [P, 4])
        self.x_in = self.arrivals("x_landed")
        self.cols_in = self.arrivals("cols_landed")
        self.stored = self.arrivals("stored")
        xv = self.a["x"].rearrange("b (t p) c -> p (b t) c", p=P)
        for b in range(NB):
            self.x_in.load(self.sp, self.X[:, TB * b:TB * b + TB, :], xv[:, TB * b:TB * b + TB, :])
        self.cols_in.load(self.sp, self.cols[:, :], self.a["cols"])
        g = self.nc.gpsimd
        zero = pool.mark(g.memset(self.ident[:, :], 0.0))
        pool.mark(g.memset(self.ones[:, :], 1.0))
        pool.mark(g.memset(self.neghalf[:, :], -0.5))
        pool.wait(zero)
        t = pool.mark(g.affine_select(out=self.ident[:, :], in_=self.ident[:, :], compare_op=ALU.not_equal,
                                      fill=1.0, base=0, pattern=[[-1, P]], channel_multiplier=1))
        pool.wait(t)
        t = pool.mark(g.tensor_copy(self.identb[:, :], self.ident[:, :]))
        for lane in (self.pe, self.act, self.dve, self.pool):
            lane.wait(t, self.x_in.token(), self.cols_in.token())
        self.stat = Ring([Slot((sb(ctx, f"st{i}", [P, 4, 6]), sb(ctx, f"mv{i}", [P, 4, 2]),
                                sb(ctx, f"ve{i}", [P, 4]), sb(ctx, f"rs{i}", [P, 4]))) for i in range(4)])

    def stats(self, rows, n, after, np_=P):
        dve, pool, v = self.dve, self.pool, self.nc.vector
        slot = self.stat.take(dve)
        st, mv, ve, rs = slot.tile
        for i in range(n):
            dve.wait(after[i])
            t = dve.mark(v.bn_stats(st[0:np_, i, :], rows(i)))
        dve.wait(t)
        for i in range(n):
            t = dve.mark(v.bn_aggr(mv[0:np_, i, :], st[0:np_, i, :]))
        dve.wait(t)
        t = dve.mark(v.tensor_scalar(ve[0:np_, 0:n], mv[0:np_, 0:n, 1], LN_EPS, None, ALU.add))
        pool.wait(t)
        t = pool.mark(self.nc.gpsimd.tensor_tensor(rs[0:np_, 0:n], ve[0:np_, 0:n], self.neghalf[0:np_, 0:n], ALU.pow))
        return slot, t

    def normalize(self, slot, t, out, rows, n, np_=P):
        dve, v = self.dve, self.nc.vector
        _, mv, _, rs = slot.tile
        dve.wait(t)
        done = [dve.mark(v.tensor_scalar(out(i), rows(i), mv[0:np_, i, 0:1], rs[0:np_, i:i + 1],
                                         ALU.subtract, ALU.mult)) for i in range(n)]
        slot.free = [done[-1]]
        return done

    def turn(self, ring, src, after, evac):
        pe = self.pe
        for c in range(KC):
            bank = ring.take(pe)
            for i in range(TB):
                pe.wait(after[i])
                m = self.nc.tensor.transpose(bank.tile[:, P * i:P * i + P], src[:, i, P * c:P * c + P], self.ident[:, :])
            bank.free = [evac(c, bank.tile, pe.mark(m))]

    def product(self, bank, pairs, after):
        self.pe.wait(after)
        for k, (l, r) in enumerate(pairs):
            m = self.nc.tensor.matmul(bank, l, r, start=k == 0, stop=k == len(pairs) - 1)
        return self.pe.mark(m)

    def rows(self, scope, names, tag):
        tile = self.sb(scope, f"rows_{tag}", [P, len(names), C])
        landed = self.arrivals(f"rows_{tag}_landed")
        for i, n in enumerate(names):
            landed.load(self.sp, tile[:, i, :], self.a[n].rearrange("(o c) -> o c", o=1).to_broadcast([P, C]))
        return {n: tile[:, i, :] for i, n in enumerate(names)}, landed.token()

    def weight(self, scope, landed, name, shape):
        tile = self.sb(scope, f"w_{name}", shape)
        landed.load(self.sp, tile[:], self.a[name])
        return tile

    def linear_attention(self, scope):
        nc, pe, act, dve, pool = self.nc, self.pe, self.act, self.dve, self.pool
        sb = lambda n, s, d=F32: self.sb(scope, "la_" + n, s, d)
        landed = self.arrivals("la_weights")
        wqkv = self.weight(scope, landed, "L0_attn_w_qkv", [P, KC, 3 * C])
        wg = self.weight(scope, landed, "L0_attn_w_gate", [P, KC, C])
        wp = self.weight(scope, landed, "L0_attn_w_proj", [P, KC, C])
        row, rows_in = self.rows(scope, ["L0_attn_bv", "L0_attn_b_proj"], "la")
        mask = sb("mask", [P, P])
        nbg = sb("nbg", [P, KC])
        t = pool.mark(nc.gpsimd.memset(mask[:, :], 1.0))
        pool.wait(t)
        mask_t = pool.mark(nc.gpsimd.affine_select(out=mask[:, :], in_=mask[:, :], compare_op=ALU.is_ge, fill=0.0,
                                                   base=0, pattern=[[1, P]], channel_multiplier=-1))
        at, n = COL_AT["L0_attn_b_gate"]
        nbg_t = dve.mark(nc.vector.tensor_scalar(nbg[:, :], self.cols[:, at:at + n], -1.0, None, ALU.mult))
        act.wait(nbg_t)
        dve.wait(mask_t, rows_in)
        pool.wait(rows_in)
        pe.wait(landed.token())
        psum = Ring(self.banks)
        sets = [dict(xh=sb(f"xh{i}", [P, TB, C]), xn=sb(f"xn{i}", [P, KC, T]), q=sb(f"q{i}", [P, KC, T]),
                     k=sb(f"k{i}", [P, KC, T]), v=sb(f"v{i}", [P, TB, C]), s=sb(f"s{i}", [P, TB, T]),
                     rd=sb(f"rd{i}", [P, T]), o=sb(f"o{i}", [P, KC, T]), xb=sb(f"xb{i}", [P, TB, C]),
                     done=[]) for i in range(LA_SETS)]
        exps = Ring([Slot(sb(f"e{i}", [P, T])) for i in range(4)])
        relus = Ring([Slot(sb(f"r{i}", [P, T])) for i in range(4)])
        gates = Ring([Slot(sb(f"g{i}", [P, T])) for i in range(4)])

        def elu1(src, src_t, bias, dst):
            e, r = exps.take(act), relus.take(dve)
            act.wait(src_t)
            et = act.mark(nc.scalar.activation(e.tile[:, :], src, ACT.Exp, bias=bias))
            dve.wait(src_t, et)
            rt = dve.mark(nc.vector.tensor_scalar(r.tile[:, :], src, bias, 0.0, ALU.add, ALU.max))
            dve.wait(rt)
            t = dve.mark(nc.vector.scalar_tensor_tensor(out=dst, in0=e.tile[:, :], scalar=1.0, in1=r.tile[:, :],
                                                        op0=ALU.min, op1=ALU.add))
            e.free, r.free = [t], [t]
            return t

        def batch(b):
            u = sets[b % LA_SETS]
            x = self.X[:, TB * b:TB * b + TB, :]
            for lane in (dve, act, pool):
                lane.wait(u["done"])
            xb_t = [pool.mark(nc.gpsimd.tensor_tensor(u["xb"][:, i, :], x[:, i, :], row["L0_attn_b_proj"], ALU.add))
                    for i in range(TB)]
            slot, t = self.stats(lambda i: x[:, i, :], TB, [None] * TB)
            yield
            xh_t = self.normalize(slot, t, lambda i: u["xh"][:, i, :], lambda i: x[:, i, :], TB)
            xn_t = []

            def evac(c, bank, t):
                act.wait(t)
                xn_t.append(act.mark(nc.scalar.activation(u["xn"][:, c, :], bank[:, :], ACT.Identity,
                                                          scale=self.col("L0_attn_ln_g", c),
                                                          bias=self.col("L0_attn_ln_b", c))))
                return xn_t[-1]
            self.turn(psum, u["xh"], xh_t, evac)
            yield
            xn = lambda k: u["xn"][:, k, :]
            k_t = []
            for c in range(KC):
                cs = slice(P * c, P * c + P)
                bank = psum.take(pe)
                t = self.product(bank.tile[:, :], [(wg[:, k, cs], xn(k)) for k in range(KC)], xn_t)
                g = gates.take(act)
                act.wait(t)
                t = act.mark(nc.scalar.activation(g.tile[:, :], bank.tile[:, :], ACT.Exp, scale=-1.0,
                                                  bias=nbg[:, c:c + 1]))
                bank.free = [t]
                dve.wait(t)
                t = dve.mark(nc.vector.tensor_scalar(g.tile[:, :], g.tile[:, :], 1.0, None, ALU.add))
                dve.wait(t)
                gt = dve.mark(nc.vector.reciprocal(g.tile[:, :], g.tile[:, :]))
                bank = psum.take(pe)
                t = self.product(bank.tile[:, :], [(wqkv[:, k, C + P * c:C + P * c + P], xn(k)) for k in range(KC)], xn_t)
                dve.wait(t, gt)
                t = dve.mark(nc.vector.scalar_tensor_tensor(out=g.tile[:, :], in0=bank.tile[:, :],
                                                            scalar=self.col("L0_attn_bk", c), in1=g.tile[:, :],
                                                            op0=ALU.add, op1=ALU.mult))
                bank.free = [t]
                k_t.append(elu1(g.tile[:, :], t, 0.0, u["k"][:, c, :]))
                g.free = [k_t[-1]]
                yield
            q_t = []
            for c in range(KC):
                bank = psum.take(pe)
                t = self.product(bank.tile[:, :], [(wqkv[:, k, P * c:P * c + P], xn(k)) for k in range(KC)], xn_t)
                q_t.append(elu1(bank.tile[:, :], t, self.col("L0_attn_bq", c), u["q"][:, c, :]))
                bank.free = [q_t[-1]]
                yield
            v_t = []
            for i in range(TB):
                bank = psum.take(pe)
                t = self.product(bank.tile[:, 0:C], [(u["xn"][:, k, P * i:P * i + P], wqkv[:, k, 2 * C:3 * C])
                                                     for k in range(KC)], xn_t)
                dve.wait(t)
                v_t.append(dve.mark(nc.vector.tensor_tensor(u["v"][:, i, :], bank.tile[:, 0:C], row["L0_attn_bv"], ALU.add)))
                bank.free = [v_t[-1]]
            yield
            s_t = []
            for j in range(TB):
                w = T - P * j
                bank = psum.take(pe)
                t = self.product(bank.tile[:, 0:w], [(u["k"][:, k, P * j:P * j + P], u["q"][:, k, P * j:T])
                                                     for k in range(KC)], k_t + q_t)
                dve.wait(t)
                s_t.append(dve.mark(nc.vector.tensor_tensor(u["s"][:, j, P * j:P * j + P], bank.tile[:, 0:P],
                                                            mask[:, :], ALU.mult)))
                bank.free = [s_t[-1]]
                if w > P:
                    act.wait(s_t[-1])
                    s_t.append(act.mark(nc.scalar.activation(u["s"][:, j, P * j + P:T], bank.tile[:, P:w], ACT.Copy)))
                    bank.free = [s_t[-1], s_t[-2]]
            yield
            bank = psum.take(pe)
            pe.wait(s_t)
            for j in range(TB):
                m = nc.tensor.matmul(bank.tile[:, P * j:T], self.ones[:, :], u["s"][:, j, P * j:T], start=j == 0,
                                     stop=j == TB - 1, skip_group_check=True)
            t = pe.mark(m)
            dve.wait(t)
            t = dve.mark(nc.vector.tensor_scalar(u["rd"][:, :], bank.tile[:, :], DEN_EPS, None, ALU.add))
            bank.free = [t]
            dve.wait(t)
            rd_t = dve.mark(nc.vector.reciprocal(u["rd"][:, :], u["rd"][:, :]))
            o_t = []
            for c in range(KC):
                bank = psum.take(pe)
                pe.wait(v_t)
                for j in range(TB):
                    m = nc.tensor.matmul(bank.tile[:, P * j:T], u["v"][:, j, P * c:P * c + P], u["s"][:, j, P * j:T],
                                         start=j == 0, stop=j == TB - 1, skip_group_check=True)
                t = pe.mark(m)
                dve.wait(t, rd_t)
                o_t.append(dve.mark(nc.vector.tensor_tensor(u["o"][:, c, :], bank.tile[:, :], u["rd"][:, :], ALU.mult)))
                bank.free = [o_t[-1]]
                yield
            yield from self.finish_tokens(b, psum, u["xb"], xb_t, u["xb"], [
                [(u["o"][:, k, P * i:P * i + P], wp[:, k, :]) for k in range(KC)] for i in range(TB)], o_t)
            u["done"] = [self.done_token]

        drive([batch(b) for b in range(NB)], LA_SETS, LA_APART)

    def finish_tokens(self, b, psum, xb, xb_t, r, pairs, after):
        nc, dve = self.nc, self.dve
        r_t = []
        for i in range(TB):
            bank = psum.take(self.pe)
            t = self.product(bank.tile[:, 0:C], pairs[i], after)
            dve.wait(t, xb_t[i])
            r_t.append(dve.mark(nc.vector.tensor_tensor(r[:, i, :], bank.tile[:, 0:C], xb[:, i, :], ALU.add)))
            bank.free = [r_t[-1]]
        yield
        slot, t = self.stats(lambda i: r[:, i, :], TB, r_t)
        yield
        done = self.normalize(slot, t, lambda i: self.X[:, TB * b + i, :], lambda i: r[:, i, :], TB)
        self.done_token = done[-1]


    def softmax_attention(self, scope, tag, D, scale, jobs, cut_room, y, raw_den):
        nc, pe, act, dve, pool, sp = self.nc, self.pe, self.act, self.dve, self.pool, self.sp
        sb = lambda n, s, d=F32: self.sb(scope, f"{tag}_" + n, s, d)
        STK = MAXROW + 2
        n_kst = 6 if any(len(j["chunk"]["cuts"]) > 1 for j in jobs) else 3
        kst = Ring([Slot(sb(f"ks{i}", [STK, HG, max(cut_room)], F32R), self.arrivals(f"{tag}_ks{i}")) for i in range(n_kst)])
        qst = Ring([Slot(sb(f"qs{i}", [STK, HG, T], F32R), self.arrivals(f"{tag}_qs{i}")) for i in range(3)])
        peaks = [self.arrivals(f"{tag}_peak{i}") for i in range(3)]
        for slot in kst.slots + qst.slots:
            slot.busy = False
        if 3 * D < MAXROW:
            for slot in qst.slots:
                slot.free = [dve.mark(nc.vector.memset(slot.tile[0:96].bitcast(F32), 0.0))]
        for n, slot in enumerate(kst.slots):
            eng, lane = ((nc.vector, dve), (nc.gpsimd, pool))[n % 2]
            if 3 * D < MAXROW:
                lane.wait(lane.mark(eng.memset(slot.tile[0:96].bitcast(F32), 0.0)))
            slot.free = [lane.mark(eng.memset(slot.tile[96:STK].bitcast(F32), -1.0))]
            lane.wait(slot.free)
        kparts = [Slot((sb(f"kh{i}", [P, w], F32R), sb(f"kl{i}", [P, w], F32R))) for i, w in enumerate(cut_room)]
        qh, ql = sb("qh", [P, T], F32R), sb("ql", [P, T], F32R)
        q_free = []
        probs = Ring([Slot(sb(f"p{i}", [P, T])) for i in range(8)])
        for slot in probs.slots:
            slot.readers = []
        if raw_den:
            pairs = Ring([Slot(sb(f"pair{i}", [P, T])) for i in range(HG)])
        rec = Ring([Slot(sb(f"rec{i}", [P, T])) for i in range(1)])
        mp = Ring([Slot((sb(f"mp{i}", [P, HG, TB, 4]), sb(f"top{i}", [P, HG, TB]))) for i in range(2)])
        mm = Ring([Slot(sb(f"mm{i}", [P, TB, 2, HG], F32R)) for i in range(2)])
        mt = Ring([Slot(sb(f"mt{i}", [2 * HG, T], F32R)) for i in range(1)])
        a_banks = Ring(self.banks[0:3])
        b_banks = Ring(self.banks[3:5] if raw_den else self.banks[3:6])
        d_banks = Ring(self.banks[5:6])
        n_banks = Ring(self.banks[6:7])
        misc = Ring(self.banks[7:8])
        self.spare = Ring(misc.slots)
        wide = Ring(b_banks.slots + misc.slots)
        if any(j["mask"] == "causal" for j in jobs):
            neg_a, neg_b = sb("neg_a", [P, P], BF16), sb("neg_b", [P, P], BF16)
            for m in (neg_a, neg_b):
                t = pool.mark(nc.gpsimd.memset(m[:, :], 0.0))
            pool.wait(t)
            pool.mark(nc.gpsimd.affine_select(out=neg_a[:, :], in_=neg_a[:, :], compare_op=ALU.is_ge, fill=NEG,
                                              base=0, pattern=[[-1, P]], channel_multiplier=1))
            t = pool.mark(nc.gpsimd.affine_select(out=neg_b[:, :], in_=neg_b[:, :], compare_op=ALU.is_ge, fill=NEG,
                                                  base=0, pattern=[[1, P]], channel_multiplier=-1))
            pe.wait(t)
        if any(j["mask"] == "upper" for j in jobs):
            upper = sb("upper", [P, P])
            cut = Ring([Slot(sb(f"cut{i}", [P, P])) for i in range(8)])
            t = pool.mark(nc.gpsimd.memset(upper[:, :], 1.0))
            pool.wait(t)
            t = pool.mark(nc.gpsimd.affine_select(out=upper[:, :], in_=upper[:, :], compare_op=ALU.is_gt, fill=0.0,
                                                  base=0, pattern=[[-1, P]], channel_multiplier=1))
            pool.wait(t)
        if not raw_den:
            spread = sb("spread", [P, P])
            raw = Ring([Slot(sb(f"raw{i}", [P, T])) for i in range(2)])
            t = pool.mark(nc.gpsimd.memset(spread[:, :], 0.0))
            pool.wait(t)
            sv = spread[:, :].rearrange("p (g r) -> p g r", g=HG)
            t = pool.mark(nc.gpsimd.affine_select(out=sv, in_=sv, compare_op=ALU.not_equal, fill=1.0, base=-D,
                                                  pattern=[[-P // HG, HG], [0, P // HG]], channel_multiplier=1))
            pe.wait(t)
            t = dve.mark(nc.vector.memset(n_banks.slots[0].tile[:, :], 0.0))
            n_banks.slots[0].free = [t]

        def stack(job, ci):
            nonlocal q_free
            c = job["chunk"]
            src = slice(D * HG * job["sub"], D * HG * (job["sub"] + 1))
            if ci is None:
                job["n"] = stack.jobs
                stack.jobs += 1
                job["ks"], job["stacked"] = [], []
                if job["first"]:
                    bank = misc.take(pe)
                    t = self.product(bank.tile[:, :], c["q"], c["q_after"]())
                    act.wait(t, q_free)
                    dve.wait(q_free)
                    ht = act.mark(nc.scalar.activation(qh[:, :], bank.tile[:, :], ACT.Identity, bias=c["qb"]))
                    dve.wait(ht)
                    t = dve.mark(nc.vector.scalar_tensor_tensor(
                        out=ql[:, :], in0=bank.tile[:, :], scalar=c["qb"], in1=qh[:, :].bitcast(F32),
                        op0=ALU.add, op1=ALU.subtract))
                    bank.free = [t]
                    c["q_parts"] = [ht, t]
                    c["k_parts"] = {}
                    q_free = []
                qs = qst.take(sp)
                qs.busy = True
                sp.wait(c["q_parts"])
                for r, part in enumerate((qh, ql, qh)):
                    qs.landed.load(sp, qs.tile[D * r:D * r + D, :, :].bitcast(F32), part[src, :].bitcast(F32))
                job["qs"] = qs
                job["q_stacked"] = qs.landed.token()
                q_free = q_free + [job["q_stacked"]]
                return
            k0, n = c["cuts"][ci]
            parts = kparts[ci % len(kparts)]
            kh, kl = parts.tile
            if job["first"]:
                bank = misc.take(pe)
                t = self.product(bank.tile[:, 0:n], c["k"](k0, n), c["k_after"]())
                act.wait(t, parts.free)
                dve.wait(parts.free)
                ht = act.mark(nc.scalar.activation(kh[:, 0:n], bank.tile[:, 0:n], ACT.Identity, bias=c["kb"]))
                dve.wait(ht)
                t = dve.mark(nc.vector.scalar_tensor_tensor(
                    out=kl[:, 0:n], in0=bank.tile[:, 0:n], scalar=c["kb"], in1=kh[:, 0:n].bitcast(F32),
                    op0=ALU.add, op1=ALU.subtract))
                bank.free, parts.free = [t], []
                c["k_parts"][ci] = [ht, t]
            ks = kst.take(sp)
            ks.busy = True
            sp.wait(c["k_parts"][ci])
            for r, part in enumerate((kh, kh, kl)):
                ks.landed.load(sp, ks.tile[D * r:D * r + D, :, 0:n].bitcast(F32), part[src, 0:n].bitcast(F32))
            job["ks"].append(ks)
            job["stacked"].append(ks.landed.token())
            parts.free = parts.free + [ks.landed.token()]
        stack.jobs = 0

        to_stack = [(job, ci) for job in jobs for ci in [None] + list(range(len(job["chunk"]["cuts"])))]

        def feed(most=1):
            while to_stack and most:
                job, ci = to_stack[0]
                ring = qst if ci is None else kst
                if ring.slots[ring.at % len(ring.slots)].busy or not job["ready"]():
                    return
                to_stack.pop(0)
                most -= 1
                stack(job, ci)

        def peak(n, job):
            causal = job["mask"] == "causal"
            peaks_of = mp.take(dve)
            part, best = peaks_of.tile
            cuts = job["chunk"]["cuts"]
            for ci, (_, cw) in enumerate(cuts):
                while len(job.get("ks", ())) <= ci:
                    before = len(to_stack)
                    feed()
                    if len(to_stack) == before:
                        yield HELD
                qs, ks = job["qs"].tile, job["ks"][ci].tile
                pe.wait(job["q_stacked"], job["stacked"][ci])
                for g in range(HG):
                    for i in range(TB):
                        w = P * (i + 1) if causal else cw
                        bank = a_banks.take(pe)
                        m = nc.tensor.matmul(bank.tile[:, 0:w], qs[0:MAXROW, g, P * i:P * i + P],
                                             ks[0:MAXROW, g, 0:w], start=True, stop=not causal)
                        if causal:
                            m = nc.tensor.matmul(bank.tile[:, P * i:P * i + P], self.identb[:, :], neg_a[:, :],
                                                 start=False, stop=True)
                        t = pe.mark(m)
                        dve.wait(t)
                        t = dve.mark(nc.vector.tensor_reduce(part[:, g, i, ci:ci + 1], bank.tile[:, 0:w], AX.X, ALU.max))
                        bank.free = [t]
                        yield
            dve.wait(t)
            if len(cuts) > 1:
                t = dve.mark(nc.vector.tensor_reduce(best[:, :, :], part[:, :, :, 0:len(cuts)], AX.X, ALU.max))
                dve.wait(t)
            both = mm.take(dve)
            top = (best[:, :, :] if len(cuts) > 1 else part[:, :, :, 0]).rearrange("p g i -> p i g")
            t = dve.mark(nc.vector.tensor_copy(both.tile[:, :, 0, :], top))
            dve.wait(t)
            t = dve.mark(nc.vector.tensor_tensor(both.tile[:, :, 1, :], top, both.tile[:, :, 0, :].bitcast(F32), ALU.subtract))
            peaks_of.free = [t]
            yield
            yield
            bank = misc.take(pe)
            pe.wait(t)
            for i in range(TB):
                m = nc.tensor.transpose(bank.tile[0:2 * HG, P * i:P * i + P],
                                        both.tile[:, i].rearrange("p s g -> p (s g)").bitcast(F32), self.ident[:, :])
            t = pe.mark(m)
            both.free = [t]
            turned = mt.take(dve)
            dve.wait(t)
            t = dve.mark(nc.vector.tensor_copy(turned.tile[:, :], bank.tile[0:2 * HG, :]))
            bank.free = [t]
            sp.wait(t)
            peaks[n % 3].load(sp, qs[MAXROW:STK, :, :].bitcast(F32), turned.tile[:, :].bitcast(F32))
            turned.free = [peaks[n % 3].token()]
            job["peaked"] = peaks[n % 3].token()
            yield

        def weigh(n, job):
            qs, mask = job["qs"].tile, job["mask"]
            nkb = (job["nk"] + P - 1) // P
            num = n_banks.take(pe)
            den = d_banks.take(pe) if raw_den else None
            pe.wait(job["peaked"], job["values_after"]())
            behind = None
            paired = []

            def values(kb, kp, q0, tiles):
                first, last = kb == 0, kb == nkb - 1
                for g, (p, t) in enumerate(tiles):
                    pe.wait(t)
                    rows = slice(32 * g, 32 * g + job["vw"])
                    v = job["values"](kb, kp, g)
                    if mask == "upper":
                        p2, t2 = job["cut"][g]
                        if kb:
                            nc.tensor.matmul(num.tile[rows, 0:P * kb], v, p.tile[0:kp, 0:P * kb], start=False, stop=False,
                                             skip_group_check=True)
                        pe.wait(t2)
                        m = nc.tensor.matmul(num.tile[rows, P * kb:P * kb + P], v, p2.tile[:, :], start=first,
                                             stop=last, skip_group_check=True)
                    else:
                        m = nc.tensor.matmul(num.tile[rows, q0:T], v, p.tile[0:kp, q0:T], start=first, stop=last,
                                             skip_group_check=True)
                sums = []
                if raw_den:
                    if paired and paired[0][0] < kb:
                        sums.append((paired[0][0] == 1, P, [(s, t) for _, s, t in paired]))
                    if alone(kb):
                        sums.append((first, kp, tiles))
                for begin, rows_n, parts in sums:
                    for g, (p, t) in enumerate(parts):
                        pe.wait(t)
                        m = nc.tensor.matmul(den.tile[32 * g:32 * g + 32, :], self.ones[0:rows_n, 0:32],
                                             p.tile[0:rows_n, :], start=begin, stop=last and parts is tiles,
                                             skip_group_check=True)
                t = pe.mark(m)
                if sums and sums[0][2] is not tiles:
                    for _, s, _ in paired:
                        s.free = [t]
                    paired.clear()
                for g, (p, _) in enumerate(tiles):
                    p.free = [t] + p.readers
                    if mask == "upper":
                        job["cut"][g][0].free = [t]
                return t

            alone = lambda kb: mask == "upper" or kb | 1 >= nkb - 1
            cuts_of = job["chunk"]["cuts"]
            before = None
            for kb in range(nkb):
                kp = min(P, job["nk"] - P * kb)
                ci = max(c for c, (k0, _) in enumerate(cuts_of) if k0 <= P * kb)
                ks, k0 = job["ks"][ci], P * kb - cuts_of[ci][0]
                last_of_cut = kb == nkb - 1 or ci + 1 < len(cuts_of) and P * (kb + 1) >= cuts_of[ci + 1][0]
                q0 = P * kb if mask == "causal" else 0
                tiles, cuts = [], []
                for g in range(HG):
                    bank = b_banks.take(pe)
                    m = nc.tensor.matmul(bank.tile[0:kp, q0:T], ks.tile[0:STK, g, k0:k0 + kp], qs[0:STK, g, q0:T],
                                         start=True, stop=mask != "causal")
                    if mask == "causal":
                        m = nc.tensor.matmul(bank.tile[:, q0:q0 + P], self.identb[:, :], neg_b[:, :], start=False, stop=True)
                    t = pe.mark(m)
                    if last_of_cut and g == HG - 1:
                        ks.free, ks.busy = [t], False
                        if kb == nkb - 1:
                            job["qs"].free, job["qs"].busy = [t], False
                    p = probs.take(act)
                    p.readers = []
                    act.wait(t)
                    t = act.mark(nc.scalar.activation(p.tile[0:kp, q0:T], bank.tile[0:kp, q0:T], ACT.Exp, scale=scale))
                    bank.free = [t]
                    tiles.append((p, t))
                    if mask == "upper":
                        p2 = cut.take(pool)
                        pool.wait(t)
                        t = pool.mark(nc.gpsimd.tensor_tensor(p2.tile[:, :], p.tile[:, P * kb:P * kb + P], upper[:, :], ALU.mult))
                        cuts.append((p2, t))
                    if g == 1 and behind:
                        values(*behind)
                        behind = None
                    if raw_den and kb % 2 and not alone(kb) and g:
                        for h in ((0, 1) if g == 1 else (g,)):
                            lane, eng = (dve, nc.vector) if h in PAIRS_ON_DVE else (pool, nc.gpsimd)
                            s = pairs.take(lane)
                            (even, even_t), (odd, odd_t) = before[h], tiles[h]
                            lane.wait(even_t, odd_t)
                            st = lane.mark(eng.tensor_tensor(s.tile[:, :], even.tile[:, :], odd.tile[:, :], ALU.add))
                            paired.append((kb, s, st))
                            odd.readers.append(st)
                            even.free = even.free + [st]
                    yield
                job["cut"] = cuts
                behind, before = (kb, kp, q0, tiles), tiles
            t = values(*behind)
            job["values_done"](t)
            r = rec.take(dve)
            if raw_den:
                dve.wait(t)
                t = dve.mark(nc.vector.reciprocal(r.tile[:, :], den.tile[:, :]))
                den.free = [t]
                dve.wait(t, job["y_free"]())
                t = dve.mark(nc.vector.tensor_tensor(job["y"], num.tile[:, :], r.tile[:, :], ALU.mult))
                num.free, r.free = [t], [t]
            else:
                w = raw.take(dve)
                dve.wait(t)
                wt = dve.mark(nc.vector.tensor_copy(w.tile[:, :], num.tile[:, :]))
                num.free = [wt]
                bank = misc.take(pe)
                t = self.product(bank.tile[:, :], [(spread[:, :], w.tile[:, :])], [wt])
                dve.wait(t)
                t = dve.mark(nc.vector.reciprocal(r.tile[:, :], bank.tile[:, :]))
                bank.free = [t]
                dve.wait(t, job["y_free"]())
                if job["add"]:
                    t = dve.mark(nc.vector.tensor_tensor(w.tile[:, :], w.tile[:, :], r.tile[:, :], ALU.mult))
                    r.free = [t]
                    dve.wait(t)
                    t = dve.mark(nc.vector.tensor_tensor(job["y"], job["y"], w.tile[:, :], ALU.add))
                else:
                    t = dve.mark(nc.vector.tensor_tensor(job["y"], w.tile[:, :], r.tile[:, :], ALU.mult))
                    r.free = [t]
                w.free = [t]
            job["y_done"](t)
            yield

        def run(before, beside_job, between=lambda n: ()):
            def early(n):
                for g in beside_job(n):
                    yield from g

            def main(n):
                for _ in weigh(n, jobs[n]):
                    feed()
                    yield
            self.spare = wide
            for g in before:
                for _ in g:
                    pass
            self.spare = misc
            peaks_at = [0, 0]
            stream = [peak(n, job) for n, job in enumerate(jobs)]
            steps = [HG * TB * len(job["chunk"]["cuts"]) + 4 for job in jobs]

            def look_ahead(to):
                while peaks_at[0] < len(jobs) and peaks_at[0] + peaks_at[1] / steps[peaks_at[0]] < to:
                    try:
                        if next(stream[peaks_at[0]]) == HELD:
                            return
                        peaks_at[1] += 1
                    except StopIteration:
                        peaks_at[0], peaks_at[1] = peaks_at[0] + 1, 0

            look_ahead(1)
            assert peaks_at[0] == 1
            for n, job in enumerate(jobs):
                self.spare = wide
                for _ in between(n):
                    pass
                self.spare = misc
                side = early(n)
                n_main = HG * ((job["nk"] + P - 1) // P)
                each = 1 if n_main <= HG * TB else 2
                for done, _ in enumerate(main(n), 1):
                    if (done - 1) % each == 0:
                        next(side, None)
                    look_ahead(min(n + 1 + done / n_main, n + 2))
                for _ in side:
                    pass
                look_ahead(n + 2)
                assert peaks_at[0] >= min(n + 2, len(jobs))
            self.spare = wide

        return run, misc

    def mixed_attention(self, scope):
        nc, pe, act, dve, pool, sp = self.nc, self.pe, self.act, self.dve, self.pool, self.sp
        sb = lambda n, s, d=F32: self.sb(scope, "mx_" + n, s, d)
        D = C // H
        landed = self.arrivals("mx_weights")
        W = {n: self.weight(scope, landed, f"L0_xattn_{n}", [P, KC, C]) for n in ("Wq", "Wk", "Wv", "Wcq")}
        W.update({n: self.weight(scope, landed, f"L0_xattn_{n}", [P, 1, C]) for n in ("Wck", "Wcv")})
        wp = self.weight(scope, landed, "L0_xattn_Wp", [P, NG, C])
        row, rows_in = self.rows(scope, ["L0_xattn_bv", "L0_xattn_bcv", "L0_xattn_bp"], "mx")
        xts = [sb(f"xt{i}", [P, KC, T]) for i in range(2)]
        ctx = Slot(sb("ctx", [P, CTXE]), self.arrivals("mx_ctx"))
        VW = D + 2
        vs = [sb(f"vs{i}", [P, TB, H, VW]) for i in range(2)]
        vc = sb("vc", [P, CB, H, VW])
        y = sb("y", [P, NG, T])
        xb, r = sb("xb", [P, TB, C]), sb("r", [P, TB, C])
        for v in vs + [vc]:
            t = dve.mark(nc.vector.memset(v[:, :, :, D:D + 1], 1.0))
        dve.wait(rows_in)
        pool.wait(rows_in)
        pe.wait(landed.token(), t)
        st = dict(xt={}, vs={}, vc={}, ctx={}, y=[], y_free=[], vc_free=[], xt_free=[[], []], xb_free=[])

        cuts_self = [(0, T)]
        jobs = []
        for b in range(NB):
            for kind in ("self", "cross"):
                chunks = []
                for c in range(KC):
                    cs = slice(P * c, P * c + P)
                    xt = xts[b % 2]
                    if kind == "self":
                        chunks.append(dict(
                            q=[(W["Wq"][:, k, cs], xt[:, k, :]) for k in range(KC)], qb=self.col("L0_xattn_bq", c),
                            k=lambda k0, n, cs=cs, xt=xt: [(W["Wk"][:, k, cs], xt[:, k, k0:k0 + n]) for k in range(KC)],
                            kb=self.col("L0_xattn_bk", c), q_after=lambda b=b: st["xt"][b], k_after=lambda b=b: st["xt"][b],
                            cuts=cuts_self))
                    else:
                        chunks.append(dict(
                            q=[(W["Wcq"][:, k, cs], xt[:, k, :]) for k in range(KC)], qb=self.col("L0_xattn_bcq", c),
                            k=lambda k0, n, cs=cs: [(W["Wck"][:, 0, cs], ctx.tile[:, k0:k0 + n])],
                            kb=self.col("L0_xattn_bck", c), q_after=lambda b=b: st["xt"][b], k_after=lambda b=b: st["ctx"][b],
                            cuts=KEY_CUTS))
                for g in range(NG):
                    per = NG // KC
                    job = dict(b=b, g=g, kind=kind, chunk=chunks[g // per], first=g % per == 0, sub=g % per,
                               mask="causal" if kind == "self" else None, nk=T if kind == "self" else CTX,
                               add=kind == "cross", y=y[:, g, :], vw=D + 1)
                    tile = vs[b % 2] if kind == "self" else vc
                    job["values"] = lambda kb, kp, h, tile=tile, g=g: tile[0:kp, kb, HG * g + h, 0:D + 1]
                    which = "vs" if kind == "self" else "vc"
                    job["values_after"] = lambda b=b, which=which: st[which][b]
                    job["values_done"] = (lambda t: None) if kind == "self" else (lambda t: st.update(vc_free=[t]))
                    job["y_free"] = lambda: st["y_free"] + st["y"]
                    job["y_done"] = lambda t: st.update(y=[t])
                    job["ready"] = lambda b=b, what="xt" if kind == "self" else "ctx": len(st[what].get(b, ())) > 0
                    jobs.append(job)
        run, misc = self.softmax_attention(scope, "mx", D, float(np.float32(1.0 / np.sqrt(D))), jobs, [T, 384, 384, 450], y, False)

        def own(b):
            xt, x = xts[b % 2], self.X[:, TB * b:TB * b + TB, :]
            st["xt"][b] = []
            dve.wait(st["vs"].get(b - 2, []))

            def evac(c, bank, t):
                dve.wait(t)
                t = dve.mark(nc.vector.tensor_copy(xt[:, c, :], bank[:, :]))
                st["xt"][b].append(t)
                return t
            dve.wait((pe.sem, pe.count) if pe.count else None)
            self.turn(self.spare, x, [None] * TB, evac)
            yield
            st["vs"][b] = []
            for i in range(TB):
                bank = self.spare.take(pe)
                t = self.product(bank.tile[:, 0:C], [(xt[:, k, P * i:P * i + P], W["Wv"][:, k, :]) for k in range(KC)],
                                 st["xt"][b])
                dve.wait(t)
                t = dve.mark(nc.vector.tensor_tensor(
                    vs[b % 2][:, i, :, 0:D], bank.tile[:, 0:C].rearrange("p (h d) -> p h d", h=H),
                    row["L0_xattn_bv"].rearrange("p (h d) -> p h d", h=H), ALU.add))
                bank.free = [t]
                st["vs"][b].append(t)
                yield

        def context(b):
            sp.wait(ctx.free)
            ctx.landed.load(sp, ctx.tile[:, :], self.a["ctx_t"][b])
            st["ctx"][b] = [ctx.landed.token()]
            st["vc"][b] = []
            yield
            dve.wait(st["vc_free"])
            for i in range(CB):
                kp = min(P, CTX - P * i)
                bank = self.spare.take(pe)
                t = self.product(bank.tile[0:kp, 0:C], [(ctx.tile[:, P * i:P * i + kp], W["Wcv"][:, 0, :])], st["ctx"][b])
                dve.wait(t)
                t = dve.mark(nc.vector.tensor_tensor(
                    vc[0:kp, i, :, 0:D], bank.tile[0:kp, 0:C].rearrange("p (h d) -> p h d", h=H),
                    row["L0_xattn_bcv"][0:kp].rearrange("p (h d) -> p h d", h=H), ALU.add))
                bank.free = [t]
                st["vc"][b].append(t)
                yield

        def finish(b):
            pool.wait(st["xb_free"])
            xb_t = [pool.mark(nc.gpsimd.tensor_tensor(xb[:, i, :], self.X[:, TB * b + i, :], row["L0_xattn_bp"], ALU.add))
                    for i in range(TB)]
            yield
            yield from self.finish_tokens(b, self.spare, xb, xb_t, r, [
                [(y[:, k, P * i:P * i + P], wp[:, k, :]) for k in range(NG)] for i in range(TB)], st["y"])
            st["y_free"] = [(pe.sem, pe.count)]
            st["xb_free"] = [self.done_token]

        def beside_job(n):
            job = jobs[n]
            b, out = job["b"], []
            if job["kind"] == "self" and job["g"] == 0 and b:
                out.append(finish(b - 1))
            if job["kind"] == "self" and job["g"] == 1:
                out.append(context(b))
            if job["kind"] == "cross" and job["g"] == NG - 2:
                ctx.free = [(pe.sem, pe.count)]
                if b + 1 < NB:
                    out.append(own(b + 1))
            return out
        run([own(0)], beside_job)
        for _ in finish(NB - 1):
            pass

    def experts(self, scope):
        nc, pe, act, dve, pool, sp = self.nc, self.pe, self.act, self.dve, self.pool, self.sp
        sb = lambda n, s, d=F32: self.sb(scope, "ex_" + n, s, d)
        landed = self.arrivals("ex_weights")
        wa = self.weight(scope, landed, "L0_ffn_attn_w", [P, KC, C])
        wn = self.weight(scope, landed, "L0_ffn_next_w", [P, KC, C])
        row, rows_in = self.rows(scope, ["L0_ffn_next_b"], "ex")
        FC = FF // P
        up = Ring([Slot(sb(f"w1_{i}", [P, KC, FF]), self.arrivals(f"ex_w1_{i}")) for i in range(3)])
        down = Ring([Slot(sb(f"w2_{i}", [P, FC, C]), self.arrivals(f"ex_w2_{i}")) for i in range(3)])
        w = {}

        def fetch(e):
            u, d = up.take(sp), down.take(sp)
            w[e] = (u, d, u.landed.load(sp, u.tile[:, :, :], self.a["L0_ffn_w1"][e]),
                    d.landed.load(sp, d.tile[:, :, :], self.a["L0_ffn_w2"][e]))
        for e in range(3):
            fetch(e)
        dve.wait(rows_in)
        pe.wait(landed.token())
        psum = Ring(self.banks)
        N = 2 * P
        sets = [dict(xh=sb(f"xh{i}", [P, 2, C]), xn=sb(f"xn{i}", [P, KC, N]), xt=sb(f"xt{i}", [P, KC, N]),
                     xa=sb(f"xa{i}", [P, KC, N]), h=sb(f"h{i}", [P, FC, N]), y=sb(f"y{i}", [P, KC, N]),
                     g=sb(f"g{i}", [P, 2, C]), done=[]) for i in range(3)]

        def expert(e):
            u = sets[e % 3]
            x = self.X[:, e:e + E + 1:E, :]
            for lane in (dve, act):
                lane.wait(u["done"])
            w1, w2, w1_t, w2_t = w[e]
            slot, t = self.stats(lambda i: x[:, i, :], 2, [None] * 2)
            yield
            xh_t = self.normalize(slot, t, lambda i: u["xh"][:, i, :], lambda i: x[:, i, :], 2)
            banks = []
            for src, after in ((x, []), (u["xh"], xh_t)):
                bank = psum.take(pe)
                pe.wait(after)
                for c in range(KC):
                    for i in range(2):
                        m = nc.tensor.transpose(bank.tile[:, N * c + P * i:N * c + P * i + P],
                                                src[:, i, P * c:P * c + P], self.ident[:, :])
                banks.append((bank, pe.mark(m)))
            bank, t = banks[0]
            act.wait(t)
            xt_t = act.mark(nc.scalar.activation(u["xt"].rearrange("p c n -> p (c n)"), bank.tile[:, :], ACT.Copy))
            bank.free = [xt_t]
            bank, t = banks[1]
            act.wait(t)
            for c in range(KC):
                xn_t = act.mark(nc.scalar.activation(u["xn"][:, c, :], bank.tile[:, N * c:N * c + N], ACT.Identity,
                                                     scale=self.col("L0_ffn_ln_g", c), bias=self.col("L0_ffn_ln_b", c)))
            bank.free = [xn_t]
            yield
            bank = psum.take(pe)
            for c in range(KC):
                t = self.product(bank.tile[:, N * c:N * c + N],
                                 [(wa[:, k, P * c:P * c + P], u["xn"][:, k, :]) for k in range(KC)], [xn_t])
            dve.wait(t, xt_t)
            for c in range(KC):
                xa_t = dve.mark(nc.vector.scalar_tensor_tensor(
                    out=u["xa"][:, c, :], in0=bank.tile[:, N * c:N * c + N], scalar=self.col("L0_ffn_attn_b", c),
                    in1=u["xt"][:, c, :], op0=ALU.add, op1=ALU.add))
            bank.free = [xa_t]
            yield
            pe.wait(w1_t)
            for f in range(0, FC, 2):
                bank = psum.take(pe)
                for j in range(2):
                    t = self.product(bank.tile[:, N * j:N * j + N],
                                     [(w1.tile[:, k, P * (f + j):P * (f + j) + P], u["xa"][:, k, :]) for k in range(KC)],
                                     [xa_t])
                act.wait(t)
                for j in range(2):
                    h_t = act.mark(nc.scalar.activation(u["h"][:, f + j, :], bank.tile[:, N * j:N * j + N], ACT.Gelu,
                                                        bias=self.col("L0_ffn_b1", FC * e + f + j)))
                bank.free = [h_t]
                yield
            w1.free = [t]
            pe.wait(w2_t)
            bank = psum.take(pe)
            for c in range(KC):
                t = self.product(bank.tile[:, N * c:N * c + N],
                                 [(w2.tile[:, f, P * c:P * c + P], u["h"][:, f, :]) for f in range(FC)], [h_t])
            w2.free = [t]
            if e + 3 < E:
                fetch(e + 3)
            dve.wait(t)
            for c in range(KC):
                y_t = dve.mark(nc.vector.tensor_scalar(u["y"][:, c, :], bank.tile[:, N * c:N * c + N],
                                                       self.col("L0_ffn_b2", KC * e + c), None, ALU.add))
            bank.free = [y_t]
            yield
            bank = psum.take(pe)
            for i in range(2):
                t = self.product(bank.tile[:, C * i:C * i + C],
                                 [(u["y"][:, k, P * i:P * i + P], wn[:, k, :]) for k in range(KC)], [y_t])
            dve.wait(t)
            for i in range(2):
                t = dve.mark(nc.vector.tensor_tensor(u["g"][:, i, :], bank.tile[:, C * i:C * i + C],
                                                     row["L0_ffn_next_b"], ALU.add))
            bank.free = [t]
            act.wait(t)
            t = act.mark(nc.scalar.activation(u["g"][:, :, :], u["g"][:, :, :], ACT.Gelu))
            dve.wait(t)
            t = dve.mark(nc.vector.tensor_tensor(u["g"][:, :, :], u["g"][:, :, :], x, ALU.add))
            yield
            slot, t = self.stats(lambda i: u["g"][:, i, :], 2, [t, t])
            yield
            u["done"] = self.normalize(slot, t, lambda i: x[:, i, :], lambda i: u["g"][:, i, :], 2)

        drive([expert(e) for e in range(E)], EX_SETS, EX_APART)

    def state_space(self, scope):
        nc, pe, act, dve, pool = self.nc, self.pe, self.act, self.dve, self.pool
        v = nc.vector
        sb = lambda n, s, d=F32: self.sb(scope, "ss_" + n, s, d)
        landed = self.arrivals("ss_weights")
        wi = self.weight(scope, landed, "ssm_in", [P, KC, 5 * SS])
        wo = self.weight(scope, landed, "ssm_out", [P, C])
        row, rows_in = self.rows(scope, ["L1_attn_out_proj_b"], "ss")
        EPS = 1e-4
        k = sb("k", [P, 8])
        expa, A, small, inv, bb, bc, am, ns = [k[:, i:i + 1] for i in range(8)]
        t = act.mark(nc.scalar.activation(expa, self.col("ssm_alog"), ACT.Exp))
        dve.wait(t)
        dve.mark(v.tensor_scalar(A, expa, -1.0, None, ALU.mult))
        dve.mark(v.tensor_tensor(bb, self.col("ssm_bb0"), self.col("ssm_bb1"), ALU.add))
        dve.mark(v.tensor_tensor(bc, self.col("ssm_bc0"), self.col("ssm_bc1"), ALU.add))
        t = dve.mark(v.tensor_scalar(small, expa, EPS, None, ALU.is_lt))
        dve.wait(t)
        dve.mark(v.tensor_tensor(am, A, small, ALU.subtract))
        t = dve.mark(v.tensor_scalar(ns, small, -1.0, 1.0, ALU.mult, ALU.add))
        dve.wait(t)
        t = dve.mark(v.reciprocal(inv, am))
        dve.wait(t)
        t = dve.mark(v.tensor_tensor(inv, inv, ns, ALU.mult))
        dve.wait(t)
        pool.wait(rows_in)
        pe.wait(landed.token())
        psum = Ring(self.banks[6:8])
        names = ("z", "l", "d", "ab", "sc", "b", "h", "c")
        sets = []
        for i in range(2):
            s = dict(xp=sb(f"xp{i}", [P, 2, KC, T + 2]), xc=sb(f"xc{i}", [P, 2, KC, T]), xb=sb(f"xb{i}", [P, 2, TB, C]))
            s.update({n: sb(f"{n}{i}", [P, T]) for n in names})
            pool.mark(nc.gpsimd.memset(s["xp"][:, :, :, 0:1], 0.0))
            pool.mark(nc.gpsimd.memset(s["xp"][:, :, :, T + 1:T + 2], 0.0))
            s["clear"] = pool.mark(nc.gpsimd.memset(s["xc"][:, :, :, T - 1:T], 0.0))
            sets.append(s)

        def pair(n):
            u = sets[n]
            dve.wait(u["clear"])
            xb_t = [[pool.mark(nc.gpsimd.tensor_tensor(u["xb"][:, s, i, :], self.X[:, TB * (2 * n + s) + i, :],
                                                       row["L1_attn_out_proj_b"], ALU.add)) for i in range(TB)]
                    for s in range(2)]
            banks = self.banks[3 * n:3 * n + 3]
            for s in range(2):
                b = 2 * n + s
                xp_t = []

                def evac(c, bank, t):
                    act.wait(t)
                    xp_t.append(act.mark(nc.scalar.activation(u["xp"][:, s, c, 1:T + 1], bank[:, :], ACT.Copy)))
                    return xp_t[-1]
                self.turn(psum, self.X[:, TB * b:TB * b + TB, :], [None] * TB, evac)
                yield
                for c in range(KC):
                    dst = u["xc"][:, s, c, 0:T - 1]
                    dve.wait(xp_t[c])
                    xc_t = dve.mark(v.tensor_scalar(dst, u["xp"][:, s, c, 0:T - 1], self.col("conv0", c),
                                                    self.col("L1_attn_conv_b", c), ALU.mult, ALU.add))
                    for j in range(1, 4):
                        dve.wait(xc_t)
                        xc_t = dve.mark(v.scalar_tensor_tensor(out=dst, in0=u["xp"][:, s, c, j:j + T - 1],
                                                               scalar=self.col(f"conv{j}", c), in1=dst,
                                                               op0=ALU.mult, op1=ALU.add))
                    yield
                pe.wait(u["clear"])
                half = slice(SS * s, SS * s + SS)
                for bank, parts in zip(banks, ((0,), (1, 2), (3, 4))):
                    prod_t = self.product(bank.tile[half, :], [(wi[:, kk, SS * p:SS * p + SS], u["xc"][:, s, kk, :])
                                                               for p in parts for kk in range(KC)], [xc_t])
                yield

            def step(ins):
                t = dve.mark(ins)
                dve.wait(t)
                return t
            bd, bB, bC = [x.tile[:, :] for x in banks]
            dve.wait(prod_t)
            z, l, d, ab, sc, bt, h, c = [u[x][:, :] for x in names]
            t = step(v.tensor_scalar(z, bd, self.col("ssm_bd"), None, ALU.add))
            banks[0].free = [t]
            t = step(v.scalar_tensor_tensor(out=l, in0=z, scalar=-1.0, in1=z, op0=ALU.mult, op1=ALU.max))
            act.wait(t)
            t = act.mark(nc.scalar.activation(l, l, ACT.Exp, scale=-1.0))
            act.wait(t)
            t = act.mark(nc.scalar.activation(l, l, ACT.Ln, bias=1.0))
            b_t = dve.mark(v.tensor_scalar(bt, bB, bb, 0.5, ALU.add, ALU.mult))
            banks[1].free = [b_t]
            c_t = dve.mark(v.tensor_scalar(c, bC, bc, 0.5, ALU.add, ALU.mult))
            banks[2].free = [c_t]
            yield
            dve.wait(t)
            step(v.scalar_tensor_tensor(out=d, in0=z, scalar=0.0, in1=l, op0=ALU.max, op1=ALU.add))
            t = step(v.tensor_scalar(d, d, A, None, ALU.mult))
            act.wait(t)
            ab_t = act.mark(nc.scalar.activation(ab, d, ACT.Exp))
            step(v.tensor_scalar(z, d, small, None, ALU.mult))
            step(v.tensor_scalar(l, z, 1.0 / 6.0, 0.5, ALU.mult, ALU.add))
            step(v.tensor_tensor(l, l, z, ALU.mult))
            step(v.tensor_scalar(l, l, 1.0, small, ALU.add, ALU.mult))
            yield
            dve.wait(ab_t)
            step(v.tensor_scalar(sc, ab, 1.0, inv, ALU.subtract, ALU.mult))
            step(v.tensor_tensor(sc, sc, l, ALU.add))
            step(v.tensor_tensor(sc, sc, bt, ALU.mult))
            step(v.tensor_tensor_scan(h, ab, sc, 0.0, ALU.mult, ALU.add))
            y_t = step(v.tensor_tensor(h, h, c, ALU.mult))
            yield
            for s in range(2):
                half = slice(SS * s, SS * s + SS)
                yield from self.finish_tokens(2 * n + s, psum, u["xb"][:, s], xb_t[s], u["xb"][:, s], [
                    [(u["h"][half, P * i:P * i + P], wo[half, :])] for i in range(TB)], [y_t])

        drive([pair(n) for n in range(NB // 2)], 2)

    def split_weight(self, scope, name, shape, raw, landed):
        nc, act, dve, sp = self.nc, self.act, self.dve, self.sp
        hi, lo = self.sb(scope, f"wh_{name}", shape, F32R), self.sb(scope, f"wl_{name}", shape, F32R)
        t = landed.load(sp, raw[:, :, :], self.a[name])
        act.wait(t)
        ht = act.mark(nc.scalar.activation(hi[:, :, :], raw[:, :, :], ACT.Copy))
        dve.wait(t, ht)
        lt = dve.mark(nc.vector.tensor_tensor(lo[:, :, :], raw[:, :, :], hi[:, :, :].bitcast(F32), ALU.subtract))
        return (hi, lo), [ht, lt]

    def split_product(self, bank, pairs, after):
        pe = self.pe
        for k, ((lh, ll), (rh, rl)) in enumerate(pairs):
            pe.wait(after[k])
            for i, (l, r) in enumerate(((lh, rh), (ll, rh), (lh, rl))):
                m = self.nc.tensor.matmul(bank, l, r, start=k == 0 and i == 0, stop=k == len(pairs) - 1 and i == 2)
        return pe.mark(m)

    def split(self, src, t, hi, lo):
        dve, v = self.dve, self.nc.vector
        dve.wait(t)
        t = dve.mark(v.tensor_copy(hi, src))
        dve.wait(t)
        return dve.mark(v.tensor_tensor(lo, src, hi.bitcast(F32), ALU.subtract))

    def mlp(self, scope, tag, xo, more, then):
        nc, pe, act, dve, pool = self.nc, self.pe, self.act, self.dve, self.pool
        sb = lambda n, s, d=F32: self.sb(scope, f"m{tag}_" + n, s, d)
        landed = self.arrivals(f"m{tag}_weights")
        FC = FF // P
        whole = Ring([Slot(sb(f"t{i}", [P, T])) for i in range(4)])
        parts = [Slot((sb(f"hh{i}", [P, FC, T], F32R), sb(f"hl{i}", [P, FC, T], F32R))) for i in range(2)]
        raws = [sb("raw2", [P, KC, FF]), sb("raw3", [P, FC, C])]
        w2, w2_t = self.split_weight(scope, f"{tag}_li2_w", [P, KC, FF], raws[0], landed)
        w3, w3_t = self.split_weight(scope, f"{tag}_li3_w", [P, FC, C], raws[1], self.arrivals(f"m{tag}_down"))
        row, rows_in = self.rows(scope, [f"L1_xattn_{tag}_li3_b"], "m" + tag)
        pool.wait(rows_in)
        pe.wait(w2_t)
        psum = Ring(self.banks)
        sets = [dict(xh=sb(f"xh{i}", [P, TB, C]), nh=sb(f"nh{i}", [P, KC, T], F32R), nl=sb(f"nl{i}", [P, KC, T], F32R),
                     xb=sb(f"xb{i}", [P, TB, C]), done=[]) for i in range(MLP_SETS)]

        def batch(b):
            u = sets[b % MLP_SETS]
            for lane in (dve, act, pool):
                lane.wait(u["done"])
            x = xo[:, TB * b:TB * b + TB, :]
            t = [pool.mark(nc.gpsimd.tensor_tensor(u["xb"][:, i, :], x[:, i, :], row[f"L1_xattn_{tag}_li3_b"], ALU.add))
                 for i in range(TB)]
            for src, src_t in more(b):
                pool.wait(t[-1], src_t)
                t = [pool.mark(nc.gpsimd.tensor_tensor(u["xb"][:, :, :], u["xb"][:, :, :], src, ALU.add))]
            xb_t = t[-1]
            slot, t = self.stats(lambda i: x[:, i, :], TB, [None] * TB)
            yield
            xh_t = self.normalize(slot, t, lambda i: u["xh"][:, i, :], lambda i: x[:, i, :], TB)
            xn_t = []

            def evac(c, bank, t):
                n = whole.take(act)
                act.wait(t)
                t = act.mark(nc.scalar.activation(n.tile[:, :], bank[:, :], ACT.Identity, scale=self.col(f"{tag}_ln3_g", c),
                                                  bias=self.col(f"{tag}_ln3_b", c)))
                xn_t.append(self.split(n.tile[:, :], t, u["nh"][:, c, :], u["nl"][:, c, :]))
                n.free = [xn_t[-1]]
                return t
            self.turn(psum, u["xh"], xh_t, evac)
            yield
            part = parts[b % 2]
            hh, hl = part.tile
            dve.wait(part.free)
            h_t = []
            for f in range(FC):
                fs = slice(P * f, P * f + P)
                bank = psum.take(pe)
                t = self.split_product(bank.tile[:, :], [((w2[0][:, k, fs], w2[1][:, k, fs]), (u["nh"][:, k, :], u["nl"][:, k, :]))
                                                         for k in range(KC)], xn_t)
                h = whole.take(act)
                act.wait(t)
                t = act.mark(nc.scalar.activation(h.tile[:, :], bank.tile[:, :], ACT.Gelu, bias=self.col(f"{tag}_li2_b", f)))
                bank.free = [t]
                h_t.append(self.split(h.tile[:, :], t, hh[:, f, :], hl[:, f, :]))
                h.free = [h_t[-1]]
                yield
            r_t = []
            pe.wait(w3_t)
            for i in range(TB):
                bank = psum.take(pe)
                at = slice(P * i, P * i + P)
                t = self.split_product(bank.tile[:, 0:C], [((hh[:, f, at], hl[:, f, at]), (w3[0][:, f, :], w3[1][:, f, :]))
                                                           for f in range(FC)], h_t)
                part.free = [t]
                dve.wait(t, xb_t)
                r_t.append(dve.mark(nc.vector.tensor_tensor(u["xb"][:, i, :], bank.tile[:, 0:C], u["xb"][:, i, :], ALU.add)))
                bank.free = [r_t[-1]]
                yield
            yield from then(b, u["xb"], r_t)
            u["done"] = [self.done_token]

        drive([batch(b) for b in range(NB)], MLP_SETS, MLP_APART)

    def norm_to(self, dst):
        def then(b, r, r_t):
            slot, t = self.stats(lambda i: r[:, i, :], TB, r_t)
            yield
            done = self.normalize(slot, t, lambda i: dst[:, TB * b + i, :], lambda i: r[:, i, :], TB)
            self.done_token = done[-1]
        return then

    def block_attention(self, scope, tag, x1, xo, cross, first=None):
        nc, pe, act, dve, pool, sp = self.nc, self.pe, self.act, self.dve, self.pool, self.sp
        sb = lambda n, s, d=F32: self.sb(scope, f"{tag}_" + n, s, d)
        D, HD = 32, 32 * H
        YC = 1 if cross else KC
        landed = self.arrivals(f"{tag}_weights")
        wq = self.weight(scope, landed, f"{tag}_wq", [P, KC, HD])
        wk = self.weight(scope, landed, f"{tag}_wk", [P, YC, HD])
        wv = self.weight(scope, landed, f"{tag}_wv", [P, YC, HD])
        wo = self.weight(scope, landed, f"{tag}_li1_w", [P, NG, C])
        bias = f"L1_xattn_{tag}_li1_b"
        row, rows_in = self.rows(scope, [bias], tag)
        nkb = CB if cross else TB
        n_xn = 1 if cross else 2
        xn = [sb(f"xn{i}", [P, KC, T]) for i in range(n_xn)]
        yn = [sb("yn0", [P, 1, CTXE])] if cross else [sb(f"yn{i}", [P, KC, T]) for i in range(2)]
        vals = [sb(f"v{i}", [P, nkb, HD]) for i in range(1 if cross else 2)]
        y = sb("y", [P, NG, T])
        xb = sb("xb", [P, TB, C])
        if cross:
            raw = Ring([Slot(sb(f"ct{i}", [P, 4, CC]), self.arrivals(f"{tag}_ct{i}")) for i in range(2)])
        pool.wait(rows_in)
        pe.wait(landed.token())
        st = dict(xn={}, yn={}, v={}, y=[], y_free=[], v_free=[[], []], xb_free=[])
        jobs = []
        for b in range(NB):
            xt, yt, v = xn[b % len(xn)], yn[b % len(yn)], vals[b % len(vals)]
            for g in range(NG):
                cs = slice(P * g, P * g + P)
                chunk = dict(q=[(wq[:, k, cs], xt[:, k, :]) for k in range(KC)], qb=0.0, kb=0.0,
                             k=lambda k0, n, cs=cs, yt=yt: [(wk[:, k, cs], yt[:, k, k0:k0 + n]) for k in range(YC)],
                             q_after=lambda b=b: st["xn"][b], k_after=lambda b=b: st["yn"][b],
                             cuts=KEY_CUTS if cross else [(0, T)])
                jobs.append(dict(
                    b=b, g=g, chunk=chunk, first=True, sub=0, mask=None if cross else "upper", nk=CTX if cross else T,
                    add=False, y=y[:, g, :], vw=D, values=lambda kb, kp, h, v=v, g=g: v[0:kp, kb, P * g + D * h:P * g + D * h + D],
                    values_after=lambda b=b: st["v"][b], values_done=lambda t, b=b: st.update(v_last=t),
                    y_free=lambda: st["y_free"] + st["y"], y_done=lambda t: st.update(y=[t]),
                    ready=lambda b=b: b in st["xn"] and len(st["xn"][b]) == KC and len(st["yn"].get(b, ())) > 0))
        run, misc = self.softmax_attention(scope, tag, D, float(D) ** -0.5, jobs,
                                           [450, 450] if cross else [T, T], y, True)

        def own(b):
            x = x1[:, TB * b:TB * b + TB, :]
            normed = None
            if first:
                yield from first(b)
                normed = self.normed
            dve.wait(st["xb_free"])
            slot, t = self.stats(lambda i: x[:, i, :], TB, [normed] * TB)
            yield
            xh_t = self.normalize(slot, t, lambda i: xb[:, i, :], lambda i: x[:, i, :], TB)
            xt, yt = xn[b % len(xn)], yn[b % len(yn)]
            st["xn"][b] = []
            if not cross:
                st["yn"][b] = []
            dve.wait((pe.sem, pe.count))

            def evac(c, bank, t):
                dve.wait(t)
                t = dve.mark(nc.vector.tensor_scalar(xt[:, c, :], bank[:, :], self.col(f"{tag}_lnx_g", c),
                                                     self.col(f"{tag}_lnx_b", c), ALU.mult, ALU.add))
                st["xn"][b].append(t)
                if not cross:
                    t = dve.mark(nc.vector.tensor_scalar(yt[:, c, :], bank[:, :], self.col(f"{tag}_lny_g", c),
                                                         self.col(f"{tag}_lny_b", c), ALU.mult, ALU.add))
                    st["yn"][b].append(t)
                return t
            self.turn(self.spare, xb, xh_t, evac)
            st["xb_free"] = [(pe.sem, pe.count)]
            yield
            if not cross:
                yield from values(b)

        def context(b):
            st["yn"][b] = []
            tile = yn[0]
            cv = self.a["ctx"][b]
            dve.wait((pe.sem, pe.count))
            for i0 in range(0, CB, 4):
                n = min(4, CB - i0)
                kp = P if n == 4 else CTX - P * i0
                slot = raw.take(sp)
                t = slot.landed.load(sp, slot.tile[0:kp, 0:n, :],
                                     cv[P * i0:P * i0 + (P * n if n == 4 else kp)].rearrange("(t p) c -> p t c", p=kp))
                s, st_t = self.stats(lambda i: slot.tile[0:kp, i, :], n, [t] * n, kp)
                yield
                xh_t = self.normalize(s, st_t, lambda i: slot.tile[0:kp, i, :], lambda i: slot.tile[0:kp, i, :], n, kp)
                bank = self.spare.take(pe)
                for i in range(n):
                    pe.wait(xh_t[i])
                    m = nc.tensor.transpose(bank.tile[:, P * i:P * i + kp], slot.tile[0:kp, i, :], self.ident[0:kp, 0:kp])
                t = pe.mark(m)
                slot.free = [t]
                dve.wait(t)
                w = P * (n - 1) + kp
                t = dve.mark(nc.vector.tensor_scalar(tile[:, 0, P * i0:P * i0 + w], bank.tile[:, 0:w],
                                                     self.col(f"{tag}_lny_g"), self.col(f"{tag}_lny_b"), ALU.mult, ALU.add))
                bank.free = [t]
                yield
            dve.wait(t)
            st["yn"][b] = [dve.mark(nc.vector.tensor_copy(tile[:, 0, CTX:CTXE], tile[:, 0, CTX - 1:CTX]))]
            yield

        def values(b):
            v, yt = vals[b % len(vals)], yn[b % len(yn)]
            act.wait(st.get("v_last"))
            st["v"][b] = []
            for i in range(nkb):
                kp = min(P, (CTX if cross else T) - P * i)
                bank = self.spare.take(pe)
                t = self.product(bank.tile[0:kp, :], [(yt[:, k, P * i:P * i + kp], wv[:, k, :]) for k in range(YC)],
                                 st["yn"][b])
                act.wait(t)
                t = act.mark(nc.scalar.activation(v[0:kp, i, :], bank.tile[0:kp, :], ACT.Copy))
                bank.free = [t]
                st["v"][b].append(t)
                yield

        def finish(b):
            pool.wait(st["xb_free"])
            xb_t = [pool.mark(nc.gpsimd.tensor_tensor(xb[:, i, :], x1[:, TB * b + i, :], row[bias], ALU.add))
                    for i in range(TB)]
            yield
            for i in range(TB):
                bank = self.spare.take(pe)
                t = self.product(bank.tile[:, 0:C], [(y[:, k, P * i:P * i + P], wo[:, k, :]) for k in range(NG)], st["y"])
                dve.wait(t, xb_t[i])
                t = dve.mark(nc.vector.tensor_tensor(xo[:, TB * b + i, :], bank.tile[:, 0:C], xb[:, i, :], ALU.add))
                bank.free = [t]
                yield
            st["y_free"] = [(pe.sem, pe.count)]
            st["xb_free"] = [t]

        def beside_job(n):
            b, g = jobs[n]["b"], jobs[n]["g"]
            out = []
            if g == 0 and b:
                out.append(finish(b - 1))
            if g == (NG - 1 if cross else 1) and b + 1 < NB:
                out.append(own(b + 1))
                if cross:
                    out.append(context(b + 1))
            return out

        def between(n):
            if cross and jobs[n]["g"] == 0:
                yield from values(jobs[n]["b"])
        run([own(0)] + ([context(0)] if cross else []), beside_job, between)
        for _ in finish(NB - 1):
            pass

    def attention_blocks(self, scope):
        nc, dve, pool, sp = self.nc, self.dve, self.pool, self.sp
        x1 = self.sb(scope, "x1", [P, NT, C])
        aside = nc.dram_tensor("x_aside", (P, NT, C), F32, kind="Internal").ap()
        parked = self.arrivals("x_parked")
        parked.load(sp, aside, self.X[:, :, :])

        def affine(tag, dst, src, src_t, row):
            for i in range(TB):
                pool.wait(src_t[i])
                t = pool.mark(nc.gpsimd.tensor_tensor(dst(i), src(i), row[f"L1_xattn_{tag}_g"], ALU.mult))
                pool.wait(t)
                t = pool.mark(nc.gpsimd.tensor_tensor(dst(i), dst(i), row[f"L1_xattn_{tag}_b"], ALU.add))
            return t

        with ExitStack() as sc:
            row, rows_in = self.rows(sc, ["L1_xattn_ln1_g", "L1_xattn_ln1_b"], "n1")
            pool.wait(rows_in)

            def first_norm(b):
                at = lambda t, i: t[:, TB * b + i, :]
                slot, t = self.stats(lambda i: at(self.X, i), TB, [None] * TB)
                yield
                h_t = self.normalize(slot, t, lambda i: at(x1, i), lambda i: at(self.X, i), TB)
                yield
                self.normed = affine("ln1", lambda i: at(x1, i), lambda i: at(x1, i), h_t, row)
                yield
            dve.wait(parked.token())
            self.block_attention(sc, "a1", x1, self.X, False, first_norm)
        self.fence()
        with ExitStack() as sc:
            row, rows_in = self.rows(sc, ["L1_xattn_ln2_g", "L1_xattn_ln2_b"], "n2")
            pool.wait(rows_in)

            def then(b, r, r_t):
                at = lambda i: x1[:, TB * b + i, :]
                slot, t = self.stats(lambda i: r[:, i, :], TB, r_t)
                yield
                h_t = self.normalize(slot, t, at, lambda i: r[:, i, :], TB)
                yield
                self.done_token = affine("ln2", at, at, h_t, row)
            self.mlp(sc, "a1", self.X, lambda b: [(x1[:, TB * b:TB * b + TB, :], None)], then)
        self.fence()
        with ExitStack() as sc:
            self.block_attention(sc, "a2", x1, self.X, True)
        self.fence()
        with ExitStack() as sc:
            back = [Slot(self.sb(sc, f"back{i}", [P, TB, C]), self.arrivals(f"back{i}")) for i in range(MLP_SETS)]
            tokens = {}

            def fetch(b):
                sp.wait(back[b % MLP_SETS].free)
                tokens[b] = back[b % MLP_SETS].landed.load(sp, back[b % MLP_SETS].tile[:, :, :], aside[:, TB * b:TB * b + TB, :])
            for b in range(MLP_SETS):
                fetch(b)

            def more(b):
                yield x1[:, TB * b:TB * b + TB, :], None
                yield back[b % MLP_SETS].tile[:, :, :], tokens[b]

            def then(b, r, r_t):
                back[b % MLP_SETS].free = [(pool.sem, pool.count)]
                if b + MLP_SETS < NB:
                    fetch(b + MLP_SETS)
                yield from self.norm_to(self.X)(b, r, r_t)
            self.mlp(sc, "a2", self.X, more, then)

    def scaled_ffn(self, scope):
        nc, pe, act, dve, pool, sp = self.nc, self.pe, self.act, self.dve, self.pool, self.sp
        sb = lambda n, s, d=F32: self.sb(scope, "sf_" + n, s, d)
        FC = FF // P
        w = {}
        for n, shape in (("w1_w", [P, KC, FF]), ("w2_w", [P, KC, FF]), ("w3_w", [P, FC, C])):
            landed = self.arrivals("sf_" + n)
            w[n] = (self.weight(scope, landed, n, shape), landed.token())
        row, rows_in = self.rows(scope, ["w3_s"], "sf")
        dve.wait(rows_in)
        psum = Ring(self.banks)
        raw = Ring([Slot(sb(f"raw{i}", [P, FC, P]), self.arrivals(f"sf_raw{i}")) for i in range(3)])
        split = Ring([Slot((sb(f"wh{i}", [P, FC, P], F32R), sb(f"wl{i}", [P, FC, P], F32R))) for i in range(3)])
        parts = {n: Slot((sb(n + "h", [P, FC, T], F32R), sb(n + "l", [P, FC, T], F32R))) for n in ("a", "b")}
        last = Slot(sb("last", [P, FC, T]))
        whole = Ring([Slot(sb(f"t{i}", [P, T])) for i in range(3)])
        gates = Ring([Slot(sb(f"s{i}", [P, T])) for i in range(2)])
        xts = Ring([Slot(sb(f"xt{i}", [P, KC, T])) for i in range(2)])
        rs = Ring([Slot(sb(f"r{i}", [P, TB, C])) for i in range(2)])

        tiles = [(n, f) for _ in range(NB) for n in ("h1_w", "h2_w") for f in range(FC)]
        loaded, ready = [], []

        def load():
            if len(loaded) < len(tiles):
                n, f = tiles[len(loaded)]
                slot = raw.take(sp)
                loaded.append((slot, slot.landed.load(sp, slot.tile[:, :, :], self.a[n][f])))

        def prepare():
            if len(ready) < len(tiles):
                slot, t = loaded[len(ready)]
                to = split.take(act)
                dve.wait(to.free)
                hi, lo = to.tile
                act.wait(t)
                ht = act.mark(nc.scalar.activation(hi[:, :, :], slot.tile[:, :, :], ACT.Copy))
                dve.wait(t, ht)
                lt = dve.mark(nc.vector.tensor_tensor(lo[:, :, :], slot.tile[:, :, :], hi[:, :, :].bitcast(F32), ALU.subtract))
                slot.free = [lt]
                ready.append((to, [ht, lt]))
                load()

        for _ in range(3):
            load()
        for _ in range(2):
            prepare()

        def keep(f, src, t, to):
            hi, lo = to.tile
            t = self.split(src.tile[:, :], t, hi[:, f, :], lo[:, f, :])
            src.free = [t]
            return t

        def turned(b):
            xt, xt_t = xts.take(act), []

            def evac(c, bank, t):
                act.wait(t)
                xt_t.append(act.mark(nc.scalar.activation(xt.tile[:, c, :], bank[:, :], ACT.Copy)))
                return xt_t[-1]
            self.turn(psum, self.X[:, TB * b:TB * b + TB, :], [None] * TB, evac)
            return xt, xt_t

        used = 0
        xt, xt_t = turned(0)
        for b in range(NB):
            x = self.X[:, TB * b:TB * b + TB, :]
            dve.wait(parts["a"].free)
            a_t = []
            for f in range(FC):
                fs = slice(P * f, P * f + P)
                pe.wait(w["w1_w"][1])
                bank = psum.take(pe)
                t = self.product(bank.tile[:, :], [(w["w1_w"][0][:, k, fs], xt.tile[:, k, :]) for k in range(KC)], xt_t)
                s = gates.take(act)
                act.wait(t)
                st = act.mark(nc.scalar.activation(s.tile[:, :], bank.tile[:, :], ACT.Silu, scale=self.col("w1_s", f)))
                bank.free = [st]
                pe.wait(w["w2_w"][1])
                bank = psum.take(pe)
                t = self.product(bank.tile[:, :], [(w["w2_w"][0][:, k, fs], xt.tile[:, k, :]) for k in range(KC)], xt_t)
                xt.free = [t]
                h = whole.take(dve)
                dve.wait(t, st)
                t = dve.mark(nc.vector.scalar_tensor_tensor(out=h.tile[:, :], in0=bank.tile[:, :],
                                                            scalar=self.col("w2_s", f), in1=s.tile[:, :],
                                                            op0=ALU.mult, op1=ALU.mult))
                bank.free, s.free = [t], [t]
                a_t.append(keep(f, h, t, parts["a"]))
            for n, src, dst in (("h1", "a", "b"), ("h2", "b", None)):
                xh, xl = parts[src].tile
                src_t, a_t = a_t, []
                if dst:
                    dve.wait(parts[dst].free)
                for f in range(FC):
                    slot, w_t = ready[used]
                    used += 1
                    wh, wl = slot.tile
                    bank = psum.take(pe)
                    pe.wait(w_t)
                    t = self.split_product(bank.tile[:, :], [((wh[:, k, :], wl[:, k, :]), (xh[:, k, :], xl[:, k, :]))
                                                             for k in range(FC)], src_t)
                    slot.free, parts[src].free = [t], [t]
                    if dst:
                        h = whole.take(act)
                        out = h.tile[:, :]
                    else:
                        act.wait(last.free)
                        out = last.tile[:, f, :]
                    act.wait(t)
                    t = act.mark(nc.scalar.activation(out, bank.tile[:, :], ACT.Gelu, scale=self.col(n + "_s", f)))
                    bank.free = [t]
                    a_t.append(keep(f, h, t, parts[dst]) if dst else t)
                    prepare()
            if b + 1 < NB:
                xt, xt_t = turned(b + 1)
            pe.wait(w["w3_w"][1])
            r, r_t = rs.take(dve), []
            for i in range(TB):
                bank = psum.take(pe)
                for k in range(FC):
                    pe.wait(a_t[k])
                    m = nc.tensor.matmul(bank.tile[:, 0:C], last.tile[:, k, P * i:P * i + P], w["w3_w"][0][:, k, :],
                                         start=k == 0, stop=k == FC - 1)
                mt = pe.mark(m)
                last.free = [mt]
                dve.wait(mt)
                rt = dve.mark(nc.vector.tensor_tensor(r.tile[:, i, :], bank.tile[:, 0:C], row["w3_s"], ALU.mult))
                bank.free = [rt]
                dve.wait(rt)
                r_t.append(dve.mark(nc.vector.tensor_tensor(r.tile[:, i, :], r.tile[:, i, :], x[:, i, :], ALU.add)))
            slot, t = self.stats(lambda i: r.tile[:, i, :], TB, r_t)
            r.free = self.normalize(slot, t, lambda i: x[:, i, :], lambda i: r.tile[:, i, :], TB)
            sp.wait(r.free)
            self.stored.load(sp, self.out.rearrange("b (t p) c -> p (b t) c", p=P)[:, TB * b:TB * b + TB, :], x)


def build(nc, a, out):
    with ExitStack() as ctx:
        d = Decoder(nc, ctx, a, out)
        d.constants()
        for stage in (d.linear_attention, d.mixed_attention, d.experts, d.state_space, d.attention_blocks,
                      d.scaled_ffn):
            with ExitStack() as scope:
                stage(scope)
            d.fence()
        d.sp.wait(d.stored.token())


def by_channel(m, D):
    m = np.asarray(m)
    lead = m.shape[:-1]
    return m.reshape(*lead, NG, HG, D).swapaxes(-1, -2).reshape(*lead, -1)


def lay_out(inp):
    f = {k: np.asarray(v) for k, v in inp.items()}
    a = {"x": f["x"]}

    def w(name, m, rows=P):
        m = np.asarray(m)
        a[name] = np.ascontiguousarray(m.reshape(m.shape[0] // rows, rows, -1).transpose(1, 0, 2))
    w("L0_attn_w_qkv", f["L0_attn_w_qkv"])
    w("L0_attn_w_gate", f["L0_attn_w_gate"])
    w("L0_attn_w_proj", f["L0_attn_w_proj"])
    for n in ("Wv", "Wcv"):
        w("L0_xattn_" + n, f["L0_xattn_" + n])
    for n in ("Wq", "Wk", "Wcq", "Wck"):
        w("L0_xattn_" + n, by_channel(f["L0_xattn_" + n], C // H))
    wp = np.zeros((NG, HG, 32, C), np.float32)
    wp[:, :, :C // H] = f["L0_xattn_Wp"].reshape(NG, HG, C // H, C)
    w("L0_xattn_Wp", wp.reshape(NG * P, C))
    for n in ("bv", "bcv", "bp"):
        a["L0_xattn_" + n] = f["L0_xattn_" + n]
    a["ctx"] = f["ctx_512"]
    t = f["ctx_512"].transpose(0, 2, 1)
    a["ctx_t"] = np.concatenate([t, t[:, :, CTX - 1:]], axis=2)
    w("L0_ffn_attn_w", f["L0_ffn_attn_w"])
    w("L0_ffn_next_w", f["L0_ffn_next_w"])
    a["L0_ffn_next_b"] = f["L0_ffn_next_b"]
    for n in ("L0_ffn_w1", "L0_ffn_w2"):
        m = f[n]
        a[n] = np.ascontiguousarray(m.reshape(E, m.shape[1] // P, P, -1).transpose(0, 2, 1, 3))
    m = f["L1_attn_in_proj_w"]
    w("ssm_in", np.concatenate([m[:SS], m[SS:3 * SS:2], m[SS + 1:3 * SS:2], m[3 * SS::2], m[3 * SS + 1::2]]).T)
    a["ssm_out"] = np.concatenate([f["L1_attn_out_proj_w"].T] * 2)
    a["L1_attn_out_proj_b"] = f["L1_attn_out_proj_b"]
    for n in ("w1_w", "w2_w", "h1_w", "h2_w", "w3_w"):
        w(n, f["L1_ffn_" + n].T)
    for n in ("h1_w", "h2_w"):
        a[n] = a[n].reshape(P, FF // P, FF // P, P).transpose(2, 0, 1, 3)
    a["w3_s"] = f["L1_ffn_w3_s"]
    for n in ("ln1_g", "ln1_b", "ln2_g", "ln2_b"):
        a["L1_xattn_" + n] = f["L1_xattn_" + n]
    for tag in ("a1", "a2"):
        for n in ("wq", "wk", "wv"):
            m = f[f"L1_xattn_{tag}_{n}"].transpose(1, 0, 2)
            m = m.reshape(m.shape[0], -1)
            w(f"{tag}_{n}", m if n == "wv" else by_channel(m, 32))
        a[f"L1_xattn_{tag}_li1_b"] = f[f"L1_xattn_{tag}_li1_b"]
        for n in ("li1_w", "li2_w", "li3_w"):
            w(f"{tag}_{n}", f[f"L1_xattn_{tag}_{n}"])
        a[f"L1_xattn_{tag}_li3_b"] = f[f"L1_xattn_{tag}_li3_b"]
    b = f["L0_attn_b_qkv"]
    a["L0_attn_bv"] = b[2 * C:]
    a["L0_attn_b_proj"] = f["L0_attn_b_proj"]
    v = {k[len("L1_xattn_"):] if k.startswith("L1_xattn_") else k[len("L1_ffn_"):] if k.startswith("L1_ffn_") else k: x
         for k, x in f.items()}
    for n in ("bq", "bk", "bcq", "bck"):
        v["L0_xattn_" + n] = by_channel(v["L0_xattn_" + n], C // H)
    v["L0_attn_bq"], v["L0_attn_bk"] = b[:C], b[C:2 * C]
    for j in range(4):
        v[f"conv{j}"] = f["L1_attn_conv_w"][:, 0, j]
    ib = f["L1_attn_in_proj_b"]
    two = lambda z: np.concatenate([z, z])
    v["ssm_bd"] = two(ib[:SS])
    v["ssm_bb0"], v["ssm_bb1"] = two(ib[SS:3 * SS:2]), two(ib[SS + 1:3 * SS:2])
    v["ssm_bc0"], v["ssm_bc1"] = two(ib[3 * SS::2]), two(ib[3 * SS + 1::2])
    v["ssm_alog"] = two(f["L1_attn_A_log"])
    a["cols"] = np.ascontiguousarray(np.concatenate([v[n].reshape(-1, P) for n, _ in COLS]).T)
    return a


def kernel(**inputs):
    import concourse.bacc as bacc
    from concourse.bass_utils import run_bass_kernel_spmd

    nc = bacc.Bacc("TRN2", target_bir_lowering=False, num_devices=1)
    arrays = {f"in_{k}": np.ascontiguousarray(v) for k, v in lay_out(inputs).items()}
    aps = {k[3:]: nc.dram_tensor(k, v.shape, mybir.dt.from_np(v.dtype), kind="ExternalInput").ap()
           for k, v in arrays.items()}
    out = nc.dram_tensor("out", (NB, T, C), F32, kind="ExternalOutput").ap()
    build(nc, aps, out)
    return run_bass_kernel_spmd(nc, [arrays], core_ids=[0]).results[0]["out"]
```
